# Optimizing a Trainium2 kernel written in Bass

```python
import numpy as np
import jax
import jax.numpy as jnp

def _softmax(x, axis=-1):
    return jax.nn.softmax(x, axis=axis)

def _gelu(x):
    return jax.nn.gelu(x, approximate=True)

def _silu(x):
    return jax.nn.silu(x)

def _sigmoid(x):
    return jax.nn.sigmoid(x)

def _layernorm(x, axis=-1, eps=1e-05):
    m = jnp.mean(x, axis=axis, keepdims=True)
    v = jnp.var(x, axis=axis, keepdims=True)
    return (x - m) / jnp.sqrt(v + eps)

def _scatter_add(tgt, idx, src, axis=0):
    return tgt.at[idx].add(src)

def _segment_sum(src, seg, n):
    return jax.ops.segment_sum(src, seg, n)
kernel_name = 'mk_lm_tower_d2_tok_ids512_r4_b92c2c'

def setup_inputs(seed: int=0):
    np.random.seed(seed)
    _w = jnp.asarray

    def _rec_inputs():
        import jax
        import jax.numpy as jnp
        _rk = jax.random.key(seed)
        x = jax.random.randint(jax.random.fold_in(_rk, 1), (2, 1024), 0, 12564, jnp.int32)
        return x
    x = _rec_inputs()

    def _L0_tok_setup():
        import jax, jax.numpy as jnp
        import numpy as np
        VOCAB = 50257
        PROJ_DIM = 128
        B, S = (8, 1024)
        key = jax.random.key(seed)
        kx, kw = jax.random.split(key)
        x = jax.random.randint(kx, (B, S), 0, VOCAB)
        W = jax.random.normal(kw, (PROJ_DIM, VOCAB), dtype=jnp.float32) * 0.02
        return {'x': x, 'W': W}
    _L0_tok_all = _L0_tok_setup()
    _L0_tok_in = {k: v for k, v in _L0_tok_all.items() if k in ('W',)}
    del _L0_tok_all

    def _L0_attn_setup():
        import jax, jax.numpy as jnp
        import numpy as np
        N_HIDDEN = 128
        NUM_HEADS = 16
        HEAD_DIM = N_HIDDEN // NUM_HEADS
        BN_EPS = 0.001
        key = jax.random.key(seed)
        ks = jax.random.split(key, 9)
        bs, seq = (8, 256)
        s = 1.0 / np.sqrt(N_HIDDEN)
        return {'inputs': jax.random.normal(ks[0], (bs, seq, N_HIDDEN), dtype=jnp.float32), 'wq': jax.random.uniform(ks[1], (N_HIDDEN, N_HIDDEN), jnp.float32, -s, s), 'bq': jax.random.uniform(ks[2], (N_HIDDEN,), jnp.float32, -s, s), 'wk': jax.random.uniform(ks[3], (N_HIDDEN, N_HIDDEN), jnp.float32, -s, s), 'bk': jax.random.uniform(ks[4], (N_HIDDEN,), jnp.float32, -s, s), 'wv': jax.random.uniform(ks[5], (N_HIDDEN, N_HIDDEN), jnp.float32, -s, s), 'bv': jax.random.uniform(ks[6], (N_HIDDEN,), jnp.float32, -s, s), 'gamma': jnp.ones((N_HIDDEN,), jnp.float32), 'beta': jnp.zeros((N_HIDDEN,), jnp.float32)}
    _L0_attn_all = _L0_attn_setup()
    _L0_attn_in = {k: v for k, v in _L0_attn_all.items() if k in ('wq', 'bq', 'wk', 'bk', 'wv', 'bv', 'gamma', 'beta')}
    del _L0_attn_all

    def _L0_ffn_setup():
        import jax, jax.numpy as jnp
        import numpy as np
        MARK_AX, OP_ADD, OP_SUB = (0, 1, 2)
        ALU_LO, ALU_HI = (16, 32)
        AX_CARRY_LO, AX_CARRY_HI = (48, 64)
        OPCODE_BASE = 80
        OUTPUT_LO, OUTPUT_HI, CARRY = (128, 144, 160)
        NIB_A, NIB_B, OP_START = (0, 1, 10)
        RESULT, CARRY_OUT = (100, 101)
        GE_POS, GE_DIM = (8, 160)
        OPC_ADD, OPC_SUB = (25, 26)
        B, S, D = (8, 1024, 128)

        def _decode_nibble(x, base):
            return jnp.argmax(x[..., base:base + 16] > 0.5, axis=-1).astype(x.dtype)

        def _pipeline(h, W, b):
            for i in range(3):
                h = jnp.einsum('bspd,od->bspo', h, W[i]) + b[i]
                if i < 2:
                    h = jax.nn.relu(h)
            return h
        key = jax.random.key(seed)
        kx, k1, k2, k3, k4 = jax.random.split(key, 5)
        x_bd = jax.random.uniform(kx, (B, S, D), dtype=jnp.float32)
        Wa = jax.random.normal(k1, (3, GE_DIM, GE_DIM), dtype=jnp.float32) * 0.05
        ba = jax.random.normal(k2, (3, GE_DIM), dtype=jnp.float32) * 0.05
        Ws = jax.random.normal(k3, (3, GE_DIM, GE_DIM), dtype=jnp.float32) * 0.05
        bs = jax.random.normal(k4, (3, GE_DIM), dtype=jnp.float32) * 0.05
        return {'x_bd': x_bd, 'Wa': Wa, 'ba': ba, 'Ws': Ws, 'bs': bs}
    _L0_ffn_all = _L0_ffn_setup()
    _L0_ffn_in = {k: v for k, v in _L0_ffn_all.items() if k in ('Wa', 'ba', 'Ws', 'bs')}
    del _L0_ffn_all

    def _L1_attn_setup():
        import jax, jax.numpy as jnp
        import numpy as np
        IN_FEATURES = 128
        EMBED = 64
        NUM_HEADS = 4
        WINDOW = 64
        ALPHA = 0.5
        B, S = (64, 128)
        key = jax.random.key(seed)
        ks = jax.random.split(key, 9)
        sd_in = 1.0 / np.sqrt(IN_FEATURES)
        sd_e = 1.0 / np.sqrt(EMBED)
        return {'inputs': jax.random.normal(ks[0], (B, S, IN_FEATURES), dtype=jnp.float32), 'Wq': jax.random.uniform(ks[1], (IN_FEATURES, EMBED), jnp.float32, -sd_in, sd_in), 'bq': jnp.zeros((EMBED,), jnp.float32), 'Wk': jax.random.uniform(ks[2], (IN_FEATURES, EMBED), jnp.float32, -sd_in, sd_in), 'bk': jnp.zeros((EMBED,), jnp.float32), 'Wv': jax.random.uniform(ks[3], (IN_FEATURES, EMBED), jnp.float32, -sd_in, sd_in), 'bv': jnp.zeros((EMBED,), jnp.float32), 'gamma': jnp.array(1.0, jnp.float32), 'theta': jnp.array(0.0, jnp.float32), 'Wout': jax.random.uniform(ks[4], (EMBED, IN_FEATURES), jnp.float32, -sd_e, sd_e), 'bout': jnp.zeros((IN_FEATURES,), jnp.float32)}
    _L1_attn_all = _L1_attn_setup()
    _L1_attn_in = {k: v for k, v in _L1_attn_all.items() if k in ('Wq', 'bq', 'Wk', 'bk', 'Wv', 'bv', 'gamma', 'theta', 'Wout', 'bout')}
    del _L1_attn_all

    def _L1_ffn_setup():
        import jax, jax.numpy as jnp
        import numpy as np
        from jax import lax
        N_HEADS = 8
        D_KEYS = 128
        HALF = D_KEYS // 2
        N_KEYS = 64
        TOP_K = 8
        D_MODEL = 128

        def _forward(queries, Wq, bq, keys, w_down, w_up):
            N, T, D = queries.shape
            x = queries.reshape(-1, D)
            q = (x @ Wq + bq).reshape(-1, N_HEADS, D_KEYS)
            q1, q2 = (q[..., :HALF], q[..., HALF:])
            s1 = jnp.einsum('bhc,hnc->bhn', q1, keys[:, 0])
            s2 = jnp.einsum('bhc,hnc->bhn', q2, keys[:, 1])
            s1t, i1 = lax.top_k(s1, TOP_K)
            s2t, i2 = lax.top_k(s2, TOP_K)
            all_scores = (s1t[..., :, None] + s2t[..., None, :]).reshape(-1, N_HEADS, TOP_K * TOP_K)
            all_idx = (i1[..., :, None] * N_KEYS + i2[..., None, :]).reshape(-1, N_HEADS, TOP_K * TOP_K)
            scores, best = lax.top_k(all_scores, TOP_K)
            indices = jnp.take_along_axis(all_idx, best, axis=-1)
            w_d = w_down[indices]
            w_u = w_up[indices]
            inner = jnp.einsum('bd,bhkd->bhk', x, w_d)
            vals = jax.nn.relu(inner) * jax.nn.softmax(scores, axis=-1)
            out = jnp.einsum('bhk,bhkd->bd', vals, w_u)
            return out.reshape(N, T, D)
        key = jax.random.key(seed)
        ks = jax.random.split(key, 6)
        N, T = (2, 256)
        queries = jax.random.normal(ks[0], (N, T, D_MODEL), dtype=jnp.float32)
        Wq = jax.random.normal(ks[1], (D_MODEL, N_HEADS * D_KEYS), dtype=jnp.float32) / np.sqrt(D_MODEL)
        bq = jnp.zeros((N_HEADS * D_KEYS,), dtype=jnp.float32)
        bound = 1.0 / np.sqrt(HALF)
        keys = jax.random.uniform(ks[2], (N_HEADS, 2, N_KEYS, HALF), dtype=jnp.float32, minval=-bound, maxval=bound)
        w_down = jax.random.normal(ks[3], (N_KEYS * N_KEYS, D_MODEL), dtype=jnp.float32) * 0.02
        w_up = jax.random.normal(ks[4], (N_KEYS * N_KEYS, D_MODEL), dtype=jnp.float32) * 0.02
        return {'queries': queries, 'Wq': Wq, 'bq': bq, 'keys': keys, 'w_down': w_down, 'w_up': w_up}
    _L1_ffn_all = _L1_ffn_setup()
    _L1_ffn_in = {k: v for k, v in _L1_ffn_all.items() if k in ('Wq', 'bq', 'keys', 'w_down', 'w_up')}
    del _L1_ffn_all
    return {'x': x, 'L0_tok_W': _L0_tok_in['W'], 'L0_attn_wq': _L0_attn_in['wq'], 'L0_attn_bq': _L0_attn_in['bq'], 'L0_attn_wk': _L0_attn_in['wk'], 'L0_attn_bk': _L0_attn_in['bk'], 'L0_attn_wv': _L0_attn_in['wv'], 'L0_attn_bv': _L0_attn_in['bv'], 'L0_attn_gamma': _L0_attn_in['gamma'], 'L0_attn_beta': _L0_attn_in['beta'], 'L0_ffn_Wa': _L0_ffn_in['Wa'], 'L0_ffn_ba': _L0_ffn_in['ba'], 'L0_ffn_Ws': _L0_ffn_in['Ws'], 'L0_ffn_bs': _L0_ffn_in['bs'], 'L1_attn_Wq': _L1_attn_in['Wq'], 'L1_attn_bq': _L1_attn_in['bq'], 'L1_attn_Wk': _L1_attn_in['Wk'], 'L1_attn_bk': _L1_attn_in['bk'], 'L1_attn_Wv': _L1_attn_in['Wv'], 'L1_attn_bv': _L1_attn_in['bv'], 'L1_attn_gamma': _L1_attn_in['gamma'], 'L1_attn_theta': _L1_attn_in['theta'], 'L1_attn_Wout': _L1_attn_in['Wout'], 'L1_attn_bout': _L1_attn_in['bout'], 'L1_ffn_Wq': _L1_ffn_in['Wq'], 'L1_ffn_bq': _L1_ffn_in['bq'], 'L1_ffn_keys': _L1_ffn_in['keys'], 'L1_ffn_w_down': _L1_ffn_in['w_down'], 'L1_ffn_w_up': _L1_ffn_in['w_up']}

def reference(x, L0_tok_W, L0_attn_wq, L0_attn_bq, L0_attn_wk, L0_attn_bk, L0_attn_wv, L0_attn_bv, L0_attn_gamma, L0_attn_beta, L0_ffn_Wa, L0_ffn_ba, L0_ffn_Ws, L0_ffn_bs, L1_attn_Wq, L1_attn_bq, L1_attn_Wk, L1_attn_bk, L1_attn_Wv, L1_attn_bv, L1_attn_gamma, L1_attn_theta, L1_attn_Wout, L1_attn_bout, L1_ffn_Wq, L1_ffn_bq, L1_ffn_keys, L1_ffn_w_down, L1_ffn_w_up):
    import jax
    import jax.numpy as jnp

    def _L0_tok_ref(x, W):
        import jax, jax.numpy as jnp
        import numpy as np
        VOCAB = 50257
        PROJ_DIM = 128
        B, S = (8, 1024)
        return jnp.take(W.T, x, axis=0)

    def _L0_attn_ref(inputs, wq, bq, wk, bk, wv, bv, gamma, beta):
        import jax, jax.numpy as jnp
        import numpy as np
        N_HIDDEN = 128
        NUM_HEADS = 16
        HEAD_DIM = N_HIDDEN // NUM_HEADS
        BN_EPS = 0.001
        b, s, h = inputs.shape
        q = jax.nn.relu(inputs @ wq + bq)
        k = jax.nn.relu(inputs @ wk + bk)
        v = jax.nn.relu(inputs @ wv + bv)
        q = q.reshape(b, s, NUM_HEADS, HEAD_DIM)
        k = k.reshape(b, s, NUM_HEADS, HEAD_DIM)
        v = v.reshape(b, s, NUM_HEADS, HEAD_DIM)
        scores = jnp.einsum('bqhd,bkhd->bhqk', q, k) / np.sqrt(HEAD_DIM).astype(np.float32)
        attn = jax.nn.softmax(scores, axis=-1)
        out = jnp.einsum('bhqk,bkhd->bqhd', attn, v).reshape(b, s, h)
        out = out + inputs
        mean = jnp.mean(out, axis=(0, 1))
        var = jnp.var(out, axis=(0, 1))
        out = (out - mean) * jax.lax.rsqrt(var + BN_EPS) * gamma + beta
        return out

    def _L0_ffn_ref(x_bd, Wa, ba, Ws, bs):
        import jax, jax.numpy as jnp
        import numpy as np
        MARK_AX, OP_ADD, OP_SUB = (0, 1, 2)
        ALU_LO, ALU_HI = (16, 32)
        AX_CARRY_LO, AX_CARRY_HI = (48, 64)
        OPCODE_BASE = 80
        OUTPUT_LO, OUTPUT_HI, CARRY = (128, 144, 160)
        NIB_A, NIB_B, OP_START = (0, 1, 10)
        RESULT, CARRY_OUT = (100, 101)
        GE_POS, GE_DIM = (8, 160)
        OPC_ADD, OPC_SUB = (25, 26)
        B, S, D = (8, 1024, 128)

        def _decode_nibble(x, base):
            return jnp.argmax(x[..., base:base + 16] > 0.5, axis=-1).astype(x.dtype)

        def _pipeline(h, W, b):
            for i in range(3):
                h = jnp.einsum('bspd,od->bspo', h, W[i]) + b[i]
                if i < 2:
                    h = jax.nn.relu(h)
            return h
        x = x_bd
        Bsz, seq, _ = x.shape
        x_ge = jnp.zeros((Bsz, seq, GE_POS, GE_DIM), dtype=x.dtype)
        x_ge = x_ge.at[..., 0, NIB_A].set(_decode_nibble(x, ALU_LO))
        x_ge = x_ge.at[..., 1, NIB_A].set(_decode_nibble(x, ALU_HI))
        x_ge = x_ge.at[..., 0, NIB_B].set(_decode_nibble(x, AX_CARRY_LO))
        x_ge = x_ge.at[..., 1, NIB_B].set(_decode_nibble(x, AX_CARRY_HI))
        x_ge = x_ge.at[..., :, OP_START + OPC_ADD].set(x[..., OPCODE_BASE + OPC_ADD][..., None])
        x_ge = x_ge.at[..., :, OP_START + OPC_SUB].set(x[..., OPCODE_BASE + OPC_SUB][..., None])
        mark = x[..., MARK_AX] > 0.5
        m_add = mark & (x[..., OP_ADD] > 0.5)
        m_sub = mark & ~(x[..., OP_ADD] > 0.5) & (x[..., OP_SUB] > 0.5)
        active = (m_add | m_sub).astype(x.dtype)
        y_add = _pipeline(x_ge, Wa, ba)
        y_sub = _pipeline(x_ge, Ws, bs)
        y = jnp.where(m_add[..., None, None], y_add, jnp.where(m_sub[..., None, None], y_sub, x_ge))
        res_lo = jnp.clip(jnp.round(y[..., 0, RESULT]), 0, 15).astype(jnp.int32)
        res_hi = jnp.clip(jnp.round(y[..., 1, RESULT]), 0, 15).astype(jnp.int32)
        oh_lo = jax.nn.one_hot(res_lo, 16, dtype=x.dtype) * active[..., None]
        oh_hi = jax.nn.one_hot(res_hi, 16, dtype=x.dtype) * active[..., None]
        carry = (jnp.round(y[..., 1, CARRY_OUT]) > 0.5).astype(x.dtype) * active
        out = x
        out = out.at[..., OUTPUT_LO:OUTPUT_LO + 16].add(2.0 * oh_lo)
        out = out.at[..., OUTPUT_HI:OUTPUT_HI + 16].add(2.0 * oh_hi)
        out = out.at[..., CARRY].add(carry)
        return out

    def _L1_attn_ref(inputs, Wq, bq, Wk, bk, Wv, bv, gamma, theta, Wout, bout):
        import jax, jax.numpy as jnp
        import numpy as np
        IN_FEATURES = 128
        EMBED = 64
        NUM_HEADS = 4
        WINDOW = 64
        ALPHA = 0.5
        B, S = (64, 128)
        b, s, _ = inputs.shape
        h = NUM_HEADS
        dh = EMBED // h
        scale = EMBED ** 0.5
        idx = jnp.arange(s)
        diff = (idx[:, None] - idx[None, :]).astype(jnp.float32)
        pos_info = diff * diff
        pos_mask = jnp.abs(idx[:, None] - idx[None, :]) > WINDOW // 2
        q = (inputs @ Wq + bq).reshape(b, s, h, dh).transpose(0, 2, 1, 3)
        k = (inputs @ Wk + bk).reshape(b, s, h, dh).transpose(0, 2, 1, 3)
        v = (inputs @ Wv + bv).reshape(b, s, h, dh).transpose(0, 2, 1, 3)
        pe = jnp.exp(-jnp.abs(gamma * pos_info - theta))
        scores = jnp.einsum('bhsd,bhtd->bhst', q, k) / scale + pe
        a1 = jax.nn.softmax(scores, axis=-1)
        a2 = jax.nn.softmax(jnp.where(pos_mask, -1000000000.0, scores), axis=-1)
        out1 = jnp.einsum('bhst,bhtd->bhsd', a1, v)
        out2 = jnp.einsum('bhst,bhtd->bhsd', a2, v)
        out = ALPHA * out1 + (1.0 - ALPHA) * out2
        out = out.transpose(0, 2, 1, 3).reshape(b, s, EMBED)
        return out @ Wout + bout

    def _L1_ffn_ref(queries, Wq, bq, keys, w_down, w_up):
        import jax, jax.numpy as jnp
        import numpy as np
        from jax import lax
        N_HEADS = 8
        D_KEYS = 128
        HALF = D_KEYS // 2
        N_KEYS = 64
        TOP_K = 8
        D_MODEL = 128

        def _forward(queries, Wq, bq, keys, w_down, w_up):
            N, T, D = queries.shape
            x = queries.reshape(-1, D)
            q = (x @ Wq + bq).reshape(-1, N_HEADS, D_KEYS)
            q1, q2 = (q[..., :HALF], q[..., HALF:])
            s1 = jnp.einsum('bhc,hnc->bhn', q1, keys[:, 0])
            s2 = jnp.einsum('bhc,hnc->bhn', q2, keys[:, 1])
            s1t, i1 = lax.top_k(s1, TOP_K)
            s2t, i2 = lax.top_k(s2, TOP_K)
            all_scores = (s1t[..., :, None] + s2t[..., None, :]).reshape(-1, N_HEADS, TOP_K * TOP_K)
            all_idx = (i1[..., :, None] * N_KEYS + i2[..., None, :]).reshape(-1, N_HEADS, TOP_K * TOP_K)
            scores, best = lax.top_k(all_scores, TOP_K)
            indices = jnp.take_along_axis(all_idx, best, axis=-1)
            w_d = w_down[indices]
            w_u = w_up[indices]
            inner = jnp.einsum('bd,bhkd->bhk', x, w_d)
            vals = jax.nn.relu(inner) * jax.nn.softmax(scores, axis=-1)
            out = jnp.einsum('bhk,bhkd->bd', vals, w_u)
            return out.reshape(N, T, D)
        return _forward(queries, Wq, bq, keys, w_down, w_up)
    h = _L0_tok_ref(x, L0_tok_W)
    h = h + _L0_attn_ref(_layernorm(h, axis=-1), L0_attn_wq, L0_attn_bq, L0_attn_wk, L0_attn_bk, L0_attn_wv, L0_attn_bv, L0_attn_gamma, L0_attn_beta)
    h = h + _L0_ffn_ref(_layernorm(h, axis=-1), L0_ffn_Wa, L0_ffn_ba, L0_ffn_Ws, L0_ffn_bs)
    h = h + _L1_attn_ref(_layernorm(h, axis=-1), L1_attn_Wq, L1_attn_bq, L1_attn_Wk, L1_attn_bk, L1_attn_Wv, L1_attn_bv, L1_attn_gamma, L1_attn_theta, L1_attn_Wout, L1_attn_bout)
    h = h + _L1_ffn_ref(_layernorm(h, axis=-1), L1_ffn_Wq, L1_ffn_bq, L1_ffn_keys, L1_ffn_w_down, L1_ffn_w_up)
    return h

_drawn_inputs = setup_inputs


def setup_inputs(seed=0):
    import zlib

    import numpy as np

    out = dict(_drawn_inputs(seed))
    spreads = {'L0_attn_gamma': (1.0, 0.2),
     'L0_attn_beta': (0.0, 0.1),
     'L1_attn_bq': (0.0, 0.8),
     'L1_attn_bk': (0.0, 0.8),
     'L1_attn_bv': (0.0, 0.267),
     'L1_attn_bout': (0.0, 0.1),
     'L1_ffn_bq': (0.0, 0.8)}
    factors = {'L0_attn_wq': 8.0,
     'L0_attn_bq': 8.0,
     'L0_attn_wk': 8.0,
     'L0_attn_bk': 8.0,
     'L0_attn_wv': 7.152,
     'L0_attn_bv': 8.0,
     'L1_attn_Wq': 8.0,
     'L1_attn_Wk': 8.0,
     'L1_attn_Wv': 3.179,
     'L1_ffn_Wq': 8.0,
     'L1_ffn_keys': 8.0,
     'L1_ffn_w_down': 8.0,
     'L1_ffn_w_up': 8.0}
    for name, (base, spread) in spreads.items():
        noise = np.random.default_rng([zlib.crc32(name.encode()), seed]).standard_normal(out[name].shape)
        drawn = base * np.exp(spread * noise) if base else spread * noise
        out[name] = jnp.asarray(drawn.astype(out[name].dtype))
    for name, factor in factors.items():
        out[name] = (out[name] * factor).astype(out[name].dtype)
    return out
```

```python
from contextlib import ExitStack

import concourse.bass as bass
from concourse import mybir

F32 = mybir.dt.float32
BF16 = mybir.dt.bfloat16
U32 = mybir.dt.uint32
I32 = mybir.dt.int32
ALU = mybir.AluOpType
ACT = mybir.ActivationFunctionType
X = mybir.AxisListType.X

P = 128
C = 128
B = 2
S = 1024
NTOK = B * S
NT = NTOK // P
KT = S // P
HL = 4
H0, D0 = 16, 8
UNITS = B * H0 // HL
H1, D1 = 4, 16
E1 = H1 * D1
WIN = 32
QC = 512
LN_EPS, BN_EPS = 1e-5, 1e-3
BIG = 1e30
Q_PART = (0, 0, 1, 0, 2, 1)
K_PART = (0, 1, 0, 2, 0, 1)
SHIFT0 = len(Q_PART) * D0
SHIFT1 = len(Q_PART) * D1
TW = S + S - P
NH, NK, TK = 8, 64, 8
PAIRS = NH * TK
UH, VL = 128, 32
HT = P // 2


class Tally:

    def __init__(self, eng, sem):
        self.eng, self.sem, self.n = eng, sem, 0

    def then_wait(self, ins):
        ins.then_inc(self.sem, 1)
        self.n += 1
        self.eng.wait_ge(self.sem, self.n)


def build_tower(nc, a, out):
    ctx = ExitStack()
    with ctx:
        def sb(name, shape, dt=F32):
            return ctx.enter_context(nc.sbuf_tensor(name, shape, dt))

        sems = {}

        def sem(name):
            if name not in sems:
                sems[name] = ctx.enter_context(nc.semaphore(name))
            return sems[name]

        h = sb("h", [P, NT, C])
        xn = sb("xn", [P, NT, C])
        tmp = sb("tmp", [P, NT, C])
        xT = sb("xT", [C, NTOK])
        stat = sb("stat", [P, 8, NT])
        ident = sb("ident", [P, P])
        ones = sb("ones", [P, P])
        idx = sb("idx", [P, NT], I32)
        wts = sb("wts", [C, 3, C])
        cols = sb("cols", [C, 4])
        rows = sb("rows", [1, 4, C])
        big = sb("big", [P, 48 * 1024], BF16)
        vall = sb("vall", [P, UNITS, KT, HL, D0 + 1])
        vst = sb("vst", [P, KT, HL, 32])
        probs = sb("probs", [P, 2, HL, QC])
        osb = sb("osb", [P, QC])
        mhalf = sb("mhalf", [P, 32, 2])
        mx = sb("mx", [P, 32])
        shf = sb("shf", [32, P])
        sh = sb("sh", [32, 3, P], BF16)
        rden = sb("rden", [P, 4, HL])
        bn = sb("bn", [P, 5, C])
        bn_r = bn[:, 3, :]
        w1 = sb("w1", [C, 3, E1])
        wout = sb("wout", [E1, C])
        cols1 = sb("cols1", [E1, 2])
        rows1 = sb("rows1", [1, 2, C])
        gt = sb("gt", [P, 2])
        dist = sb("dist", [P, TW])
        near = sb("near", [P, 3, P])
        wmask = sb("wmask", [P, 256])
        wscr = sb("wscr", [P, 2, 192])
        mx1 = sb("mx1", [P, 64])
        wf = sb("wf", [C, NH * P])
        bf = sb("bf", [1, NH * P])
        bqt = sb("bqt", [P, NH])
        ps = ctx.enter_context(nc.psum_tensor("ps", [P, 8, QC], F32))
        score_ps = ps[:, 0:4, :].rearrange("p (s x) n -> p s x n", s=2)
        max_ps = ps[:, 4:6, :]
        o_ps = ps[:, 6:8, :]

        QS = big[:, 0:32768].rearrange("p (u h n) -> p u h n", u=UNITS, h=HL)
        KS = big[:, 32768:49152].rearrange("p (u h n) -> p u h n", u=UNITS, h=2)
        attn = tmp[:].rearrange("p t c -> p (t c)").rearrange("p (u t c) -> p u t c", u=UNITS, t=KT)
        q_cm = probs[:].rearrange("p a b n -> p (a b n)")[:, 0:NTOK]
        k_cm = probs[:].rearrange("p a b n -> p (a b n)")[:, NTOK:2 * NTOK]
        splits = sb("splits", [C, 3, NTOK], BF16)

        def part(at, n):
            return big[:, at:at + n]
        QS1 = part(0, 8192).rearrange("p (b h n) -> p b h n", b=B, h=H1)
        QW1 = part(8192, 8192).rearrange("p (b h n) -> p b h n", b=B, h=H1)
        KS1 = part(16384, 8192).rearrange("p (b h n) -> p b h n", b=B, h=H1)
        wdt = part(24576, 8192).bitcast(F32).rearrange("p (v u) -> p v u", v=VL)
        wup = part(32768, 8192).bitcast(F32).rearrange("p (v d) -> p v d", v=VL)
        wdr = part(40960, 8192).bitcast(F32).rearrange("p (v d) -> p v d", v=VL)
        sh1 = sb("sh1", [64, 3, P], BF16)
        shf1 = sb("shf1", [64, P])
        vall1 = vall[:].rearrange("p u t h d -> p (u t h d)")[:, 0:B * KT * H1 * (D1 + 1)]\
            .rearrange("p (b t h d) -> p b t h d", b=B, t=KT, h=H1)
        attn1 = tmp[:].rearrange("p t c -> p (t c)")[:, 0:NT * E1].rearrange("p (t c) -> p t c", t=NT)
        aT = xT[0:E1, :]
        ge = part(0, 16384).bitcast(F32).rearrange("p (x v n) -> p x v n", x=2, v=VL)
        onehot = part(16384, 4096).bitcast(F32).rearrange("p (x c u) -> p x c u", x=2, c=8)
        weigh = part(20480, 2048).bitcast(F32).rearrange("p (x c v) -> p x c v", x=2, c=8)
        gated = part(22528, 2048).bitcast(F32).rearrange("p (x i n) -> p x i n", x=2, i=4)
        flat = probs[:].rearrange("p a b n -> p (a b n)")
        room = [0]

        def pick(n):
            room[0] += n
            return flat[:, room[0] - n:room[0]]
        top = pick(128).rearrange("p (h q k) -> p h q k", h=NH, q=2)
        top_at = pick(128).bitcast(U32).rearrange("p (h q k) -> p h q k", h=NH, q=2)
        sums = pick(512).rearrange("p (h i j) -> p h i j", h=NH, i=TK)
        best = pick(64).rearrange("p (h k) -> p h k", h=NH)
        best_at = pick(64).bitcast(U32).rearrange("p (h k) -> p h k", h=NH)
        side = [pick(64).bitcast(U32).rearrange("p (h k) -> p h k", h=NH) for _ in range(2)]
        match = [pick(512).rearrange("p (h k i) -> p h k i", h=NH, k=TK) for _ in range(2)]
        key_at = [pick(64) for _ in range(2)]
        upper = pick(64)
        ev = pick(64).rearrange("p (h k) -> p h k", h=NH)
        evd = pick(64).rearrange("p (h k) -> p h k", h=NH)
        esum = pick(8)
        rsum = pick(8)
        trip = pick(384).rearrange("p (w d n) -> p w d n", w=3, d=2)
        uvw = pick(384).rearrange("p (x w n) -> p x w n", x=2, w=3)
        zt = pick(128)
        assert room[0] <= flat.shape[1]
        iota_f = sb("iota_f", [P, P])
        kbd = flat[:, 0:1024].rearrange("p (h c) -> p h c", h=NH)
        wqr = flat[:, 1024:2048]
        wqT = flat[:, 2048:3072].rearrange("p (h c) -> p h c", h=NH)
        kT = flat[:, 3072:4096].rearrange("p (h n) -> p h n", h=NH)
        s_ps = ps[:, 0:2, :].rearrange("p a n -> p (a n)").rearrange("p (h q n) -> p h q n", h=NH, q=2)
        g_ps, in_ps, acc_ps, t_ps = ps[:, 2:4, :], ps[:, 4:6, :], ps[:, 6, 0:C], ps[:, 7, :]

        q_scr = nc.dram_tensor("q_scr", [3, C, NTOK], BF16).ap()
        k_scr = nc.dram_tensor("k_scr", [3, C, NTOK], BF16).ap()
        q1_scr = nc.dram_tensor("q1_scr", [3, E1, NTOK], BF16).ap()
        k1_scr = nc.dram_tensor("k1_scr", [3, E1, NTOK], BF16).ap()
        out_v = out.rearrange("b (t p) c -> p (b t) c", p=P)

        def spread(col, n):
            return col.unsqueeze(2).broadcast_to([col.shape[0], col.shape[1], n])

        t_par = [0]

        block = ctx.enter_context(nc.Block())

        w_in, tok_in, gathered = sem("w_in"), sem("tok_in"), sem("gathered")
        consts, consts_f, zeroed = sem("consts"), sem("consts_f"), sem("zeroed")
        ln_var, ln_sqrt, ln_done = sem("ln_var"), sem("ln_sqrt"), sem("ln_done")
        turned, turned_out = sem("turned"), sem("turned_out")
        proj, proj_out = sem("proj"), sem("proj_out")
        split_done, split_out, stack_in = sem("split_done"), sem("split_out"), sem("stack_in")
        v_done, v_out = sem("v_done"), sem("v_out")
        max_scores, max_read, unit_max = sem("max_scores"), sem("max_read"), sem("unit_max")
        max_turned, shift_split, shift_rows = sem("max_turned"), sem("shift_split"), sem("shift_rows")
        scores_ready, exp_done, pv_done = sem("scores_ready"), sem("exp_done"), sem("pv_done")
        v_staged, o_read, o_turned, o_norm = sem("v_staged"), sem("o_read"), sem("o_turned"), sem("o_norm")
        saved = sem("saved")
        bn_ready, bn_made, bn_root = sem("bn_ready"), sem("bn_made"), sem("bn_root")
        w1_in, fold_in, fold_ready, fold_made, fold_out = (sem(x) for x in (
            "w1_in", "fold_in", "fold_ready", "fold_made", "fold_out"))
        dist_num, dist_arg, dist_done = sem("dist_num"), sem("dist_arg"), sem("dist_done")
        wd_in, wu_in, wd_turned, wd_out = sem("wd_in"), sem("wu_in"), sem("wd_turned"), sem("wd_out")
        proj1, proj1_out, split1_done, split1_out, stack1_in = (sem(x) for x in (
            "proj1", "proj1_out", "split1_done", "split1_out", "stack1_in"))
        zeroed1, v1_done, v1_out = sem("zeroed1"), sem("v1_done"), sem("v1_out")
        max1_scores, max1_read, unit1_max, max1_turned, shift1_split, shift1_rows = (sem(x) for x in (
            "max1_scores", "max1_read", "unit1_max", "max1_turned", "shift1_split", "shift1_rows"))
        scores1_ready, exp1_done, scaled_dve, scaled_pool, pv1_done = (sem(x) for x in (
            "scores1_ready", "exp1_done", "scaled_dve", "scaled_pool", "pv1_done"))
        v1_staged, o1_read, o1_turned, o1_norm = (sem(x) for x in ("v1_staged", "o1_read", "o1_turned", "o1_norm"))
        attn1_done, a_turned, a_out, wo_made, wo_added = (sem(x) for x in (
            "attn1_done", "a_turned", "a_out", "wo_made", "wo_added"))
        zt_staged, s_ready, s_picked, diff_done, pexp_done, trip_done, trip_turned, uvw_ready = (sem(x) for x in (
            "zt_staged", "s_ready", "s_picked", "diff_done", "pexp_done", "trip_done", "trip_turned", "uvw_ready"))
        a_made, b_made, b_weighted, g_made, ge_out, inner_ready, gr_done, acc_used, h_out = (sem(x) for x in (
            "a_made", "b_made", "b_weighted", "g_made", "ge_out", "inner_ready", "gr_done", "acc_used", "h_out"))
        pick_order = sem("pick_order")

        STEPS1 = [(qh, kt, pr) for qh in range(2) for kt in range(KT) for pr in range(2)]
        WSTEPS = [(i, k) for i in range(KT) for k in (i - 1, i, i + 1) if 0 <= k < KT]
        NE1, NV1 = len(STEPS1) + len(WSTEPS), KT * 2 + len(WSTEPS)
        MAX1 = [("full", hl, qt, kh) for hl in range(HL) for qt in range(KT) for kh in range(2)] + \
               [("near", hl, qt, 0) for hl in range(HL) for qt in range(KT)]

        def window_of(qt):
            return (0, 64) if qt == 0 else (S - 192, 0) if qt == KT - 1 else (qt * P - WIN, 32)

        STEPS0 = [(qh, kt, pr) for qh in range(2) for kt in range(KT) for pr in range(2)]

        @block.sync
        def _(sp):
            for i, w in enumerate(("L0_attn_wq", "L0_attn_wk", "L0_attn_wv")):
                sp.dma_start(wts[:, i, :], a[w]).then_inc(w_in, 16)
            for i, w in enumerate(("L0_attn_bq", "L0_attn_bk")):
                sp.dma_start(cols[:, i:i + 1], a[w].rearrange("(c o) -> c o", o=1)).then_inc(w_in, 16)
            for i, w in enumerate(("L0_attn_bv", "L0_attn_gamma", "L0_attn_beta")):
                sp.dma_start(rows[:, i, :], a[w].rearrange("(o c) -> o c", o=1)).then_inc(w_in, 16)
            for i, w in enumerate(("L1_attn_Wq", "L1_attn_Wk", "L1_attn_Wv")):
                sp.dma_start(w1[:, i, :], a[w]).then_inc(w1_in, 16)
            sp.dma_start(wout[:], a["L1_attn_Wout"]).then_inc(w1_in, 16)
            for i, w in enumerate(("L1_attn_bq", "L1_attn_bk")):
                sp.dma_start(cols1[:, i:i + 1], a[w].rearrange("(c o) -> c o", o=1)).then_inc(w1_in, 16)
            sp.dma_start(rows1[:, 0, 0:E1], a["L1_attn_bv"].rearrange("(o c) -> o c", o=1)).then_inc(w1_in, 16)
            sp.dma_start(rows1[:, 1, :], a["L1_attn_bout"].rearrange("(o c) -> o c", o=1)).then_inc(w1_in, 16)
            sp.dma_start(wqr, a["L1_ffn_Wq"]).then_inc(fold_in, 16)
            sp.dma_start(bqt[:], a["bqt"]).then_inc(fold_in, 16)
            sp.wait_ge(fold_ready, 1)
            for q in range(2):
                sp.dma_start(kbd[NK * q:NK * q + NK, :, NK * q:NK * q + NK],
                             a["L1_ffn_keys"][:, q].rearrange("h n c -> n h c")).then_inc(fold_in, 16)
            sp.wait_ge(split_done, 3)
            sp.dma_start(q_scr.rearrange("s c t -> c s t"), splits[:]).then_inc(split_out, 16)
            sp.wait_ge(split_done, 6)
            sp.dma_start(k_scr.rearrange("s c t -> c s t"), splits[:]).then_inc(split_out, 16)
            sp.wait_ge(split_out, 32)
            sp.wait_ge(zeroed, 2)
            Q8 = big[:, 0:32768].rearrange("p (b g r n) -> p b g r n", b=B, g=8, r=2)
            K8 = big[:, 32768:49152].rearrange("p (b g n) -> p b g n", b=B, g=8)
            for b in range(B):
                for r in range(len(Q_PART)):
                    for par in range(2):
                        at = 64 * par + D0 * r
                        qsrc = q_scr[Q_PART[r], :, b * S:(b + 1) * S].rearrange("(g r d) t -> r d g t", r=2, d=D0)
                        ksrc = k_scr[K_PART[r], :, b * S:(b + 1) * S].rearrange("(g r d) t -> r d g t", r=2, d=D0)
                        sp.dma_start(Q8[at:at + D0, b, :, par, :], qsrc[par]).then_inc(stack_in, 16)
                        sp.dma_start(K8[at:at + D0, b, :, :], ksrc[par]).then_inc(stack_in, 16)

            def send_shift(n):
                sp.wait_ge(shift_split, 4 * n + 4)
                for i in range(3):
                    for par in range(2):
                        at = 64 * par + SHIFT0 + i
                        for x in range(2):
                            sp.dma_start(QS[at:at + 1, n, 2 * x + par, :].rearrange("o (t n) -> o t n", n=P),
                                         sh[16 * par + 8 * x:16 * par + 8 * x + 8, i, :]).then_inc(shift_rows, 16)

            with sp.Fori(0, UNITS) as n:
                send_shift(n)
            sp.wait_ge(pv_done, 16 * UNITS)
            sp.dma_start(wdr, a["L1_ffn_w_down"].rearrange("(u v) d -> u v d", v=VL)).then_inc(wd_in, 16)
            sp.dma_start(wup, a["L1_ffn_w_up"].rearrange("(u v) d -> u v d", v=VL)).then_inc(wu_in, 16)
            sp.wait_ge(split1_done, 3)
            sp.dma_start(q1_scr.rearrange("s c t -> c s t"), splits[0:E1, :, :]).then_inc(split1_out, 16)
            sp.wait_ge(split1_done, 6)
            sp.dma_start(k1_scr.rearrange("s c t -> c s t"), splits[0:E1, :, :]).then_inc(split1_out, 16)
            sp.wait_ge(split1_out, 32)
            sp.wait_ge(zeroed1, 3)
            for b in range(B):
                for r in range(len(Q_PART)):
                    at = D1 * r
                    qsrc = q1_scr[Q_PART[r], :, b * S:(b + 1) * S].rearrange("(h d) t -> d h t", d=D1)
                    ksrc = k1_scr[K_PART[r], :, b * S:(b + 1) * S].rearrange("(h d) t -> d h t", d=D1)
                    sp.dma_start(QS1[at:at + D1, b, :, :], qsrc).then_inc(stack1_in, 16)
                    sp.dma_start(KS1[at:at + D1, b, :, :], ksrc).then_inc(stack1_in, 16)
                    sp.dma_start(QW1[at:at + D1, b, :, :], qsrc).then_inc(stack1_in, 16)
            for b in range(B):
                sp.wait_ge(shift1_split, 4 * b + 4)
                for i in range(3):
                    at = SHIFT1 + i
                    sp.dma_start(QS1[at:at + 1, b, :, :].rearrange("o h (t n) -> o (h t) n", n=P),
                                 sh1[0:32, i, :]).then_inc(shift1_rows, 16)
                    sp.dma_start(QW1[at:at + 1, b, :, :].rearrange("o h (t n) -> o (h t) n", n=P),
                                 sh1[32:64, i, :]).then_inc(shift1_rows, 16)
            with sp.Fori(0, NT) as t:
                sp.wait_ge(h_out, t + 1)
                sp.dma_start(out_v[:, t, :], h[:, t, :]).then_inc(saved, 16)
            sp.wait_ge(saved, 16 * NT)

        @block.gpsimd
        def _(pool):
            pool.dma_start(idx[:], a["tok"]).then_inc(tok_in, 16)
            for i, w in enumerate(("L1_attn_gamma", "L1_attn_theta")):
                pool.dma_start(gt[:, i:i + 1], a[w].partition_broadcast(P)).then_inc(sem("gt_in"), 16)
            pool.memset(ident[:], 0.0).then_inc(consts, 1)
            pool.memset(ones[:], 1.0).then_inc(consts, 1)
            pool.wait_ge(consts, 2)
            pool.affine_select(out=ident[:], in_=ident[:], compare_op=ALU.not_equal, fill=1.0, base=0,
                               pattern=[[-1, P]], channel_multiplier=1).then_inc(consts, 1)
            pool.wait_ge(tok_in, 16)
            for t in range(NT):
                pool.indirect_dma_start(h[:, t, :], None, a["emb"],
                                        bass.IndirectOffsetOnAxis(idx[:, t:t + 1].bitcast(U32), 0)).then_inc(gathered, 16)
            pool.iota(dist[:].bitcast(I32), [[1, TW]], base=-(S - P), channel_multiplier=-1).then_inc(dist_num, 1)
            pool.iota(iota_f[:], [[1, P]], base=0, channel_multiplier=0,
                      allow_small_or_imprecise_dtypes=True).then_inc(consts_f, 1)
            pool.memset(wmask[:], 0.0).then_inc(consts_f, 1)
            pool.wait_ge(consts_f, 2)
            pool.affine_select(out=wmask[:], in_=wmask[:], compare_op=ALU.is_ge, fill=-BIG, base=64 + WIN,
                               pattern=[[-1, 256]], channel_multiplier=1).then_inc(consts_f, 1)
            pool.wait_ge(consts_f, 3)
            pool.affine_select(out=wmask[:], in_=wmask[:], compare_op=ALU.is_ge, fill=-BIG, base=WIN - 64,
                               pattern=[[1, 256]], channel_multiplier=-1).then_inc(consts_f, 1)
            pool.wait_ge(dist_done, 3)
            for d in range(3):
                src = S - P - P * (d - 1)
                pool.tensor_copy(near[:, d, :], dist[:, src:src + P]).then_inc(consts_f, 1)
                pool.wait_ge(consts_f, 4 + 3 * d + 1)
                pool.affine_select(out=near[:, d, :], in_=near[:, d, :], compare_op=ALU.is_ge, fill=0.0,
                                   base=WIN + P * (d - 1), pattern=[[-1, P]], channel_multiplier=1).then_inc(consts_f, 1)
                pool.wait_ge(consts_f, 4 + 3 * d + 2)
                pool.affine_select(out=near[:, d, :], in_=near[:, d, :], compare_op=ALU.is_ge, fill=0.0,
                                   base=WIN - P * (d - 1), pattern=[[1, P]], channel_multiplier=-1).then_inc(consts_f, 1)
            pool.memset(vst[:], 0.0).then_inc(consts, 1)
            pool.memset(vall[:, :, :, :, D0:D0 + 1], 1.0).then_inc(consts, 1)
            pool.wait_ge(consts, 5)
            pool.wait_ge(v_out, NT)
            pool.tensor_copy(vst[:, :, :, 0:D0 + 1], vall[:, 0, :, :, :]).then_inc(v_staged, 1)
            with pool.Fori(1, UNITS) as n:
                pool.wait_ge(pv_done, 16 * n)
                pool.tensor_copy(vst[:, :, :, 0:D0 + 1], vall[:, n, :, :, :]).then_inc(v_staged, 1)
            pool.wait_ge(pv_done, 16 * UNITS)
            pool.memset(vall1[:, :, :, :, D1:D1 + 1], 1.0).then_inc(zeroed1, 1)
            pool.memset(part(0, 16384).bitcast(F32), 0.0).then_inc(zeroed1, 1)
            pool.memset(part(16384, 8192), -1.0).then_inc(zeroed1, 1)
            for b in range(B):
                pool.wait_ge(v1_out, NT)
                if b:
                    pool.wait_ge(pv1_done, NV1)
                pool.tensor_copy(vst[:, :, :, 0:D1 + 1], vall1[:, b, :, :, :]).then_inc(v1_staged, 1)
                for e, (qh, kt, pr) in enumerate(STEPS1):
                    if pr == 1:
                        pool.wait_ge(exp1_done, NE1 * b + e + 1)
                        at = qh * QC - kt * P + S - P
                        slot = probs[:, e // 2 % 2, 2:4, :]
                        pool.tensor_tensor(slot, slot, dist[:, at:at + QC].unsqueeze(1).broadcast_to([P, 2, QC]),
                                           ALU.mult).then_inc(scaled_pool, 1)
            def weigh_tile(t):
                for g in range(8):
                    pool.wait_ge(b_made, 8 * t + g + 1)
                    j = g % 2
                    pool.tensor_tensor(weigh[:, j], weigh[:, j], spread(uvw[:, t_par[0], 2, 8 * g:8 * g + 8], 64),
                                       ALU.mult).then_inc(b_weighted, 1)

            with pool.Fori(0, NT // 2) as m:
                for t_par[0] in range(2):
                    weigh_tile(2 * m + t_par[0])

        @block.scalar
        def _(act):
            def ln_root(k):
                act.wait_ge(ln_var, k)
                act.activation(stat[:, 3, :], stat[:, 2, :], ACT.Sqrt).then_inc(ln_sqrt, 1)

            act.wait_ge(dist_arg, 1)
            for i, (f, sc) in enumerate(((ACT.Abs, 1.0), (ACT.Exp, -1.0), (ACT.Exp, 1.0))):
                if i:
                    act.wait_ge(dist_done, i)
                act.activation(dist[:], dist[:], f, scale=sc).then_inc(dist_done, 1)
            for i in range(4):
                dst = (wqT, kT)[i // 2]
                act.wait_ge(fold_made, i + 1)
                act.activation(dst[:, 4 * (i % 2):4 * (i % 2) + 4, :].rearrange("p h c -> p (h c)"), ps[:, i, :],
                               ACT.Copy).then_inc(fold_out, 1)
            for i in range(2):
                act.wait_ge(fold_made, 5)
                act.activation(wf[:, i * QC:(i + 1) * QC], ps[:, 4 + i, :], ACT.Copy).then_inc(fold_out, 1)
                act.activation(bf[:, i * QC:(i + 1) * QC], ps[0:1, 6 + i, :], ACT.Copy).then_inc(fold_out, 1)
            ln_root(1)
            act.wait_ge(w_in, 16 * 8)
            act.wait_ge(fold_made, 5)
            for i, dst in enumerate((q_cm, k_cm)):
                for j in range(4):
                    act.wait_ge(proj, 4 * i + j + 1)
                    act.activation(dst[:, j * QC:(j + 1) * QC], ps[:, j, :], ACT.Relu,
                                   bias=cols[:, i:i + 1]).then_inc(proj_out, 1)
            for t in range(NT):
                b, kt = divmod(t, KT)
                act.wait_ge(v_done, t + 1)
                act.activation(vall[:, 4 * b:4 * b + 4, kt, :, 0:D0],
                               ps[:, 4 + t % 4, 0:C].rearrange("p (g h d) -> p g h d", g=4, h=HL),
                               ACT.Relu).then_inc(v_out, 1)

            def exps(n):
                for e, (qh, kt, pr) in enumerate(STEPS0):
                    act.wait_ge(scores_ready, 32 * n + e + 1)
                    v = e // 2
                    if not isinstance(n, int) or 16 * n + v >= 2:
                        act.wait_ge(pv_done, 16 * n + v - 1)
                    act.activation(probs[:, v % 2, 2 * pr:2 * pr + 2, :], score_ps[:, e % 2, :, :], ACT.Exp,
                                   scale=D0 ** -0.5).then_inc(exp_done, 1)

            act.wait_ge(split_done, 6)
            exps(0)
            with act.Fori(1, UNITS) as n:
                exps(n)
            act.wait_ge(bn_ready, 3)
            act.activation(bn[:, 2, :], bn[:, 1, :], ACT.Sqrt).then_inc(bn_root, 1)
            ln_root(2)
            ln_root(3)
            for r in range(8):
                act.wait_ge(wd_turned, r + 1)
                act.activation(wdt[:, 4 * r:4 * r + 4, :].rearrange("p v u -> p (v u)"), ps[:, 4 + r % 4, :],
                               ACT.Copy).then_inc(wd_out, 1)
            act.wait_ge(w1_in, 16 * 8)
            for i, dst in enumerate((q_cm, k_cm)):
                for j in range(4):
                    act.wait_ge(proj1, 4 * i + j + 1)
                    act.activation(dst[0:E1, j * QC:(j + 1) * QC], ps[0:E1, j, :], ACT.Identity,
                                   bias=cols1[:, i:i + 1]).then_inc(proj1_out, 1)
            act.wait_ge(zeroed1, 1)
            for t in range(NT):
                b, kt = divmod(t, KT)
                act.wait_ge(v1_done, t + 1)
                act.activation(vall1[:, b, kt, :, 0:D1],
                               ps[:, 4 + t % 4, 0:E1].rearrange("p (h d) -> p h d", h=H1), ACT.Copy).then_inc(v1_out, 1)
            act.wait_ge(split1_done, 6)
            for b in range(B):
                for e in range(NE1):
                    act.wait_ge(scores1_ready, NE1 * b + e + 1)
                    if e < len(STEPS1):
                        qh, kt, pr = STEPS1[e]
                        v = e // 2
                        dst, src = probs[:, v % 2, 2 * pr:2 * pr + 2, :], score_ps[:, e % 2, :, :]
                    else:
                        v = e - len(STEPS1) + 16
                        dst, src = probs[:, v % 2, 0, :], score_ps[:, e % 2, 0, :]
                    if NV1 * b + v >= 2:
                        act.wait_ge(pv1_done, NV1 * b + v - 1)
                    act.activation(dst, src, ACT.Exp, scale=E1 ** -0.5).then_inc(exp1_done, 1)
            for j in range(4):
                act.wait_ge(a_turned, j + 1)
                act.activation(aT[:, j * QC:(j + 1) * QC], ps[0:E1, j, :], ACT.Copy).then_inc(a_out, 1)
            ln_root(4)
            def stage_zt(t):
                act.wait_ge(s_ready, t)
                act.activation(zt, xT[:, bass.ts(t, P)], ACT.Copy).then_inc(zt_staged, 1)

            def pick_acts(t, x):
                act.wait_ge(diff_done, t + 1)
                act.activation(ev, evd, ACT.Exp).then_inc(pexp_done, 1)
                act.wait_ge(trip_turned, t + 1)
                src = t_ps[:, 0:384].rearrange("p (w n) -> p w n", w=3)
                for y in range(2):
                    act.activation(uvw[HT * y:HT * y + HT, x, :, :], src[HT * y:HT * y + HT, :, HT * y:HT * y + HT],
                                   ACT.Copy).then_inc(uvw_ready, 1)

            def ge_tile(t, x, g0, g1):
                for g in range(g0, g1):
                    if g == 0 and not (isinstance(t, int) and t < 2):
                        act.wait_ge(gr_done, 8 * (t - 1))
                    act.wait_ge(g_made, 8 * t + g + 1)
                    act.activation(ge[:, x, :, :].rearrange("p v (y n) -> p y v n", y=2)[:, :, :, 8 * g:8 * g + 8],
                                   g_ps[:, g % 2, :].rearrange("p (c y v) -> p y v c", c=8, y=2),
                                   ACT.Copy).then_inc(ge_out, 1)

            act.wait_ge(turned_out, 12)
            stage_zt(0)
            pick_acts(0, 0)

            def tile(t, x, more):
                if more:
                    stage_zt(t + 1)
                ge_tile(t, x, 0, 6)
                if more:
                    pick_acts(t + 1, 1 - x)
                ge_tile(t, x, 6, 8)

            for x in range(2):
                tile(x, x, True)
            with act.Fori(1, NT // 2 - 1) as m:
                for x in range(2):
                    tile(2 * m + x, x, True)
            for x in range(2):
                tile(NT - 2 + x, x, x == 0)

        @block.tensor
        def _(pe):
            pe.wait_ge(consts, 3)

            def turn_ln(k):
                pe.wait_ge(ln_done, k)
                for j in range(4):
                    for i in range(4):
                        last = pe.transpose(ps[:, j, i * P:(i + 1) * P], xn[:, 4 * j + i, :], ident[:])
                    last.then_inc(turned, 1)

            pe.wait_ge(fold_in, 16 * 4)
            for i in range(4):
                src = (wqr.rearrange("p (h c) -> p h c", h=NH), kbd)[i // 2]
                for j in range(4):
                    last = pe.transpose(ps[:, i, j * P:(j + 1) * P], src[:, 4 * (i % 2) + j, :], ident[:])
                last.then_inc(fold_made, 1)
            pe.wait_ge(fold_out, 4)
            for hh in range(NH):
                pe.matmul(ps[:, 4 + hh // 4, hh % 4 * P:hh % 4 * P + P], wqT[:, hh, :], kT[:, hh, :], start=True, stop=True)
                last = pe.matmul(ps[0:1, 6 + hh // 4, hh % 4 * P:hh % 4 * P + P], bqt[:, hh:hh + 1], kT[:, hh, :],
                                 start=True, stop=True)
            last.then_inc(fold_made, 1)
            turn_ln(1)
            pe.wait_ge(w_in, 16 * 8)
            pe.wait_ge(fold_out, 8)
            pe.wait_ge(turned_out, 4)
            for i in range(2):
                for j in range(4):
                    if i:
                        pe.wait_ge(proj_out, j + 1)
                    pe.matmul(ps[:, j, :], wts[:, i, :], xT[:, j * QC:(j + 1) * QC], start=True, stop=True)\
                        .then_inc(proj, 1)
            for t in range(NT):
                if t >= 4:
                    pe.wait_ge(v_out, t - 3)
                pe.matmul(ps[:, 4 + t % 4, 0:C], xT[:, t * P:(t + 1) * P], wts[:, 2, :], start=True, stop=False)
                pe.matmul(ps[:, 4 + t % 4, 0:C], ones[0:1, :], rows[0:1, 0, :], start=False, stop=True)\
                    .then_inc(v_done, 1)

            MAX0 = [(par, x, qt, kh) for par in range(2) for x in range(2) for qt in range(KT) for kh in range(2)]

            def max_task(n, i):
                par, x, qt, kh = MAX0[i]
                if i == 0 and not (isinstance(n, int) and n == 0):
                    pe.wait_ge(shift_split, 4 * n)
                if not isinstance(n, int) or 64 * n + i >= 2:
                    pe.wait_ge(max_read, 64 * n + i - 1)
                pe.matmul(max_ps[:, i % 2, :], QS[:, n, 2 * x + par, qt * P:(qt + 1) * P],
                          KS[:, n, x, kh * QC:(kh + 1) * QC], start=True, stop=True).then_inc(max_scores, 1)

            def turn_max(n):
                pe.wait_ge(unit_max, n + 1)
                pe.transpose(max_ps[0:32, 0, 0:P], mx[:], ident[:]).then_inc(max_turned, 1)

            def pv(n, v):
                qh, kt = divmod(v, KT)
                if v == 0:
                    pe.wait_ge(v_staged, n + 1)
                if kt == 0 and (not isinstance(n, int) or 2 * n + qh >= 2):
                    pe.wait_ge(o_norm, 2 * n + qh - 1)
                pe.wait_ge(exp_done, 32 * n + 2 * v + 2)
                for hl in range(HL):
                    last = pe.matmul(o_ps[32 * hl:32 * hl + 32, qh, :], vst[:, kt, hl, :], probs[:, v % 2, hl, :],
                                     start=kt == 0, stop=kt == KT - 1)
                last.then_inc(pv_done, 1)

            def turn_o(n, qh):
                pe.wait_ge(o_read, 2 * n + qh + 1)
                for i in range(4):
                    last = pe.transpose(o_ps[:, qh, i * P:(i + 1) * P], osb[:, i * P:(i + 1) * P], ident[:])
                last.then_inc(o_turned, 1)

            def unit(n, more):
                pe.wait_ge(shift_rows, 16 * 12 * (n + 1))
                for e, (qh, kt, pr) in enumerate(STEPS0):
                    if not isinstance(n, int) or 32 * n + e >= 2:
                        pe.wait_ge(exp_done, 32 * n + e - 1)
                    for x in range(2):
                        last = pe.matmul(score_ps[:, e % 2, x, :], KS[:, n, pr, kt * P:(kt + 1) * P],
                                         QS[:, n, 2 * pr + x, qh * QC:(qh + 1) * QC], start=True, stop=True)
                    last.then_inc(scores_ready, 1)
                    if more:
                        max_task(n + 1, 2 * e)
                        max_task(n + 1, 2 * e + 1)
                    if e % 2 and e >= 3:
                        pv(n, e // 2 - 1)
                    if e == 22:
                        turn_o(n, 0)
                pv(n, 15)
                turn_o(n, 1)
                if more:
                    turn_max(n + 1)

            pe.wait_ge(v_out, NT)
            pe.wait_ge(stack_in, 16 * 48)
            for i in range(64):
                max_task(0, i)
            turn_max(0)
            unit(0, True)
            with pe.Fori(1, UNITS - 1) as n:
                unit(n, True)
            unit(UNITS - 1, False)

            pe.wait_ge(bn_ready, 1)
            for t in range(NT):
                last = pe.matmul(ps[:, 0, 0:C], ones[:], xn[:, t, :], start=t == 0, stop=t == NT - 1)
            last.then_inc(bn_made, 1)
            pe.wait_ge(bn_ready, 2)
            for t in range(NT):
                pe.matmul(ps[:, 1, 0:C], ones[:], tmp[:, t, :], start=t == 0, stop=t == NT - 1)
            for i in range(2):
                last = pe.matmul(ps[:, 2 + i, 0:C], ones[0:1, :], rows[0:1, 1 + i, :], start=True, stop=True)
            last.then_inc(bn_made, 1)
            pe.wait_ge(wd_in, 16)
            for r in range(8):
                if r >= 4:
                    pe.wait_ge(wd_out, r - 3)
                for i in range(4):
                    last = pe.transpose(ps[:, 4 + r % 4, i * P:(i + 1) * P], wdr[:, 4 * r + i, :], ident[:])
                last.then_inc(wd_turned, 1)
            turn_ln(3)
            pe.wait_ge(w1_in, 16 * 8)
            pe.wait_ge(turned_out, 8)
            for i in range(2):
                for j in range(4):
                    if i:
                        pe.wait_ge(proj1_out, j + 1)
                    pe.matmul(ps[0:E1, j, :], w1[:, i, :], xT[:, j * QC:(j + 1) * QC], start=True, stop=True)\
                        .then_inc(proj1, 1)
            pe.wait_ge(wd_out, 8)
            for t in range(NT):
                if t >= 4:
                    pe.wait_ge(v1_out, t - 3)
                pe.matmul(ps[:, 4 + t % 4, 0:E1], xT[:, t * P:(t + 1) * P], w1[:, 2, :], start=True, stop=False)
                pe.matmul(ps[:, 4 + t % 4, 0:E1], ones[0:1, :], rows1[0:1, 0, 0:E1], start=False, stop=True)\
                    .then_inc(v1_done, 1)

            def max1_task(b, i):
                kind, hl, qt, kh = MAX1[i]
                k = len(MAX1) * b + i
                if i == 0 and b:
                    pe.wait_ge(shift1_split, 4 * b)
                if k >= 2:
                    pe.wait_ge(max1_read, k - 1)
                k0, n = (kh * QC, QC) if kind == "full" else (window_of(qt)[0], 192)
                pe.matmul(max_ps[:, i % 2, 0:n], QS1[:, b, hl, qt * P:(qt + 1) * P], KS1[:, b, hl, k0:k0 + n],
                          start=True, stop=True).then_inc(max1_scores, 1)

            def turn_max1(b):
                pe.wait_ge(unit1_max, b + 1)
                pe.transpose(max_ps[0:64, 0, 0:P], mx1[:], ident[:]).then_inc(max1_turned, 1)

            def pv1(b, v):
                if v == 0:
                    pe.wait_ge(v1_staged, b + 1)
                if v < 16:
                    qh, kt = divmod(v, KT)
                    if kt == 0 and 4 * b + qh >= 2:
                        pe.wait_ge(o1_norm, 4 * b + qh - 1)
                    pe.wait_ge(scaled_dve, NV1 * b + v + 1)
                    pe.wait_ge(scaled_pool, 16 * b + v + 1)
                    for hl in range(HL):
                        last = pe.matmul(o_ps[32 * hl:32 * hl + 32, qh, :], vst[:, kt, hl, :], probs[:, v % 2, hl, :],
                                         start=kt == 0, stop=kt == KT - 1)
                else:
                    i, kt = WSTEPS[v - 16]
                    if i % 4 == 0 and kt == max(i - 1, 0):
                        pe.wait_ge(o1_norm, 4 * b + 2 + i // 4 - 1)
                    pe.wait_ge(scaled_dve, NV1 * b + v + 1)
                    for hl in range(HL):
                        last = pe.matmul(o_ps[32 * hl:32 * hl + 32, i // 4, i % 4 * P:i % 4 * P + P], vst[:, kt, hl, :],
                                         probs[:, v % 2, 0, hl * P:(hl + 1) * P],
                                         start=kt == max(i - 1, 0), stop=kt == min(i + 1, KT - 1))
                last.then_inc(pv1_done, 1)

            def turn_o1(w):
                pe.wait_ge(o1_read, w + 1)
                for i in range(4):
                    last = pe.transpose(o_ps[:, w % 2, i * P:(i + 1) * P], osb[:, i * P:(i + 1) * P], ident[:])
                last.then_inc(o1_turned, 1)

            def sequence(b, more):
                pe.wait_ge(shift1_rows, 16 * 6 * (b + 1))
                todo = 0
                for e in range(NE1):
                    if NE1 * b + e >= 2:
                        pe.wait_ge(exp1_done, NE1 * b + e - 1)
                    if e < len(STEPS1):
                        qh, kt, pr = STEPS1[e]
                        for x in range(2):
                            last = pe.matmul(score_ps[:, e % 2, x, :], KS1[:, b, 2 * pr + x, kt * P:(kt + 1) * P],
                                             QS1[:, b, 2 * pr + x, qh * QC:(qh + 1) * QC], start=True, stop=True)
                    else:
                        i, kt = WSTEPS[e - len(STEPS1)]
                        for hl in range(HL):
                            last = pe.matmul(score_ps[:, e % 2, 0, hl * P:(hl + 1) * P],
                                             KS1[:, b, hl, kt * P:(kt + 1) * P],
                                             QW1[:, b, hl, i * P:(i + 1) * P], start=True, stop=True)
                    last.then_inc(scores1_ready, 1)
                    if more:
                        while todo < min(len(MAX1), 2 * e + 2):
                            max1_task(b + 1, todo)
                            todo += 1
                    if e < len(STEPS1):
                        if e % 2 and e >= 3:
                            pv1(b, e // 2 - 1)
                    else:
                        pv1(b, e - len(STEPS1) + 15)
                    if e == 22:
                        turn_o1(4 * b)
                    if e == 36:
                        turn_o1(4 * b + 1)
                    if e == 48:
                        turn_o1(4 * b + 2)
                pv1(b, NV1 - 1)
                turn_o1(4 * b + 3)
                if more:
                    turn_max1(b + 1)

            pe.wait_ge(v1_out, NT)
            pe.wait_ge(stack1_in, 16 * 36)
            for i in range(len(MAX1)):
                max1_task(0, i)
            turn_max1(0)
            sequence(0, True)
            sequence(1, False)
            pe.wait_ge(attn1_done, 2 * B)
            for j in range(4):
                for i in range(4):
                    last = pe.transpose(ps[0:E1, j, i * P:(i + 1) * P], attn1[:, 4 * j + i, :], ident[:])
                last.then_inc(a_turned, 1)
            for j in range(4):
                pe.wait_ge(a_out, j + 1)
                for i in range(4):
                    t = 4 * j + i
                    o = ps[:, 4 + j, i * P:(i + 1) * P]
                    pe.matmul(o, aT[:, t * P:(t + 1) * P], wout[:], start=True, stop=False)
                    last = pe.matmul(o, ones[0:1, :], rows1[0:1, 1, :], start=False, stop=True)
                last.then_inc(wo_made, 1)
            turn_ln(4)

            def key_scores(t):
                pe.wait_ge(zt_staged, t + 1)
                if not isinstance(t, int) or t >= 1:
                    pe.wait_ge(s_picked, t)
                for i in range(2):
                    pe.matmul(ps[:, i, :], zt, wf[:, i * QC:(i + 1) * QC], start=True, stop=False)
                    last = pe.matmul(ps[:, i, :], ones[0:1, :], bf[0:1, i * QC:(i + 1) * QC], start=False, stop=True)
                last.then_inc(s_ready, 1)

            def turn_trip(t):
                pe.wait_ge(trip_done, t + 1)
                if not isinstance(t, int) or t >= 1:
                    pe.wait_ge(uvw_ready, 2 * t)
                for w in range(3):
                    last = pe.transpose(t_ps[:, w * P:(w + 1) * P], trip[:, w].rearrange("p d n -> p (d n)"), ident[:])
                last.then_inc(trip_turned, 1)

            def gates(t, g):
                pe.wait_ge(a_made, 8 * t + g + 1)
                pe.wait_ge(b_weighted, 8 * t + g + 1)
                if not (isinstance(t, int) and 8 * t + g < 2):
                    pe.wait_ge(ge_out, 8 * t + g - 1)
                for c in range(8):
                    last = pe.matmul(g_ps[:, g % 2, c * 64:(c + 1) * 64], onehot[:, g % 2, c, :], weigh[:, g % 2, c, :],
                                     start=True, stop=True)
                last.then_inc(g_made, 1)

            def inner(t, q):
                if not (isinstance(t, int) and 8 * t + q < 2):
                    pe.wait_ge(gr_done, 8 * t + q - 1)
                for i in range(4):
                    last = pe.matmul(in_ps[:, q % 2, i * P:(i + 1) * P], wdt[:, 4 * q + i, :], xT[:, bass.ts(t, P)],
                                     start=True, stop=True)
                last.then_inc(inner_ready, 1)

            def gather_out(t, q):
                pe.wait_ge(gr_done, 8 * t + q + 1)
                if q == 0 and not (isinstance(t, int) and t == 0):
                    pe.wait_ge(h_out, t)
                for i in range(4):
                    last = pe.matmul(acc_ps, gated[:, q % 2, i, :], wup[:, 4 * q + i, :],
                                     start=q == 0 and i == 0, stop=q == 7 and i == 3)
                last.then_inc(acc_used, 1)

            def tile(t, back, more):
                for g in range(8):
                    if more and g == 0:
                        key_scores(t + 1)
                    if back:
                        inner(t - 1, g)
                        if g:
                            gather_out(t - 1, g - 1)
                    gates(t, g)
                    if more and g == 6:
                        turn_trip(t + 1)
                if back:
                    gather_out(t - 1, 7)

            pe.wait_ge(turned_out, 12)
            pe.wait_ge(wu_in, 16)
            key_scores(0)
            turn_trip(0)
            tile(0, False, True)
            tile(1, True, True)
            with pe.Fori(1, NT // 2 - 1) as m:
                for x in range(2):
                    tile(2 * m + x, True, True)
            tile(NT - 2, True, True)
            tile(NT - 1, True, False)
            for q in range(8):
                inner(NT - 1, q)
                if q:
                    gather_out(NT - 1, q - 1)
            gather_out(NT - 1, 7)

        @block.vector
        def _(dve):
            order = Tally(dve, sem("dve_order"))
            dve.memset(big[:, 0:32768].bitcast(F32), 0.0).then_inc(zeroed, 1)
            dve.memset(big[:, 32768:49152], -1.0).then_inc(zeroed, 1)

            dve.memset(kbd, 0.0).then_inc(fold_ready, 1)
            dve.wait_ge(sem("gt_in"), 32)
            dve.wait_ge(dist_num, 1)
            order.then_wait(dve.tensor_copy(xT[:, 0:TW], dist[:].bitcast(I32)))
            order.then_wait(dve.tensor_tensor(xT[:, 0:TW], xT[:, 0:TW], xT[:, 0:TW], ALU.mult))
            dve.tensor_scalar(dist[:], xT[:, 0:TW], gt[:, 0:1], gt[:, 1:2], ALU.mult, ALU.subtract).then_inc(dist_arg, 1)

            def newton(r, x):
                s = stat[:, 5, :] if r is not bn_r else bn[:, 4, :]
                order.then_wait(dve.tensor_tensor(s, r, r, ALU.mult))
                order.then_wait(dve.tensor_tensor(s, s, x, ALU.mult))
                order.then_wait(dve.tensor_scalar(s, s, -0.5, 1.5, ALU.mult, ALU.add))
                order.then_wait(dve.tensor_tensor(r, r, s, ALU.mult))

            def layer_norm(k):
                order.then_wait(dve.tensor_reduce(stat[:, 0, :], h[:], X, ALU.add))
                order.then_wait(dve.tensor_scalar(stat[:, 1, :], stat[:, 0, :], 1.0 / C, None, ALU.mult))
                order.then_wait(dve.tensor_tensor(xn[:], h[:], spread(stat[:, 1, :], C), ALU.subtract))
                order.then_wait(dve.tensor_tensor(tmp[:], xn[:], xn[:], ALU.mult))
                order.then_wait(dve.tensor_reduce(stat[:, 0, :], tmp[:], X, ALU.add))
                dve.tensor_scalar(stat[:, 2, :], stat[:, 0, :], 1.0 / C, LN_EPS, ALU.mult, ALU.add).then_inc(ln_var, 1)
                dve.wait_ge(ln_sqrt, k)
                order.then_wait(dve.reciprocal(stat[:, 4, :], stat[:, 3, :]))
                newton(stat[:, 4, :], stat[:, 2, :])
                dve.tensor_tensor(xn[:], xn[:], spread(stat[:, 4, :], C), ALU.mult).then_inc(ln_done, 1)

            def take_turned(k):
                for j in range(4):
                    dve.wait_ge(turned, 4 * (k - 1) + j + 1)
                    dve.tensor_copy(xT[:, j * QC:(j + 1) * QC], ps[:, j, :]).then_inc(turned_out, 1)

            def split3(src, rows_, done, sent):
                scr = tmp[0:rows_].rearrange("p t c -> p (t c)")
                if sent:
                    dve.wait_ge(*sent)
                dve.tensor_copy(splits[0:rows_, 0, :], src).then_inc(done, 1)
                n = 3 if sent else 0
                dve.wait_ge(done, n + 1)
                order.then_wait(dve.tensor_tensor(scr, src, splits[0:rows_, 0, :], ALU.subtract))
                dve.tensor_copy(splits[0:rows_, 1, :], scr).then_inc(done, 1)
                dve.wait_ge(done, n + 2)
                dve.tensor_tensor(splits[0:rows_, 2, :], scr, splits[0:rows_, 1, :], ALU.subtract).then_inc(done, 1)
                dve.wait_ge(done, n + 3)

            dve.wait_ge(gathered, 16 * NT)
            layer_norm(1)
            take_turned(1)
            dve.wait_ge(proj_out, 4)
            split3(q_cm, C, split_done, None)
            dve.wait_ge(proj_out, 8)
            split3(k_cm, C, split_done, (split_out, 16))

            def max_read_task(n, i):
                par, x, qt, kh = i // 32, i // 16 % 2, i // 2 % 8, i % 2
                dve.wait_ge(max_scores, 64 * n + i + 1)
                dve.tensor_reduce(mhalf[:, i // 2, kh:kh + 1], max_ps[:, i % 2, :], X, ALU.max).then_inc(max_read, 1)

            def shift_of(n):
                dve.wait_ge(max_read, 64 * n + 64)
                if not isinstance(n, int) or n >= 1:
                    dve.wait_ge(max_turned, n)
                dve.tensor_reduce(mx[:], mhalf[:], X, ALU.max).then_inc(unit_max, 1)
                dve.wait_ge(max_turned, n + 1)
                if not isinstance(n, int) or n >= 1:
                    dve.wait_ge(shift_rows, 16 * 12 * n)
                src = max_ps[0:32, 0, 0:P]
                dve.tensor_copy(sh[:, 0, :], src).then_inc(shift_split, 1)
                dve.wait_ge(shift_split, 4 * n + 1)
                dve.tensor_tensor(shf[:], src, sh[:, 0, :], ALU.subtract).then_inc(shift_split, 1)
                dve.wait_ge(shift_split, 4 * n + 2)
                dve.tensor_copy(sh[:, 1, :], shf[:]).then_inc(shift_split, 1)
                dve.wait_ge(shift_split, 4 * n + 3)
                dve.tensor_tensor(sh[:, 2, :], shf[:], sh[:, 1, :], ALU.subtract).then_inc(shift_split, 1)

            def read_o(n, qh):
                dve.wait_ge(pv_done, 16 * n + 8 * qh + 8)
                if not isinstance(n, int) or 2 * n + qh >= 1:
                    dve.wait_ge(o_turned, 2 * n + qh)
                dve.tensor_copy(osb[:], o_ps[:, qh, :]).then_inc(o_read, 1)

            def norm_o(n, qh):
                dve.wait_ge(o_turned, 2 * n + qh + 1)
                if not isinstance(n, int) or 2 * n + qh >= 1:
                    dve.wait_ge(o_norm, 2 * n + qh)
                o = o_ps[:, qh, :].rearrange("p (t h m) -> p t h m", t=4, h=HL)
                dve.reciprocal(rden[:], o[:, :, :, D0]).then_inc(sem("rden_done"), 1)
                dve.wait_ge(sem("rden_done"), 2 * n + qh + 1)
                dst = attn[:, n, 4 * qh:4 * qh + 4, :].rearrange("p t (h d) -> p t h d", h=HL)
                dve.tensor_tensor(dst, o[:, :, :, 0:D0],
                                  rden[:].unsqueeze(3).broadcast_to([P, 4, HL, D0]), ALU.mult).then_inc(o_norm, 1)

            def unit(n, more):
                for e in range(32):
                    if more:
                        max_read_task(n + 1, 2 * e)
                        max_read_task(n + 1, 2 * e + 1)
                    if e == 20:
                        read_o(n, 0)
                    if e == 26:
                        norm_o(n, 0)
                read_o(n, 1)
                norm_o(n, 1)
                if more:
                    shift_of(n + 1)

            for i in range(64):
                max_read_task(0, i)
            shift_of(0)
            unit(0, True)
            with dve.Fori(1, UNITS - 1) as n:
                unit(n, True)
            unit(UNITS - 1, False)

            dve.wait_ge(o_norm, 2 * UNITS)
            for b in range(B):
                xb = xn[:, b * KT:(b + 1) * KT, :].rearrange("p t (g c) -> p g t c", g=4)
                last = dve.tensor_tensor(xb, xb, attn[:, 4 * b:4 * b + 4, :, :], ALU.add)
                if b == 0:
                    order.then_wait(last)
            last.then_inc(bn_ready, 1)
            dve.wait_ge(bn_ready, 1)

            def along_tokens(row):
                return row.unsqueeze(1).broadcast_to([P, NT, C])

            dve.wait_ge(bn_made, 1)
            order.then_wait(dve.tensor_scalar(bn[:, 0, :], ps[:, 0, 0:C], 1.0 / NTOK, None, ALU.mult))
            order.then_wait(dve.tensor_tensor(xn[:], xn[:], along_tokens(bn[:, 0, :]), ALU.subtract))
            dve.tensor_tensor(tmp[:], xn[:], xn[:], ALU.mult).then_inc(bn_ready, 1)
            dve.wait_ge(bn_made, 2)
            dve.tensor_scalar(bn[:, 1, :], ps[:, 1, 0:C], 1.0 / NTOK, BN_EPS, ALU.mult, ALU.add).then_inc(bn_ready, 1)
            dve.wait_ge(bn_root, 1)
            order.then_wait(dve.reciprocal(bn_r, bn[:, 2, :]))
            newton(bn_r, bn[:, 1, :])
            order.then_wait(dve.tensor_tensor(bn_r, bn_r, ps[:, 2, 0:C], ALU.mult))
            order.then_wait(dve.tensor_tensor(xn[:], xn[:], along_tokens(bn_r), ALU.mult))
            order.then_wait(dve.tensor_tensor(xn[:], xn[:], along_tokens(ps[:, 3, 0:C]), ALU.add))
            order.then_wait(dve.tensor_tensor(h[:], h[:], xn[:], ALU.add))
            layer_norm(2)
            dve.wait_ge(ln_done, 2)
            order.then_wait(dve.tensor_tensor(h[:], h[:], xn[:], ALU.add))
            layer_norm(3)
            take_turned(2)
            dve.wait_ge(proj1_out, 4)
            split3(q_cm[0:E1, :], E1, split1_done, None)
            dve.wait_ge(proj1_out, 8)
            split3(k_cm[0:E1, :], E1, split1_done, (split1_out, 16))

            def max1_read_task(b, i):
                kind, hl, qt, kh = MAX1[i]
                k = len(MAX1) * b + i
                dve.wait_ge(max1_scores, k + 1)
                if kind == "full":
                    dve.tensor_reduce(mhalf[:, i // 2, kh:kh + 1], max_ps[:, i % 2, :], X, ALU.max).then_inc(max1_read, 1)
                else:
                    at = window_of(qt)[1]
                    if k >= 2:
                        dve.wait_ge(max1_read, k - 1)
                    dve.tensor_tensor_reduce(wscr[:, i % 2, :], max_ps[:, i % 2, 0:192], wmask[:, at:at + 192], 1.0, -3e38,
                                             ALU.add, ALU.max, mx1[:, 32 + 8 * hl + qt:33 + 8 * hl + qt]).then_inc(max1_read, 1)

            def shift1_of(b):
                dve.wait_ge(max1_read, len(MAX1) * (b + 1))
                if b:
                    dve.wait_ge(max1_turned, b)
                dve.tensor_reduce(mx1[:, 0:32], mhalf[:], X, ALU.max).then_inc(unit1_max, 1)
                dve.wait_ge(max1_turned, b + 1)
                if b:
                    dve.wait_ge(shift1_rows, 16 * 6 * b)
                src = max_ps[0:64, 0, 0:P]
                dve.tensor_copy(sh1[:, 0, :], src).then_inc(shift1_split, 1)
                dve.wait_ge(shift1_split, 4 * b + 1)
                dve.tensor_tensor(shf1[:], src, sh1[:, 0, :], ALU.subtract).then_inc(shift1_split, 1)
                dve.wait_ge(shift1_split, 4 * b + 2)
                dve.tensor_copy(sh1[:, 1, :], shf1[:]).then_inc(shift1_split, 1)
                dve.wait_ge(shift1_split, 4 * b + 3)
                dve.tensor_tensor(sh1[:, 2, :], shf1[:], sh1[:, 1, :], ALU.subtract).then_inc(shift1_split, 1)

            def scale1(b, e):
                dve.wait_ge(exp1_done, NE1 * b + e + 1)
                if e < len(STEPS1):
                    qh, kt, pr = STEPS1[e]
                    at = qh * QC - kt * P + S - P
                    slot = probs[:, e // 2 % 2, 0:2, :]
                    by = dist[:, at:at + QC].unsqueeze(1).broadcast_to([P, 2, QC])
                else:
                    i, kt = WSTEPS[e - len(STEPS1)]
                    v = e - len(STEPS1) + 16
                    slot = probs[:, v % 2, 0, :].rearrange("p (h n) -> p h n", h=HL)
                    by = near[:, kt - i + 1, :].unsqueeze(1).broadcast_to([P, HL, P])
                dve.tensor_tensor(slot, slot, by, ALU.mult).then_inc(scaled_dve, 1)

            def read_o1(w):
                b, k = divmod(w, 4)
                dve.wait_ge(pv1_done, NV1 * b + (8, 16, 16 + 11, NV1)[k])
                if w:
                    dve.wait_ge(o1_turned, w)
                dve.tensor_copy(osb[:], o_ps[:, w % 2, :]).then_inc(o1_read, 1)

            def norm_o1(w):
                b, k = divmod(w, 4)
                dve.wait_ge(o1_turned, w + 1)
                o = o_ps[:, w % 2, :].rearrange("p (t h m) -> p t h m", t=4, h=HL)
                order.then_wait(dve.reciprocal(rden[:], o[:, :, :, D1]))
                at = KT * b + 4 * (k % 2)
                dst = attn1[:, at:at + 4, :].rearrange("p t (h d) -> p t h d", h=H1)
                r4 = rden[:].unsqueeze(3).broadcast_to([P, 4, H1, D1])
                if k < 2:
                    dve.scalar_tensor_tensor(out=dst, in0=o[:, :, :, 0:D1], scalar=0.5, in1=r4, op0=ALU.mult,
                                             op1=ALU.mult).then_inc(o1_norm, 1)
                    dve.wait_ge(o1_norm, w + 1)
                else:
                    o2 = xT[:, 0:4 * E1].rearrange("p (t h d) -> p t h d", t=4, h=H1)
                    dve.scalar_tensor_tensor(out=o2, in0=o[:, :, :, 0:D1], scalar=0.5, in1=r4, op0=ALU.mult,
                                             op1=ALU.mult).then_inc(o1_norm, 1)
                    dve.wait_ge(o1_norm, w + 1)
                    dve.tensor_tensor(dst, dst, o2, ALU.add).then_inc(attn1_done, 1)
                    dve.wait_ge(attn1_done, 2 * b + k - 1)

            def sequence(b, more):
                todo = 0
                for e in range(NE1):
                    if more:
                        while todo < min(len(MAX1), 2 * e + 2):
                            max1_read_task(b + 1, todo)
                            todo += 1
                    if e >= len(STEPS1) or STEPS1[e][2] == 0:
                        scale1(b, e)
                    if e == 20:
                        read_o1(4 * b)
                    if e == 26:
                        norm_o1(4 * b)
                    if e == 34:
                        read_o1(4 * b + 1)
                    if e == 37:
                        norm_o1(4 * b + 1)
                    if e == 46:
                        read_o1(4 * b + 2)
                    if e == 49:
                        norm_o1(4 * b + 2)
                read_o1(4 * b + 3)
                norm_o1(4 * b + 3)
                if more:
                    shift1_of(b + 1)

            for i in range(len(MAX1)):
                max1_read_task(0, i)
            shift1_of(0)
            sequence(0, True)
            sequence(1, False)
            for j in range(4):
                dve.wait_ge(wo_made, j + 1)
                hj = h[:, 4 * j:4 * j + 4, :]
                order.then_wait(dve.tensor_tensor(hj, hj, ps[:, 4 + j, :].rearrange("p (t c) -> p t c", t=4), ALU.add))
            layer_norm(4)
            take_turned(3)

            def key_max(t, g):
                for hh in range(2 * g, 2 * g + 2):
                    for q in range(2):
                        last = dve.max(top[:, hh, q, :], s_ps[:, hh, q, :])
                last.then_inc(pick_order, 1)

            def key_places(t, g):
                for hh in range(2 * g, 2 * g + 2):
                    for q in range(2):
                        last = dve.max_index(top_at[:, hh, q, :], top[:, hh, q, :], s_ps[:, hh, q, :])
                if g == 3:
                    last.then_inc(s_picked, 1)

            def pair_sums(t):
                dve.tensor_tensor(sums, top[:, :, 0, :].unsqueeze(3).broadcast_to([P, NH, TK, TK]),
                                  top[:, :, 1, :].unsqueeze(2).broadcast_to([P, NH, TK, TK]), ALU.add).then_inc(pick_order, 1)

            def pick_pairs(t):
                for hh in range(NH):
                    last = dve.max(best[:, hh, :], sums[:, hh].rearrange("p i j -> p (i j)"))
                last.then_inc(pick_order, 1)
                dve.wait_ge(pick_order, PICKS * t + 6)
                dve.tensor_tensor(evd, best, best[:, :, 0:1].broadcast_to([P, NH, TK]), ALU.subtract).then_inc(diff_done, 1)
                for hh in range(NH):
                    last = dve.max_index(best_at[:, hh, :], best[:, hh, :], sums[:, hh].rearrange("p i j -> p (i j)"))
                last.then_inc(pick_order, 1)
                dve.wait_ge(pick_order, PICKS * t + 7)
                dve.tensor_scalar(side[0], best_at, 3, None, ALU.logical_shift_right)
                dve.tensor_scalar(side[1], best_at, 7, None, ALU.bitwise_and).then_inc(pick_order, 1)
                dve.wait_ge(pick_order, PICKS * t + 8)

            def pick_experts(t):
                dve.wait_ge(s_picked, t + 1)
                eight = iota_f[:, 0:TK].unsqueeze(1).unsqueeze(1).broadcast_to([P, NH, TK, TK])
                for q in range(2):
                    last = dve.tensor_tensor(match[q], side[q].unsqueeze(3).broadcast_to([P, NH, TK, TK]), eight, ALU.is_equal)
                last.then_inc(pick_order, 1)
                dve.wait_ge(pick_order, PICKS * t + 9)
                for q in range(2):
                    last = dve.tensor_tensor(match[q], match[q],
                                             top_at[:, :, q, :].unsqueeze(2).broadcast_to([P, NH, TK, TK]), ALU.mult)
                last.then_inc(pick_order, 1)
                dve.wait_ge(pick_order, PICKS * t + 10)
                for q in range(2):
                    last = dve.tensor_reduce(key_at[q].rearrange("p (h k) -> p h k", h=NH), match[q], X, ALU.add)
                last.then_inc(pick_order, 1)
                dve.wait_ge(pick_order, PICKS * t + 11)
                dve.tensor_scalar(upper, key_at[1], float(VL), None, ALU.is_ge).then_inc(pick_order, 1)
                dve.wait_ge(pick_order, PICKS * t + 12)
                if not isinstance(t, int) or t >= 1:
                    dve.wait_ge(trip_turned, t)
                dve.scalar_tensor_tensor(out=trip[:, 0, 0, :], in0=key_at[0], scalar=2.0, in1=upper, op0=ALU.mult, op1=ALU.add)
                dve.scalar_tensor_tensor(out=trip[:, 1, 0, :], in0=upper, scalar=-float(VL), in1=key_at[1], op0=ALU.mult,
                                         op1=ALU.add).then_inc(pick_order, 1)
                dve.wait_ge(pick_order, PICKS * t + 13)
                dve.tensor_copy(trip[:, 0, 1, :], trip[:, 0, 0, :])
                dve.tensor_scalar(trip[:, 1, 1, :], trip[:, 1, 0, :], float(VL), None, ALU.add)
                dve.wait_ge(pexp_done, t + 1)
                dve.tensor_reduce(esum, ev, X, ALU.add).then_inc(pick_order, 1)
                dve.wait_ge(pick_order, PICKS * t + 14)
                dve.reciprocal(rsum, esum).then_inc(pick_order, 1)
                dve.wait_ge(pick_order, PICKS * t + 15)
                for d in range(2):
                    last = dve.tensor_tensor(trip[:, 2, d, :].rearrange("p (h k) -> p h k", h=NH), ev, spread(rsum, TK), ALU.mult)
                last.then_inc(trip_done, 1)

            PICKS = 15

            def onehot_v(t, x, g):
                if g == 0:
                    dve.wait_ge(uvw_ready, 2 * t + 2)
                if not (isinstance(t, int) and 8 * t + g < 2):
                    dve.wait_ge(g_made, 8 * t + g - 1)
                dve.tensor_tensor(weigh[:, g % 2], iota_f[:, 0:64].unsqueeze(1).broadcast_to([P, 8, 64]),
                                  spread(uvw[:, x, 1, 8 * g:8 * g + 8], 64), ALU.is_equal).then_inc(b_made, 1)

            def onehot_u(t, x, g):
                dve.tensor_tensor(onehot[:, g % 2], iota_f[:].unsqueeze(1).broadcast_to([P, 8, P]),
                                  spread(uvw[:, x, 0, 8 * g:8 * g + 8], P), ALU.is_equal).then_inc(a_made, 1)

            def gate_inner(t, x, q):
                dve.wait_ge(inner_ready, 8 * t + q + 1)
                if q == 0:
                    dve.wait_ge(ge_out, 8 * t + 8)
                if not (isinstance(t, int) and 8 * t + q < 2):
                    dve.wait_ge(acc_used, 8 * t + q - 1)
                dve.scalar_tensor_tensor(out=gated[:, q % 2], in0=in_ps[:, q % 2, :].rearrange("p (i n) -> p i n", i=4),
                                         scalar=0.0, in1=ge[:, x, 4 * q:4 * q + 4, :], op0=ALU.max, op1=ALU.mult)\
                    .then_inc(gr_done, 1)

            def add_out(t):
                dve.wait_ge(acc_used, 8 * t + 8)
                ht = h[:, bass.ts(t, 1), :].rearrange("p o c -> p (o c)")
                dve.tensor_tensor(ht, ht, acc_ps, ALU.add).then_inc(h_out, 1)

            def tile(t, x, back, more):
                for g in range(8):
                    if more and g == 0:
                        dve.wait_ge(s_ready, t + 2)
                    onehot_v(t, x, g)
                    if more and g < 4:
                        key_max(t + 1, g)
                        dve.wait_ge(pick_order, PICKS * (t + 1) + g + 1)
                    if more and g == 4:
                        pair_sums(t + 1)
                        dve.wait_ge(pick_order, PICKS * (t + 1) + 5)
                    onehot_u(t, x, g)
                    if more and g < 4:
                        key_places(t + 1, g)
                    if more and g == 4:
                        pick_pairs(t + 1)
                    if more and g == 5:
                        pick_experts(t + 1)
                    if back:
                        gate_inner(t - 1, 1 - x, g)
                if back:
                    add_out(t - 1)

            dve.wait_ge(s_ready, 1)
            for g in range(4):
                key_max(0, g)
                dve.wait_ge(pick_order, g + 1)
                key_places(0, g)
            pair_sums(0)
            dve.wait_ge(pick_order, 5)
            pick_pairs(0)
            pick_experts(0)
            tile(0, 0, False, True)
            tile(1, 1, True, True)
            with dve.Fori(1, NT // 2 - 1) as m:
                for x in range(2):
                    tile(2 * m + x, x, True, True)
            tile(NT - 2, 0, True, True)
            tile(NT - 1, 1, True, False)
            for q in range(8):
                gate_inner(NT - 1, 1, q)
            add_out(NT - 1)


def kernel(**inputs):
    import numpy as np
    import concourse.bacc as bacc
    from concourse.bass_utils import run_bass_kernel_spmd

    nc = bacc.Bacc("TRN2", target_bir_lowering=False, num_devices=1)
    arrays, aps = {}, {}

    def put(name, arr):
        arr = np.ascontiguousarray(arr)
        arrays[name + "_in"] = arr
        aps[name] = nc.dram_tensor(name + "_in", arr.shape, mybir.dt.from_np(arr.dtype), kind="ExternalInput").ap()

    put("tok", np.asarray(inputs["x"]).reshape(NT, P).T)
    put("emb", np.asarray(inputs["L0_tok_W"]).T)
    put("bqt", np.asarray(inputs["L1_ffn_bq"]).reshape(NH, P).T)
    for name in _WEIGHTS:
        put(name, np.asarray(inputs[name]))
    for name in ("L1_attn_gamma", "L1_attn_theta"):
        put(name, np.asarray(inputs[name]).reshape(1))
    out = nc.dram_tensor("out_dram", (B, S, C), F32, kind="ExternalOutput").ap()
    build_tower(nc, aps, out)
    r = run_bass_kernel_spmd(nc, [arrays], core_ids=[0])
    return r.results[0]["out_dram"]


_WEIGHTS = ["L0_attn_wq", "L0_attn_bq", "L0_attn_wk", "L0_attn_bk", "L0_attn_wv", "L0_attn_bv",
            "L0_attn_gamma", "L0_attn_beta", "L1_attn_Wq", "L1_attn_bq", "L1_attn_Wk", "L1_attn_bk",
            "L1_attn_Wv", "L1_attn_bv", "L1_attn_Wout", "L1_attn_bout", "L1_ffn_Wq", "L1_ffn_keys",
            "L1_ffn_w_down", "L1_ffn_w_up"]
```

```python
from contextlib import ExitStack

import concourse.bass as bass
from concourse import mybir

F32 = mybir.dt.float32
BF16 = mybir.dt.bfloat16
U32 = mybir.dt.uint32
I32 = mybir.dt.int32
ALU = mybir.AluOpType
ACT = mybir.ActivationFunctionType
X = mybir.AxisListType.X

P = 128
C = 128
B = 2
S = 1024
NTOK = B * S
NT = NTOK // P
KT = S // P
HL = 4
H0, D0 = 16, 8
UNITS = B * H0 // HL
H1, D1 = 4, 16
E1 = H1 * D1
WIN = 32
QC = 512
LN_EPS, BN_EPS = 1e-5, 1e-3
BIG = 1e30
Q_PART = (0, 0, 1, 0, 2, 1)
K_PART = (0, 1, 0, 2, 0, 1)
LEAD0 = 20
SHIFT0 = len(Q_PART) * D0
SHIFT1 = len(Q_PART) * D1
TW = S + S - P
NH, NK, TK = 8, 64, 8
PAIRS = NH * TK
UH, VL = 128, 32
HT = P // 2


class Tally:

    def __init__(self, eng, sem):
        self.eng, self.sem, self.n = eng, sem, 0

    def then_wait(self, ins):
        ins.then_inc(self.sem, 1)
        self.n += 1
        self.eng.wait_ge(self.sem, self.n)


def build_tower(nc, a, out):
    ctx = ExitStack()
    with ctx:
        def sb(name, shape, dt=F32):
            return ctx.enter_context(nc.sbuf_tensor(name, shape, dt))

        sems = {}

        def sem(name):
            if name not in sems:
                sems[name] = ctx.enter_context(nc.semaphore(name))
            return sems[name]

        h = sb("h", [P, NT, C])
        xn = sb("xn", [P, NT, C])
        tmp = sb("tmp", [P, NT, C])
        xT = sb("xT", [C, NTOK])
        stat = sb("stat", [P, 8, NT])
        ident = sb("ident", [P, P])
        ones = sb("ones", [P, P])
        idx = sb("idx", [P, NT], I32)
        wts = sb("wts", [C, 3, C])
        cols = sb("cols", [C, 4])
        rows = sb("rows", [1, 4, C])
        big = sb("big", [P, 48 * 1024], BF16)
        vall = sb("vall", [P, UNITS, KT, HL, D0 + 1])
        vst = sb("vst", [P, KT, HL, 32])
        probs = sb("probs", [P, 2, HL, QC])
        osb = sb("osb", [P, QC])
        mhalf = sb("mhalf", [P, 32, 2])
        mx = sb("mx", [P, 32])
        shf = sb("shf", [32, P])
        sh = sb("sh", [32, 3, P], BF16)
        rden = sb("rden", [P, 4, HL])
        bn = sb("bn", [P, 5, C])
        bn_r = bn[:, 3, :]
        w1 = sb("w1", [C, 3, E1])
        wout = sb("wout", [E1, C])
        cols1 = sb("cols1", [E1, 2])
        rows1 = sb("rows1", [1, 2, C])
        gt = sb("gt", [P, 2])
        dist = sb("dist", [P, TW])
        near = sb("near", [P, 3, P])
        wmask = sb("wmask", [P, 256])
        wscr = sb("wscr", [P, 2, 192])
        mx1 = sb("mx1", [P, 64])
        wf = sb("wf", [C, NH * P])
        bf = sb("bf", [1, NH * P])
        bqt = sb("bqt", [P, NH])
        bf3 = sb("bf3", [3, NH * P], BF16)
        ones3 = sb("ones3", [3, P], BF16)
        ps = ctx.enter_context(nc.psum_tensor("ps", [P, 8, QC], F32))
        score_ps = ps[:, 0:4, :].rearrange("p (s x) n -> p s x n", s=2)
        max_ps = ps[:, 4:6, :]
        o_ps = ps[:, 6:8, :]

        QS = big[:, 0:32768].rearrange("p (r u x n) -> p r u x n", r=2, u=UNITS, x=2)
        KS = big[:, 32768:49152].rearrange("p (u h n) -> p u h n", u=UNITS, h=2)
        attn = tmp[:].rearrange("p t c -> p (t c)").rearrange("p (u t c) -> p u t c", u=UNITS, t=KT)
        q_cm = probs[:].rearrange("p a b n -> p (a b n)")[:, 0:NTOK]
        k_cm = probs[:].rearrange("p a b n -> p (a b n)")[:, NTOK:2 * NTOK]
        splits = sb("splits", [C, 3, NTOK], BF16)
        bfs = splits[0:1, :, 0:NH * P]

        def part(at, n):
            return big[:, at:at + n]
        QS1 = part(0, 8192).rearrange("p (b h n) -> p b h n", b=B, h=H1)
        QW1 = part(8192, 8192).rearrange("p (b h n) -> p b h n", b=B, h=H1)
        KS1 = part(16384, 8192).rearrange("p (b h n) -> p b h n", b=B, h=H1)
        wdt = part(24576, 8192).bitcast(F32).rearrange("p (v u) -> p v u", v=VL)
        wup = part(32768, 8192).bitcast(F32).rearrange("p (v d) -> p v d", v=VL)
        wdr = part(40960, 8192).bitcast(F32).rearrange("p (v d) -> p v d", v=VL)
        sh1 = sb("sh1", [64, 3, P], BF16)
        shf1 = sb("shf1", [64, P])
        vall1 = vall[:].rearrange("p u t h d -> p (u t h d)")[:, 0:B * KT * H1 * (D1 + 1)]\
            .rearrange("p (b t h d) -> p b t h d", b=B, t=KT, h=H1)
        attn1 = tmp[:].rearrange("p t c -> p (t c)")[:, 0:NT * E1].rearrange("p (t c) -> p t c", t=NT)
        aT = xT[0:E1, :]
        ge = part(0, 16384).bitcast(F32).rearrange("p (x v n) -> p x v n", x=2, v=VL)
        onehot = part(16384, 4096).bitcast(F32).rearrange("p (x c u) -> p x c u", x=2, c=8)
        weigh = part(20480, 2048).bitcast(F32).rearrange("p (x c v) -> p x c v", x=2, c=8)
        gated = part(22528, 2048).bitcast(F32).rearrange("p (x i n) -> p x i n", x=2, i=4)
        flat = probs[:].rearrange("p a b n -> p (a b n)")
        room = [0]

        def pick(n):
            room[0] += n
            return flat[:, room[0] - n:room[0]]
        top = pick(128).rearrange("p (h q k) -> p h q k", h=NH, q=2)
        top_at = pick(128).bitcast(U32).rearrange("p (h q k) -> p h q k", h=NH, q=2)
        sums = pick(512).rearrange("p (h i j) -> p h i j", h=NH, i=TK)
        best = pick(64).rearrange("p (h k) -> p h k", h=NH)
        best_at = pick(64).bitcast(U32).rearrange("p (h k) -> p h k", h=NH)
        side = [pick(64).bitcast(U32).rearrange("p (h k) -> p h k", h=NH) for _ in range(2)]
        match = [pick(512).rearrange("p (h k i) -> p h k i", h=NH, k=TK) for _ in range(2)]
        key_at = [pick(64) for _ in range(2)]
        upper = pick(64)
        ev = pick(64).rearrange("p (h k) -> p h k", h=NH)
        evd = pick(64).rearrange("p (h k) -> p h k", h=NH)
        esum = pick(8)
        rsum = pick(8)
        trip = pick(384).rearrange("p (w d n) -> p w d n", w=3, d=2)
        uvw = pick(384).rearrange("p (x w n) -> p x w n", x=2, w=3)
        zt = pick(128)
        assert room[0] <= flat.shape[1]
        iota_f = sb("iota_f", [P, P])
        kbd = flat[:, 0:1024].rearrange("p (h c) -> p h c", h=NH)
        wqr = flat[:, 1024:2048]
        wqT = flat[:, 2048:3072].rearrange("p (h c) -> p h c", h=NH)
        kT = flat[:, 3072:4096].rearrange("p (h n) -> p h n", h=NH)
        s_ps = ps[:, 0:2, :].rearrange("p a n -> p (a n)").rearrange("p (h q n) -> p h q n", h=NH, q=2)
        g_ps, in_ps, acc_ps, t_ps = ps[:, 2:4, :], ps[:, 4:6, :], ps[:, 6, 0:C], ps[:, 7, :]

        q_scr = nc.dram_tensor("q_scr", [3, C, NTOK], BF16).ap()
        k_scr = nc.dram_tensor("k_scr", [3, C, NTOK], BF16).ap()
        q1_scr = nc.dram_tensor("q1_scr", [3, E1, NTOK], BF16).ap()
        k1_scr = nc.dram_tensor("k1_scr", [3, E1, NTOK], BF16).ap()
        out_v = out.rearrange("b (t p) c -> p (b t) c", p=P)

        def spread(col, n):
            return col.unsqueeze(2).broadcast_to([col.shape[0], col.shape[1], n])

        t_par = [0]

        block = ctx.enter_context(nc.Block())

        w_in, tok_in, gathered = sem("w_in"), sem("tok_in"), sem("gathered")
        consts, consts_f, zeroed = sem("consts"), sem("consts_f"), sem("zeroed")
        ln_var, ln_sqrt, ln_done = sem("ln_var"), sem("ln_sqrt"), sem("ln_done")
        turned, turned_out = sem("turned"), sem("turned_out")
        proj, proj_out = sem("proj"), sem("proj_out")
        split_done, split_out, stack_in = sem("split_done"), sem("split_out"), sem("stack_in")
        v_done, v_out = sem("v_done"), sem("v_out")
        max_scores, max_read, unit_max = sem("max_scores"), sem("max_read"), sem("unit_max")
        max_turned, shift_split, shift_rows = sem("max_turned"), sem("shift_split"), sem("shift_rows")
        scores_ready, exp_done, pv_done = sem("scores_ready"), sem("exp_done"), sem("pv_done")
        v_staged, o_read, o_turned, o_norm = sem("v_staged"), sem("o_read"), sem("o_turned"), sem("o_norm")
        saved = sem("saved")
        bn_ready, bn_made, bn_root = sem("bn_ready"), sem("bn_made"), sem("bn_root")
        w1_in, fold_in, fold_ready, fold_made, fold_out = (sem(x) for x in (
            "w1_in", "fold_in", "fold_ready", "fold_made", "fold_out"))
        dist_num, dist_arg, dist_done = sem("dist_num"), sem("dist_arg"), sem("dist_done")
        wd_in, wu_in, wd_turned, wd_out = sem("wd_in"), sem("wu_in"), sem("wd_turned"), sem("wd_out")
        proj1, proj1_out, split1_done, split1_out, stack1_in = (sem(x) for x in (
            "proj1", "proj1_out", "split1_done", "split1_out", "stack1_in"))
        zeroed1, v1_done, v1_out = sem("zeroed1"), sem("v1_done"), sem("v1_out")
        max1_scores, max1_read, unit1_max, max1_turned, shift1_split, shift1_rows = (sem(x) for x in (
            "max1_scores", "max1_read", "unit1_max", "max1_turned", "shift1_split", "shift1_rows"))
        scores1_ready, exp1_done, scaled_dve, scaled_pool, pv1_done = (sem(x) for x in (
            "scores1_ready", "exp1_done", "scaled_dve", "scaled_pool", "pv1_done"))
        v1_staged, o1_read, o1_turned, o1_norm = (sem(x) for x in ("v1_staged", "o1_read", "o1_turned", "o1_norm"))
        attn1_done, a_turned, a_out, wo_made, wo_added = (sem(x) for x in (
            "attn1_done", "a_turned", "a_out", "wo_made", "wo_added"))
        zt_staged, s_ready, s_picked, diff_done, pexp_done, trip_done, trip_turned, uvw_ready = (sem(x) for x in (
            "zt_staged", "s_ready", "s_picked", "diff_done", "pexp_done", "trip_done", "trip_turned", "uvw_ready"))
        a_made, b_made, b_weighted, g_made, ge_out, inner_ready, gr_done, acc_used, h_out = (sem(x) for x in (
            "a_made", "b_made", "b_weighted", "g_made", "ge_out", "inner_ready", "gr_done", "acc_used", "h_out"))
        pick_order, bf_split, bf_in = sem("pick_order"), sem("bf_split"), sem("bf_in")

        STEPS1 = [(qh, kt, pr) for qh in range(2) for kt in range(KT) for pr in range(2)]
        WSTEPS = [(i, k) for i in range(KT) for k in (i - 1, i, i + 1) if 0 <= k < KT]
        NE1, NV1 = len(STEPS1) + len(WSTEPS), KT * 2 + len(WSTEPS)
        MAX1 = [("full", hl, qt, kh) for hl in range(HL) for qt in range(KT) for kh in range(2)] + \
               [("near", hl, qt, 0) for hl in range(HL) for qt in range(KT)]

        def window_of(qt):
            return (0, 64) if qt == 0 else (S - 192, 0) if qt == KT - 1 else (qt * P - WIN, 32)

        STEPS0 = [(qh, kt, pr) for qh in range(2) for kt in range(KT) for pr in range(2)]
        MAX0 = [(par, x, qt, kh) for par in range(2) for x in range(2) for qt in range(KT) for kh in range(2)]
        MAXED = (len(MAX0) - LEAD0) // 2 - 1

        def max_unit_at(n, k, left):
            ahead, i = divmod(k + LEAD0, len(MAX0))
            return (n + 1 + ahead, i) if left > ahead else None

        @block.sync
        def _(sp):
            for i, w in enumerate(("L0_attn_wq", "L0_attn_wk", "L0_attn_wv")):
                sp.dma_start(wts[:, i, :], a[w]).then_inc(w_in, 16)
            for i, w in enumerate(("L0_attn_bq", "L0_attn_bk")):
                sp.dma_start(cols[:, i:i + 1], a[w].rearrange("(c o) -> c o", o=1)).then_inc(w_in, 16)
            for i, w in enumerate(("L0_attn_bv", "L0_attn_gamma", "L0_attn_beta")):
                sp.dma_start(rows[:, i, :], a[w].rearrange("(o c) -> o c", o=1)).then_inc(w_in, 16)
            for i, w in enumerate(("L1_attn_Wq", "L1_attn_Wk", "L1_attn_Wv")):
                sp.dma_start(w1[:, i, :], a[w]).then_inc(w1_in, 16)
            sp.dma_start(wout[:], a["L1_attn_Wout"]).then_inc(w1_in, 16)
            for i, w in enumerate(("L1_attn_bq", "L1_attn_bk")):
                sp.dma_start(cols1[:, i:i + 1], a[w].rearrange("(c o) -> c o", o=1)).then_inc(w1_in, 16)
            sp.dma_start(rows1[:, 0, 0:E1], a["L1_attn_bv"].rearrange("(o c) -> o c", o=1)).then_inc(w1_in, 16)
            sp.dma_start(rows1[:, 1, :], a["L1_attn_bout"].rearrange("(o c) -> o c", o=1)).then_inc(w1_in, 16)
            sp.dma_start(wqr, a["L1_ffn_Wq"]).then_inc(fold_in, 16)
            sp.dma_start(bqt[:], a["bqt"]).then_inc(fold_in, 16)
            sp.wait_ge(fold_ready, 1)
            for q in range(2):
                sp.dma_start(kbd[NK * q:NK * q + NK, :, NK * q:NK * q + NK],
                             a["L1_ffn_keys"][:, q].rearrange("h n c -> n h c")).then_inc(fold_in, 16)
            sp.wait_ge(bf_split, 1)
            sp.dma_start(bf3[:], bfs).then_inc(bf_in, 16)
            sp.wait_ge(split_done, 3)
            sp.dma_start(q_scr.rearrange("s c t -> c s t"), splits[:]).then_inc(split_out, 16)
            sp.wait_ge(split_done, 6)
            sp.dma_start(k_scr.rearrange("s c t -> c s t"), splits[:]).then_inc(split_out, 16)
            sp.wait_ge(split_out, 32)
            sp.wait_ge(zeroed, 2)
            Q8 = big[:, 0:32768].rearrange("p (r b g n) -> p r b g n", r=2, b=B, g=8)
            K8 = big[:, 32768:49152].rearrange("p (b g n) -> p b g n", b=B, g=8)
            for b in range(B):
                for r in range(len(Q_PART)):
                    for par in range(2):
                        at = 64 * par + D0 * r
                        qsrc = q_scr[Q_PART[r], :, b * S:(b + 1) * S].rearrange("(g r d) t -> r d g t", r=2, d=D0)
                        ksrc = k_scr[K_PART[r], :, b * S:(b + 1) * S].rearrange("(g r d) t -> r d g t", r=2, d=D0)
                        sp.dma_start(Q8[at:at + D0, par, b, :, :], qsrc[par]).then_inc(stack_in, 16)
                        sp.dma_start(K8[at:at + D0, b, :, :], ksrc[par]).then_inc(stack_in, 16)

            def send_shift(n):
                sp.wait_ge(shift_split, 4 * n + 4)
                for i in range(3):
                    for par in range(2):
                        at = 64 * par + SHIFT0 + i
                        sp.dma_start(QS[at:at + 1, par, n, :, :].rearrange("o x (t n) -> o (x t) n", n=P),
                                     sh[16 * par:16 * par + 16, i, :]).then_inc(shift_rows, 16)

            with sp.Fori(0, UNITS) as n:
                send_shift(n)
            sp.wait_ge(pv_done, 16 * UNITS)
            sp.dma_start(wdr, a["L1_ffn_w_down"].rearrange("(u v) d -> u v d", v=VL)).then_inc(wd_in, 16)
            sp.dma_start(wup, a["L1_ffn_w_up"].rearrange("(u v) d -> u v d", v=VL)).then_inc(wu_in, 16)
            sp.wait_ge(split1_done, 3)
            sp.dma_start(q1_scr.rearrange("s c t -> c s t"), splits[0:E1, :, :]).then_inc(split1_out, 16)
            sp.wait_ge(split1_done, 6)
            sp.dma_start(k1_scr.rearrange("s c t -> c s t"), splits[0:E1, :, :]).then_inc(split1_out, 16)
            sp.wait_ge(split1_out, 32)
            sp.wait_ge(zeroed1, 3)
            for b in range(B):
                for r in range(len(Q_PART)):
                    at = D1 * r
                    qsrc = q1_scr[Q_PART[r], :, b * S:(b + 1) * S].rearrange("(h d) t -> d h t", d=D1)
                    ksrc = k1_scr[K_PART[r], :, b * S:(b + 1) * S].rearrange("(h d) t -> d h t", d=D1)
                    sp.dma_start(QS1[at:at + D1, b, :, :], qsrc).then_inc(stack1_in, 16)
                    sp.dma_start(KS1[at:at + D1, b, :, :], ksrc).then_inc(stack1_in, 16)
                    sp.dma_start(QW1[at:at + D1, b, :, :], qsrc).then_inc(stack1_in, 16)
            for b in range(B):
                sp.wait_ge(shift1_split, 4 * b + 4)
                for i in range(3):
                    at = SHIFT1 + i
                    sp.dma_start(QS1[at:at + 1, b, :, :].rearrange("o h (t n) -> o (h t) n", n=P),
                                 sh1[0:32, i, :]).then_inc(shift1_rows, 16)
                    sp.dma_start(QW1[at:at + 1, b, :, :].rearrange("o h (t n) -> o (h t) n", n=P),
                                 sh1[32:64, i, :]).then_inc(shift1_rows, 16)
            with sp.Fori(0, NT) as t:
                sp.wait_ge(h_out, t + 1)
                sp.dma_start(out_v[:, t, :], h[:, t, :]).then_inc(saved, 16)
            sp.wait_ge(saved, 16 * NT)

        @block.gpsimd
        def _(pool):
            pool.dma_start(idx[:], a["tok"]).then_inc(tok_in, 16)
            for i, w in enumerate(("L1_attn_gamma", "L1_attn_theta")):
                pool.dma_start(gt[:, i:i + 1], a[w].partition_broadcast(P)).then_inc(sem("gt_in"), 16)
            pool.memset(ident[:], 0.0).then_inc(consts, 1)
            pool.memset(ones[:], 1.0).then_inc(consts, 1)
            pool.memset(ones3[:], 1.0).then_inc(consts_f, 1)
            pool.wait_ge(consts, 2)
            pool.affine_select(out=ident[:], in_=ident[:], compare_op=ALU.not_equal, fill=1.0, base=0,
                               pattern=[[-1, P]], channel_multiplier=1).then_inc(consts, 1)
            pool.wait_ge(tok_in, 16)
            for t in range(NT):
                pool.indirect_dma_start(h[:, t, :], None, a["emb"],
                                        bass.IndirectOffsetOnAxis(idx[:, t:t + 1].bitcast(U32), 0)).then_inc(gathered, 16)
            pool.iota(dist[:].bitcast(I32), [[1, TW]], base=-(S - P), channel_multiplier=-1).then_inc(dist_num, 1)
            pool.iota(iota_f[:], [[1, P]], base=0, channel_multiplier=0,
                      allow_small_or_imprecise_dtypes=True).then_inc(consts_f, 1)
            pool.memset(wmask[:], 0.0).then_inc(consts_f, 1)
            pool.wait_ge(consts_f, 3)
            pool.affine_select(out=wmask[:], in_=wmask[:], compare_op=ALU.is_ge, fill=-BIG, base=64 + WIN,
                               pattern=[[-1, 256]], channel_multiplier=1).then_inc(consts_f, 1)
            pool.wait_ge(consts_f, 4)
            pool.affine_select(out=wmask[:], in_=wmask[:], compare_op=ALU.is_ge, fill=-BIG, base=WIN - 64,
                               pattern=[[1, 256]], channel_multiplier=-1).then_inc(consts_f, 1)
            pool.wait_ge(dist_done, 3)
            for d in range(3):
                src = S - P - P * (d - 1)
                pool.tensor_copy(near[:, d, :], dist[:, src:src + P]).then_inc(consts_f, 1)
                pool.wait_ge(consts_f, 5 + 3 * d + 1)
                pool.affine_select(out=near[:, d, :], in_=near[:, d, :], compare_op=ALU.is_ge, fill=0.0,
                                   base=WIN + P * (d - 1), pattern=[[-1, P]], channel_multiplier=1).then_inc(consts_f, 1)
                pool.wait_ge(consts_f, 5 + 3 * d + 2)
                pool.affine_select(out=near[:, d, :], in_=near[:, d, :], compare_op=ALU.is_ge, fill=0.0,
                                   base=WIN - P * (d - 1), pattern=[[1, P]], channel_multiplier=-1).then_inc(consts_f, 1)
            pool.memset(vst[:], 0.0).then_inc(consts, 1)
            pool.memset(vall[:, :, :, :, D0:D0 + 1], 1.0).then_inc(consts, 1)
            pool.wait_ge(consts, 5)
            pool.wait_ge(v_out, NT)
            pool.tensor_copy(vst[:, :, :, 0:D0 + 1], vall[:, 0, :, :, :]).then_inc(v_staged, 1)
            with pool.Fori(1, UNITS) as n:
                pool.wait_ge(pv_done, 16 * n)
                pool.tensor_copy(vst[:, :, :, 0:D0 + 1], vall[:, n, :, :, :]).then_inc(v_staged, 1)
            pool.wait_ge(pv_done, 16 * UNITS)
            pool.memset(vall1[:, :, :, :, D1:D1 + 1], 1.0).then_inc(zeroed1, 1)
            pool.memset(part(0, 16384).bitcast(F32), 0.0).then_inc(zeroed1, 1)
            pool.memset(part(16384, 8192), -1.0).then_inc(zeroed1, 1)
            for b in range(B):
                pool.wait_ge(v1_out, NT)
                if b:
                    pool.wait_ge(pv1_done, NV1)
                pool.tensor_copy(vst[:, :, :, 0:D1 + 1], vall1[:, b, :, :, :]).then_inc(v1_staged, 1)
                for e, (qh, kt, pr) in enumerate(STEPS1):
                    if pr == 1:
                        pool.wait_ge(exp1_done, NE1 * b + e + 1)
                        at = qh * QC - kt * P + S - P
                        slot = probs[:, e // 2 % 2, 2:4, :]
                        pool.tensor_tensor(slot, slot, dist[:, at:at + QC].unsqueeze(1).broadcast_to([P, 2, QC]),
                                           ALU.mult).then_inc(scaled_pool, 1)
            def weigh_tile(t):
                for g in range(8):
                    pool.wait_ge(b_made, 8 * t + g + 1)
                    j = g % 2
                    pool.tensor_tensor(weigh[:, j], weigh[:, j], spread(uvw[:, t_par[0], 2, 8 * g:8 * g + 8], 64),
                                       ALU.mult).then_inc(b_weighted, 1)

            with pool.Fori(0, NT // 2) as m:
                for t_par[0] in range(2):
                    weigh_tile(2 * m + t_par[0])

        @block.scalar
        def _(act):
            def ln_root(k):
                act.wait_ge(ln_var, k)
                act.activation(stat[:, 3, :], stat[:, 2, :], ACT.Sqrt).then_inc(ln_sqrt, 1)

            act.wait_ge(dist_arg, 1)
            for i, (f, sc) in enumerate(((ACT.Abs, 1.0), (ACT.Exp, -1.0), (ACT.Exp, 1.0))):
                if i:
                    act.wait_ge(dist_done, i)
                act.activation(dist[:], dist[:], f, scale=sc).then_inc(dist_done, 1)
            for i in range(4):
                dst = (wqT, kT)[i // 2]
                act.wait_ge(fold_made, i + 1)
                act.activation(dst[:, 4 * (i % 2):4 * (i % 2) + 4, :].rearrange("p h c -> p (h c)"), ps[:, i, :],
                               ACT.Copy).then_inc(fold_out, 1)
            for i in range(2):
                act.wait_ge(fold_made, 5)
                act.activation(wf[:, i * QC:(i + 1) * QC], ps[:, 4 + i, :], ACT.Copy).then_inc(fold_out, 1)
                act.activation(bf[:, i * QC:(i + 1) * QC], ps[0:1, 6 + i, :], ACT.Copy).then_inc(fold_out, 1)
            ln_root(1)
            act.wait_ge(w_in, 16 * 8)
            act.wait_ge(fold_made, 5)
            for i, dst in enumerate((q_cm, k_cm)):
                for j in range(4):
                    act.wait_ge(proj, 4 * i + j + 1)
                    act.activation(dst[:, j * QC:(j + 1) * QC], ps[:, j, :], ACT.Relu,
                                   bias=cols[:, i:i + 1]).then_inc(proj_out, 1)
            for t in range(NT):
                b, kt = divmod(t, KT)
                act.wait_ge(v_done, t + 1)
                act.activation(vall[:, 4 * b:4 * b + 4, kt, :, 0:D0],
                               ps[:, 4 + t % 4, 0:C].rearrange("p (g h d) -> p g h d", g=4, h=HL),
                               ACT.Relu).then_inc(v_out, 1)

            def exps(n):
                for e, (qh, kt, pr) in enumerate(STEPS0):
                    act.wait_ge(scores_ready, 32 * n + e + 1)
                    v = e // 2
                    if not isinstance(n, int) or 16 * n + v >= 2:
                        act.wait_ge(pv_done, 16 * n + v - 1)
                    act.activation(probs[:, v % 2, 2 * pr:2 * pr + 2, :], score_ps[:, e % 2, :, :], ACT.Exp,
                                   scale=D0 ** -0.5).then_inc(exp_done, 1)

            act.wait_ge(split_done, 6)
            exps(0)
            with act.Fori(1, UNITS) as n:
                exps(n)
            act.wait_ge(bn_ready, 3)
            act.activation(bn[:, 2, :], bn[:, 1, :], ACT.Sqrt).then_inc(bn_root, 1)
            ln_root(2)
            ln_root(3)
            for r in range(8):
                act.wait_ge(wd_turned, r + 1)
                act.activation(wdt[:, 4 * r:4 * r + 4, :].rearrange("p v u -> p (v u)"), ps[:, 4 + r % 4, :],
                               ACT.Copy).then_inc(wd_out, 1)
            act.wait_ge(w1_in, 16 * 8)
            for i, dst in enumerate((q_cm, k_cm)):
                for j in range(4):
                    act.wait_ge(proj1, 4 * i + j + 1)
                    act.activation(dst[0:E1, j * QC:(j + 1) * QC], ps[0:E1, j, :], ACT.Identity,
                                   bias=cols1[:, i:i + 1]).then_inc(proj1_out, 1)
            act.wait_ge(zeroed1, 1)
            for t in range(NT):
                b, kt = divmod(t, KT)
                act.wait_ge(v1_done, t + 1)
                act.activation(vall1[:, b, kt, :, 0:D1],
                               ps[:, 4 + t % 4, 0:E1].rearrange("p (h d) -> p h d", h=H1), ACT.Copy).then_inc(v1_out, 1)
            act.wait_ge(split1_done, 6)
            for b in range(B):
                for e in range(NE1):
                    act.wait_ge(scores1_ready, NE1 * b + e + 1)
                    if e < len(STEPS1):
                        qh, kt, pr = STEPS1[e]
                        v = e // 2
                        dst, src = probs[:, v % 2, 2 * pr:2 * pr + 2, :], score_ps[:, e % 2, :, :]
                    else:
                        v = e - len(STEPS1) + 16
                        dst, src = probs[:, v % 2, 0, :], score_ps[:, e % 2, 0, :]
                    if NV1 * b + v >= 2:
                        act.wait_ge(pv1_done, NV1 * b + v - 1)
                    act.activation(dst, src, ACT.Exp, scale=E1 ** -0.5).then_inc(exp1_done, 1)
            for j in range(4):
                act.wait_ge(a_turned, j + 1)
                act.activation(aT[:, j * QC:(j + 1) * QC], ps[0:E1, j, :], ACT.Copy).then_inc(a_out, 1)
            ln_root(4)
            def stage_zt(t):
                if not isinstance(t, int) or t >= 1:
                    act.wait_ge(s_ready, t)
                act.activation(zt, xT[:, bass.ts(t, P)], ACT.Copy).then_inc(zt_staged, 1)

            def pick_exp(t):
                act.wait_ge(diff_done, t + 1)
                act.activation(ev, evd, ACT.Exp).then_inc(pexp_done, 1)

            def put_picks(t, x):
                act.wait_ge(trip_turned, t + 1)
                src = t_ps[:, 0:384].rearrange("p (w n) -> p w n", w=3)
                for y in range(2):
                    act.activation(uvw[HT * y:HT * y + HT, x, :, :], src[HT * y:HT * y + HT, :, HT * y:HT * y + HT],
                                   ACT.Copy).then_inc(uvw_ready, 1)

            def ge_tile(t, x, g0, g1):
                for g in range(g0, g1):
                    if g == 0 and not (isinstance(t, int) and t < 2):
                        act.wait_ge(gr_done, 8 * (t - 1))
                    act.wait_ge(g_made, 8 * t + g + 1)
                    act.activation(ge[:, x, :, :].rearrange("p v (y n) -> p y v n", y=2)[:, :, :, 8 * g:8 * g + 8],
                                   g_ps[:, g % 2, :].rearrange("p (c y v) -> p y v c", c=8, y=2),
                                   ACT.Copy).then_inc(ge_out, 1)

            act.wait_ge(turned_out, 12)
            stage_zt(0)
            stage_zt(1)
            pick_exp(0)
            put_picks(0, 0)

            def tile(t, x, ahead):
                if ahead == 2:
                    stage_zt(t + 2)
                ge_tile(t, x, 0, 4)
                if ahead:
                    pick_exp(t + 1)
                ge_tile(t, x, 4, 6)
                if ahead:
                    put_picks(t + 1, 1 - x)
                ge_tile(t, x, 6, 8)

            for x in range(2):
                tile(x, x, 2)
            with act.Fori(1, NT // 2 - 1) as m:
                for x in range(2):
                    tile(2 * m + x, x, 2)
            for x in range(2):
                tile(NT - 2 + x, x, 1 - x)

        @block.tensor
        def _(pe):
            pe.wait_ge(consts, 3)

            def turn_ln(k):
                pe.wait_ge(ln_done, k)
                for j in range(4):
                    for i in range(4):
                        last = pe.transpose(ps[:, j, i * P:(i + 1) * P], xn[:, 4 * j + i, :], ident[:])
                    last.then_inc(turned, 1)

            pe.wait_ge(fold_in, 16 * 4)
            for i in range(4):
                src = (wqr.rearrange("p (h c) -> p h c", h=NH), kbd)[i // 2]
                for j in range(4):
                    last = pe.transpose(ps[:, i, j * P:(j + 1) * P], src[:, 4 * (i % 2) + j, :], ident[:])
                last.then_inc(fold_made, 1)
            pe.wait_ge(fold_out, 4)
            for hh in range(NH):
                pe.matmul(ps[:, 4 + hh // 4, hh % 4 * P:hh % 4 * P + P], wqT[:, hh, :], kT[:, hh, :], start=True, stop=True)
                last = pe.matmul(ps[0:1, 6 + hh // 4, hh % 4 * P:hh % 4 * P + P], bqt[:, hh:hh + 1], kT[:, hh, :],
                                 start=True, stop=True)
            last.then_inc(fold_made, 1)
            turn_ln(1)
            pe.wait_ge(w_in, 16 * 8)
            pe.wait_ge(fold_out, 8)
            pe.wait_ge(turned_out, 4)
            for i in range(2):
                for j in range(4):
                    if i:
                        pe.wait_ge(proj_out, j + 1)
                    pe.matmul(ps[:, j, :], wts[:, i, :], xT[:, j * QC:(j + 1) * QC], start=True, stop=True)\
                        .then_inc(proj, 1)
            for t in range(NT):
                if t >= 4:
                    pe.wait_ge(v_out, t - 3)
                pe.matmul(ps[:, 4 + t % 4, 0:C], xT[:, t * P:(t + 1) * P], wts[:, 2, :], start=True, stop=False)
                pe.matmul(ps[:, 4 + t % 4, 0:C], ones[0:1, :], rows[0:1, 0, :], start=False, stop=True)\
                    .then_inc(v_done, 1)

            def max_task(n, i):
                par, x, qt, kh = MAX0[i]
                if not isinstance(n, int) or 64 * n + i >= 2:
                    pe.wait_ge(max_read, 64 * n + i - 1)
                pe.matmul(max_ps[:, i % 2, :], QS[:, par, n, x, qt * P:(qt + 1) * P],
                          KS[:, n, x, kh * QC:(kh + 1) * QC], start=True, stop=True).then_inc(max_scores, 1)

            def turn_max(n):
                pe.wait_ge(unit_max, n + 1)
                if not isinstance(n, int) or n >= 1:
                    pe.wait_ge(o_norm, 2 * n - 1)
                pe.transpose(o_ps[0:32, 0, 0:P], mx[:], ident[:]).then_inc(max_turned, 1)

            def pv(n, v, part):
                qh, kt = divmod(v, KT)
                if v == 0 and part == 0:
                    pe.wait_ge(v_staged, n + 1)
                    pe.wait_ge(shift_split, 4 * n + 4)
                if kt == 0 and part == 0 and (not isinstance(n, int) or 2 * n + qh >= 2):
                    pe.wait_ge(o_norm, 2 * n + qh - 1)
                if part == 0:
                    pe.wait_ge(exp_done, 32 * n + 2 * v + 2)
                at = part * QC // 2
                for hl in range(HL):
                    last = pe.matmul(o_ps[32 * hl:32 * hl + 32, qh, at:at + QC // 2], vst[:, kt, hl, :],
                                     probs[:, v % 2, hl, at:at + QC // 2], start=kt == 0 and part == 0,
                                     stop=kt == KT - 1 and part == 1)
                if part == 1:
                    last.then_inc(pv_done, 1)

            def turn_o(n, qh):
                pe.wait_ge(o_read, 2 * n + qh + 1)
                for i in range(4):
                    last = pe.transpose(o_ps[:, qh, i * P:(i + 1) * P], osb[:, i * P:(i + 1) * P], ident[:])
                last.then_inc(o_turned, 1)

            def unit(n, left):
                pe.wait_ge(shift_rows, 16 * 6 * (n + 1))
                for e, (qh, kt, pr) in enumerate(STEPS0):
                    if max_unit_at(n, 2 * e, left):
                        max_task(*max_unit_at(n, 2 * e, left))
                    if not isinstance(n, int) or 32 * n + e >= 2:
                        pe.wait_ge(exp_done, 32 * n + e - 1)
                    for x in range(2):
                        last = pe.matmul(score_ps[:, e % 2, x, :], KS[:, n, pr, kt * P:(kt + 1) * P],
                                         QS[:, x, n, pr, qh * QC:(qh + 1) * QC], start=True, stop=True)
                    last.then_inc(scores_ready, 1)
                    if max_unit_at(n, 2 * e + 1, left):
                        max_task(*max_unit_at(n, 2 * e + 1, left))
                    if e >= 2:
                        pv(n, e // 2 - 1, e % 2)
                    if e == 19:
                        turn_o(n, 0)
                    if left and e == MAXED + 2:
                        turn_max(n + 1)
                pv(n, 15, 0)
                pv(n, 15, 1)
                turn_o(n, 1)

            pe.wait_ge(v_out, NT)
            pe.wait_ge(stack_in, 16 * 48)
            for i in range(len(MAX0)):
                max_task(0, i)
            turn_max(0)
            for i in range(LEAD0):
                max_task(1, i)
            unit(0, UNITS - 1)
            with pe.Fori(1, UNITS - 2) as n:
                unit(n, 2)
            unit(UNITS - 2, 1)
            unit(UNITS - 1, 0)

            pe.wait_ge(bn_ready, 1)
            for t in range(NT):
                last = pe.matmul(ps[:, 0, 0:C], ones[:], xn[:, t, :], start=t == 0, stop=t == NT - 1)
            last.then_inc(bn_made, 1)
            pe.wait_ge(bn_ready, 2)
            for t in range(NT):
                pe.matmul(ps[:, 1, 0:C], ones[:], tmp[:, t, :], start=t == 0, stop=t == NT - 1)
            for i in range(2):
                last = pe.matmul(ps[:, 2 + i, 0:C], ones[0:1, :], rows[0:1, 1 + i, :], start=True, stop=True)
            last.then_inc(bn_made, 1)
            pe.wait_ge(wd_in, 16)
            for r in range(8):
                if r >= 4:
                    pe.wait_ge(wd_out, r - 3)
                for i in range(4):
                    last = pe.transpose(ps[:, 4 + r % 4, i * P:(i + 1) * P], wdr[:, 4 * r + i, :], ident[:])
                last.then_inc(wd_turned, 1)
            turn_ln(3)
            pe.wait_ge(w1_in, 16 * 8)
            pe.wait_ge(turned_out, 8)
            for i in range(2):
                for j in range(4):
                    if i:
                        pe.wait_ge(proj1_out, j + 1)
                    pe.matmul(ps[0:E1, j, :], w1[:, i, :], xT[:, j * QC:(j + 1) * QC], start=True, stop=True)\
                        .then_inc(proj1, 1)
            pe.wait_ge(wd_out, 8)
            for t in range(NT):
                if t >= 4:
                    pe.wait_ge(v1_out, t - 3)
                pe.matmul(ps[:, 4 + t % 4, 0:E1], xT[:, t * P:(t + 1) * P], w1[:, 2, :], start=True, stop=False)
                pe.matmul(ps[:, 4 + t % 4, 0:E1], ones[0:1, :], rows1[0:1, 0, 0:E1], start=False, stop=True)\
                    .then_inc(v1_done, 1)

            def max1_task(b, i):
                kind, hl, qt, kh = MAX1[i]
                k = len(MAX1) * b + i
                if i == 0 and b:
                    pe.wait_ge(shift1_split, 4 * b)
                if k >= 2:
                    pe.wait_ge(max1_read, k - 1)
                k0, n = (kh * QC, QC) if kind == "full" else (window_of(qt)[0], 192)
                pe.matmul(max_ps[:, i % 2, 0:n], QS1[:, b, hl, qt * P:(qt + 1) * P], KS1[:, b, hl, k0:k0 + n],
                          start=True, stop=True).then_inc(max1_scores, 1)

            def turn_max1(b):
                pe.wait_ge(unit1_max, b + 1)
                pe.transpose(max_ps[0:64, 0, 0:P], mx1[:], ident[:]).then_inc(max1_turned, 1)

            def pv1(b, v):
                if v == 0:
                    pe.wait_ge(v1_staged, b + 1)
                if v < 16:
                    qh, kt = divmod(v, KT)
                    if kt == 0 and 4 * b + qh >= 2:
                        pe.wait_ge(o1_norm, 4 * b + qh - 1)
                    pe.wait_ge(scaled_dve, NV1 * b + v + 1)
                    pe.wait_ge(scaled_pool, 16 * b + v + 1)
                    for hl in range(HL):
                        last = pe.matmul(o_ps[32 * hl:32 * hl + 32, qh, :], vst[:, kt, hl, :], probs[:, v % 2, hl, :],
                                         start=kt == 0, stop=kt == KT - 1)
                else:
                    i, kt = WSTEPS[v - 16]
                    if i % 4 == 0 and kt == max(i - 1, 0):
                        pe.wait_ge(o1_norm, 4 * b + 2 + i // 4 - 1)
                    pe.wait_ge(scaled_dve, NV1 * b + v + 1)
                    for hl in range(HL):
                        last = pe.matmul(o_ps[32 * hl:32 * hl + 32, i // 4, i % 4 * P:i % 4 * P + P], vst[:, kt, hl, :],
                                         probs[:, v % 2, 0, hl * P:(hl + 1) * P],
                                         start=kt == max(i - 1, 0), stop=kt == min(i + 1, KT - 1))
                last.then_inc(pv1_done, 1)

            def turn_o1(w):
                pe.wait_ge(o1_read, w + 1)
                for i in range(4):
                    last = pe.transpose(o_ps[:, w % 2, i * P:(i + 1) * P], osb[:, i * P:(i + 1) * P], ident[:])
                last.then_inc(o1_turned, 1)

            def sequence(b, more):
                pe.wait_ge(shift1_rows, 16 * 6 * (b + 1))
                todo = 0
                for e in range(NE1):
                    if NE1 * b + e >= 2:
                        pe.wait_ge(exp1_done, NE1 * b + e - 1)
                    if e < len(STEPS1):
                        qh, kt, pr = STEPS1[e]
                        for x in range(2):
                            last = pe.matmul(score_ps[:, e % 2, x, :], KS1[:, b, 2 * pr + x, kt * P:(kt + 1) * P],
                                             QS1[:, b, 2 * pr + x, qh * QC:(qh + 1) * QC], start=True, stop=True)
                    else:
                        i, kt = WSTEPS[e - len(STEPS1)]
                        for hl in range(HL):
                            last = pe.matmul(score_ps[:, e % 2, 0, hl * P:(hl + 1) * P],
                                             KS1[:, b, hl, kt * P:(kt + 1) * P],
                                             QW1[:, b, hl, i * P:(i + 1) * P], start=True, stop=True)
                    last.then_inc(scores1_ready, 1)
                    if more:
                        while todo < min(len(MAX1), 2 * e + 2):
                            max1_task(b + 1, todo)
                            todo += 1
                    if e < len(STEPS1):
                        if e % 2 and e >= 3:
                            pv1(b, e // 2 - 1)
                    else:
                        pv1(b, e - len(STEPS1) + 15)
                    if e == 22:
                        turn_o1(4 * b)
                    if e == 36:
                        turn_o1(4 * b + 1)
                    if e == 48:
                        turn_o1(4 * b + 2)
                pv1(b, NV1 - 1)
                turn_o1(4 * b + 3)
                if more:
                    turn_max1(b + 1)

            pe.wait_ge(v1_out, NT)
            pe.wait_ge(stack1_in, 16 * 36)
            for i in range(len(MAX1)):
                max1_task(0, i)
            turn_max1(0)
            sequence(0, True)
            sequence(1, False)
            pe.wait_ge(attn1_done, 2 * B)
            for j in range(4):
                for i in range(4):
                    last = pe.transpose(ps[0:E1, j, i * P:(i + 1) * P], attn1[:, 4 * j + i, :], ident[:])
                last.then_inc(a_turned, 1)
            for j in range(4):
                pe.wait_ge(a_out, j + 1)
                for i in range(4):
                    t = 4 * j + i
                    o = ps[:, 4 + j, i * P:(i + 1) * P]
                    pe.matmul(o, aT[:, t * P:(t + 1) * P], wout[:], start=True, stop=False)
                    last = pe.matmul(o, ones[0:1, :], rows1[0:1, 1, :], start=False, stop=True)
                last.then_inc(wo_made, 1)
            turn_ln(4)

            def key_scores(t, parts=(0, 1)):
                if 0 in parts:
                    pe.wait_ge(zt_staged, t + 1)
                    if not isinstance(t, int) or t >= 1:
                        pe.wait_ge(s_picked, t)
                for i in parts:
                    pe.matmul(ps[:, i, :], zt, wf[:, i * QC:(i + 1) * QC], start=True, stop=False)
                    last = pe.matmul(ps[:, i, :], ones3[:], bf3[:, i * QC:(i + 1) * QC], start=False, stop=True)
                if 1 in parts:
                    last.then_inc(s_ready, 1)

            def turn_trip(t):
                pe.wait_ge(trip_done, t + 1)
                if not isinstance(t, int) or t >= 1:
                    pe.wait_ge(uvw_ready, 2 * t)
                for w in range(3):
                    last = pe.transpose(t_ps[:, w * P:(w + 1) * P], trip[:, w].rearrange("p d n -> p (d n)"), ident[:])
                last.then_inc(trip_turned, 1)

            def gates(t, g):
                pe.wait_ge(a_made, 8 * t + g + 1)
                pe.wait_ge(b_weighted, 8 * t + g + 1)
                if not (isinstance(t, int) and 8 * t + g < 2):
                    pe.wait_ge(ge_out, 8 * t + g - 1)
                for c in range(8):
                    last = pe.matmul(g_ps[:, g % 2, c * 64:(c + 1) * 64], onehot[:, g % 2, c, :], weigh[:, g % 2, c, :],
                                     start=True, stop=True)
                last.then_inc(g_made, 1)

            def inner(t, q):
                if not (isinstance(t, int) and 8 * t + q < 2):
                    pe.wait_ge(gr_done, 8 * t + q - 1)
                for i in range(4):
                    last = pe.matmul(in_ps[:, q % 2, i * P:(i + 1) * P], wdt[:, 4 * q + i, :], xT[:, bass.ts(t, P)],
                                     start=True, stop=True)
                last.then_inc(inner_ready, 1)

            def gather_out(t, q):
                pe.wait_ge(gr_done, 8 * t + q + 1)
                if q == 0 and not (isinstance(t, int) and t == 0):
                    pe.wait_ge(h_out, t)
                for i in range(4):
                    last = pe.matmul(acc_ps, gated[:, q % 2, i, :], wup[:, 4 * q + i, :],
                                     start=q == 0 and i == 0, stop=q == 7 and i == 3)
                last.then_inc(acc_used, 1)

            def tile(t, back, ahead):
                for g in range(8):
                    if ahead == 2 and g in (3, 4):
                        key_scores(t + 2, (g - 3,))
                    if back:
                        inner(t - 1, g)
                        if g:
                            gather_out(t - 1, g - 1)
                    gates(t, g)
                    if ahead and g == 6:
                        turn_trip(t + 1)
                if back:
                    gather_out(t - 1, 7)

            pe.wait_ge(turned_out, 12)
            pe.wait_ge(wu_in, 16)
            pe.wait_ge(bf_in, 16)
            key_scores(0)
            key_scores(1)
            turn_trip(0)
            tile(0, False, 2)
            tile(1, True, 2)
            with pe.Fori(1, NT // 2 - 1) as m:
                for x in range(2):
                    tile(2 * m + x, True, 2)
            tile(NT - 2, True, 1)
            tile(NT - 1, True, 0)
            for q in range(8):
                inner(NT - 1, q)
                if q:
                    gather_out(NT - 1, q - 1)
            gather_out(NT - 1, 7)

        @block.vector
        def _(dve):
            order = Tally(dve, sem("dve_order"))
            dve.memset(big[:, 0:32768].bitcast(F32), 0.0).then_inc(zeroed, 1)
            dve.memset(big[:, 32768:49152], -1.0).then_inc(zeroed, 1)

            dve.memset(kbd, 0.0).then_inc(fold_ready, 1)
            dve.wait_ge(sem("gt_in"), 32)
            dve.wait_ge(dist_num, 1)
            order.then_wait(dve.tensor_copy(xT[:, 0:TW], dist[:].bitcast(I32)))
            order.then_wait(dve.tensor_tensor(xT[:, 0:TW], xT[:, 0:TW], xT[:, 0:TW], ALU.mult))
            dve.tensor_scalar(dist[:], xT[:, 0:TW], gt[:, 0:1], gt[:, 1:2], ALU.mult, ALU.subtract).then_inc(dist_arg, 1)

            def newton(r, x):
                s = stat[:, 5, :] if r is not bn_r else bn[:, 4, :]
                order.then_wait(dve.tensor_tensor(s, r, r, ALU.mult))
                order.then_wait(dve.tensor_tensor(s, s, x, ALU.mult))
                order.then_wait(dve.tensor_scalar(s, s, -0.5, 1.5, ALU.mult, ALU.add))
                order.then_wait(dve.tensor_tensor(r, r, s, ALU.mult))

            def layer_norm(k):
                order.then_wait(dve.tensor_reduce(stat[:, 0, :], h[:], X, ALU.add))
                order.then_wait(dve.tensor_scalar(stat[:, 1, :], stat[:, 0, :], 1.0 / C, None, ALU.mult))
                order.then_wait(dve.tensor_tensor(xn[:], h[:], spread(stat[:, 1, :], C), ALU.subtract))
                order.then_wait(dve.tensor_tensor(tmp[:], xn[:], xn[:], ALU.mult))
                order.then_wait(dve.tensor_reduce(stat[:, 0, :], tmp[:], X, ALU.add))
                dve.tensor_scalar(stat[:, 2, :], stat[:, 0, :], 1.0 / C, LN_EPS, ALU.mult, ALU.add).then_inc(ln_var, 1)
                dve.wait_ge(ln_sqrt, k)
                order.then_wait(dve.reciprocal(stat[:, 4, :], stat[:, 3, :]))
                newton(stat[:, 4, :], stat[:, 2, :])
                dve.tensor_tensor(xn[:], xn[:], spread(stat[:, 4, :], C), ALU.mult).then_inc(ln_done, 1)

            def take_turned(k):
                for j in range(4):
                    dve.wait_ge(turned, 4 * (k - 1) + j + 1)
                    dve.tensor_copy(xT[:, j * QC:(j + 1) * QC], ps[:, j, :]).then_inc(turned_out, 1)

            def split3(src, rows_, done, sent):
                scr = tmp[0:rows_].rearrange("p t c -> p (t c)")
                if sent:
                    dve.wait_ge(*sent)
                dve.tensor_copy(splits[0:rows_, 0, :], src).then_inc(done, 1)
                n = 3 if sent else 0
                dve.wait_ge(done, n + 1)
                order.then_wait(dve.tensor_tensor(scr, src, splits[0:rows_, 0, :], ALU.subtract))
                dve.tensor_copy(splits[0:rows_, 1, :], scr).then_inc(done, 1)
                dve.wait_ge(done, n + 2)
                dve.tensor_tensor(splits[0:rows_, 2, :], scr, splits[0:rows_, 1, :], ALU.subtract).then_inc(done, 1)
                dve.wait_ge(done, n + 3)

            dve.wait_ge(gathered, 16 * NT)
            layer_norm(1)
            dve.wait_ge(fold_out, 8)
            rowr = tmp[0:1].rearrange("p t c -> p (t c)")[:, 0:NH * P]
            order.then_wait(dve.tensor_copy(bfs[:, 0, :], bf[:]))
            order.then_wait(dve.tensor_tensor(rowr, bf[:], bfs[:, 0, :], ALU.subtract))
            order.then_wait(dve.tensor_copy(bfs[:, 1, :], rowr))
            dve.tensor_tensor(bfs[:, 2, :], rowr, bfs[:, 1, :], ALU.subtract).then_inc(bf_split, 1)
            dve.wait_ge(bf_split, 1)
            take_turned(1)
            dve.wait_ge(proj_out, 4)
            dve.wait_ge(bf_in, 16)
            split3(q_cm, C, split_done, None)
            dve.wait_ge(proj_out, 8)
            split3(k_cm, C, split_done, (split_out, 16))

            def max_read_task(n, i):
                par, x, qt, kh = i // 32, i // 16 % 2, i // 2 % 8, i % 2
                if i == 0 and not (isinstance(n, int) and n == 0):
                    dve.wait_ge(unit_max, n)
                dve.wait_ge(max_scores, 64 * n + i + 1)
                dve.tensor_reduce(mhalf[:, i // 2, kh:kh + 1], max_ps[:, i % 2, :], X, ALU.max).then_inc(max_read, 1)

            def max_of(n):
                dve.wait_ge(max_read, 64 * n + 64)
                if not isinstance(n, int) or n >= 1:
                    dve.wait_ge(max_turned, n)
                dve.tensor_reduce(mx[:], mhalf[:], X, ALU.max).then_inc(unit_max, 1)

            def shift_of(n):
                dve.wait_ge(max_turned, n + 1)
                if not isinstance(n, int) or n >= 1:
                    dve.wait_ge(shift_rows, 16 * 6 * n)
                src = o_ps[0:32, 0, 0:P]
                dve.tensor_copy(sh[:, 0, :], src).then_inc(shift_split, 1)
                dve.wait_ge(shift_split, 4 * n + 1)
                dve.tensor_tensor(shf[:], src, sh[:, 0, :], ALU.subtract).then_inc(shift_split, 1)
                dve.wait_ge(shift_split, 4 * n + 2)
                dve.tensor_copy(sh[:, 1, :], shf[:]).then_inc(shift_split, 1)
                dve.wait_ge(shift_split, 4 * n + 3)
                dve.tensor_tensor(sh[:, 2, :], shf[:], sh[:, 1, :], ALU.subtract).then_inc(shift_split, 1)

            def read_o(n, qh):
                dve.wait_ge(pv_done, 16 * n + 8 * qh + 8)
                if not isinstance(n, int) or 2 * n + qh >= 1:
                    dve.wait_ge(o_turned, 2 * n + qh)
                dve.tensor_copy(osb[:], o_ps[:, qh, :]).then_inc(o_read, 1)

            def norm_o(n, qh):
                dve.wait_ge(o_turned, 2 * n + qh + 1)
                if not isinstance(n, int) or 2 * n + qh >= 1:
                    dve.wait_ge(o_norm, 2 * n + qh)
                o = o_ps[:, qh, :].rearrange("p (t h m) -> p t h m", t=4, h=HL)
                dve.reciprocal(rden[:], o[:, :, :, D0]).then_inc(sem("rden_done"), 1)
                dve.wait_ge(sem("rden_done"), 2 * n + qh + 1)
                dst = attn[:, n, 4 * qh:4 * qh + 4, :].rearrange("p t (h d) -> p t h d", h=HL)
                dve.tensor_tensor(dst, o[:, :, :, 0:D0],
                                  rden[:].unsqueeze(3).broadcast_to([P, 4, HL, D0]), ALU.mult).then_inc(o_norm, 1)

            def unit(n, left):
                for e in range(len(STEPS0)):
                    for k in (2 * e, 2 * e + 1):
                        if max_unit_at(n, k, left):
                            max_read_task(*max_unit_at(n, k, left))
                    if e == 18:
                        read_o(n, 0)
                    if e == 20:
                        norm_o(n, 0)
                    if left and e == MAXED:
                        max_of(n + 1)
                    if left and e == MAXED + 2:
                        shift_of(n + 1)
                read_o(n, 1)
                norm_o(n, 1)

            for i in range(len(MAX0)):
                max_read_task(0, i)
            max_of(0)
            shift_of(0)
            for i in range(LEAD0):
                max_read_task(1, i)
            unit(0, UNITS - 1)
            with dve.Fori(1, UNITS - 2) as n:
                unit(n, 2)
            unit(UNITS - 2, 1)
            unit(UNITS - 1, 0)

            dve.wait_ge(o_norm, 2 * UNITS)
            for b in range(B):
                xb = xn[:, b * KT:(b + 1) * KT, :].rearrange("p t (g c) -> p g t c", g=4)
                last = dve.tensor_tensor(xb, xb, attn[:, 4 * b:4 * b + 4, :, :], ALU.add)
                if b == 0:
                    order.then_wait(last)
            last.then_inc(bn_ready, 1)
            dve.wait_ge(bn_ready, 1)

            def along_tokens(row):
                return row.unsqueeze(1).broadcast_to([P, NT, C])

            dve.wait_ge(bn_made, 1)
            order.then_wait(dve.tensor_scalar(bn[:, 0, :], ps[:, 0, 0:C], 1.0 / NTOK, None, ALU.mult))
            order.then_wait(dve.tensor_tensor(xn[:], xn[:], along_tokens(bn[:, 0, :]), ALU.subtract))
            dve.tensor_tensor(tmp[:], xn[:], xn[:], ALU.mult).then_inc(bn_ready, 1)
            dve.wait_ge(bn_made, 2)
            dve.tensor_scalar(bn[:, 1, :], ps[:, 1, 0:C], 1.0 / NTOK, BN_EPS, ALU.mult, ALU.add).then_inc(bn_ready, 1)
            dve.wait_ge(bn_root, 1)
            order.then_wait(dve.reciprocal(bn_r, bn[:, 2, :]))
            newton(bn_r, bn[:, 1, :])
            order.then_wait(dve.tensor_tensor(bn_r, bn_r, ps[:, 2, 0:C], ALU.mult))
            order.then_wait(dve.tensor_tensor(xn[:], xn[:], along_tokens(bn_r), ALU.mult))
            order.then_wait(dve.tensor_tensor(xn[:], xn[:], along_tokens(ps[:, 3, 0:C]), ALU.add))
            order.then_wait(dve.tensor_tensor(h[:], h[:], xn[:], ALU.add))
            layer_norm(2)
            dve.wait_ge(ln_done, 2)
            order.then_wait(dve.tensor_tensor(h[:], h[:], xn[:], ALU.add))
            layer_norm(3)
            take_turned(2)
            dve.wait_ge(proj1_out, 4)
            split3(q_cm[0:E1, :], E1, split1_done, None)
            dve.wait_ge(proj1_out, 8)
            split3(k_cm[0:E1, :], E1, split1_done, (split1_out, 16))

            def max1_read_task(b, i):
                kind, hl, qt, kh = MAX1[i]
                k = len(MAX1) * b + i
                dve.wait_ge(max1_scores, k + 1)
                if kind == "full":
                    dve.tensor_reduce(mhalf[:, i // 2, kh:kh + 1], max_ps[:, i % 2, :], X, ALU.max).then_inc(max1_read, 1)
                else:
                    at = window_of(qt)[1]
                    if k >= 2:
                        dve.wait_ge(max1_read, k - 1)
                    dve.tensor_tensor_reduce(wscr[:, i % 2, :], max_ps[:, i % 2, 0:192], wmask[:, at:at + 192], 1.0, -3e38,
                                             ALU.add, ALU.max, mx1[:, 32 + 8 * hl + qt:33 + 8 * hl + qt]).then_inc(max1_read, 1)

            def shift1_of(b):
                dve.wait_ge(max1_read, len(MAX1) * (b + 1))
                if b:
                    dve.wait_ge(max1_turned, b)
                dve.tensor_reduce(mx1[:, 0:32], mhalf[:], X, ALU.max).then_inc(unit1_max, 1)
                dve.wait_ge(max1_turned, b + 1)
                if b:
                    dve.wait_ge(shift1_rows, 16 * 6 * b)
                src = max_ps[0:64, 0, 0:P]
                dve.tensor_copy(sh1[:, 0, :], src).then_inc(shift1_split, 1)
                dve.wait_ge(shift1_split, 4 * b + 1)
                dve.tensor_tensor(shf1[:], src, sh1[:, 0, :], ALU.subtract).then_inc(shift1_split, 1)
                dve.wait_ge(shift1_split, 4 * b + 2)
                dve.tensor_copy(sh1[:, 1, :], shf1[:]).then_inc(shift1_split, 1)
                dve.wait_ge(shift1_split, 4 * b + 3)
                dve.tensor_tensor(sh1[:, 2, :], shf1[:], sh1[:, 1, :], ALU.subtract).then_inc(shift1_split, 1)

            def scale1(b, e):
                dve.wait_ge(exp1_done, NE1 * b + e + 1)
                if e < len(STEPS1):
                    qh, kt, pr = STEPS1[e]
                    at = qh * QC - kt * P + S - P
                    slot = probs[:, e // 2 % 2, 0:2, :]
                    by = dist[:, at:at + QC].unsqueeze(1).broadcast_to([P, 2, QC])
                else:
                    i, kt = WSTEPS[e - len(STEPS1)]
                    v = e - len(STEPS1) + 16
                    slot = probs[:, v % 2, 0, :].rearrange("p (h n) -> p h n", h=HL)
                    by = near[:, kt - i + 1, :].unsqueeze(1).broadcast_to([P, HL, P])
                dve.tensor_tensor(slot, slot, by, ALU.mult).then_inc(scaled_dve, 1)

            def read_o1(w):
                b, k = divmod(w, 4)
                dve.wait_ge(pv1_done, NV1 * b + (8, 16, 16 + 11, NV1)[k])
                if w:
                    dve.wait_ge(o1_turned, w)
                dve.tensor_copy(osb[:], o_ps[:, w % 2, :]).then_inc(o1_read, 1)

            def norm_o1(w):
                b, k = divmod(w, 4)
                dve.wait_ge(o1_turned, w + 1)
                o = o_ps[:, w % 2, :].rearrange("p (t h m) -> p t h m", t=4, h=HL)
                order.then_wait(dve.reciprocal(rden[:], o[:, :, :, D1]))
                at = KT * b + 4 * (k % 2)
                dst = attn1[:, at:at + 4, :].rearrange("p t (h d) -> p t h d", h=H1)
                r4 = rden[:].unsqueeze(3).broadcast_to([P, 4, H1, D1])
                if k < 2:
                    dve.scalar_tensor_tensor(out=dst, in0=o[:, :, :, 0:D1], scalar=0.5, in1=r4, op0=ALU.mult,
                                             op1=ALU.mult).then_inc(o1_norm, 1)
                    dve.wait_ge(o1_norm, w + 1)
                else:
                    o2 = xT[:, 0:4 * E1].rearrange("p (t h d) -> p t h d", t=4, h=H1)
                    dve.scalar_tensor_tensor(out=o2, in0=o[:, :, :, 0:D1], scalar=0.5, in1=r4, op0=ALU.mult,
                                             op1=ALU.mult).then_inc(o1_norm, 1)
                    dve.wait_ge(o1_norm, w + 1)
                    dve.tensor_tensor(dst, dst, o2, ALU.add).then_inc(attn1_done, 1)
                    dve.wait_ge(attn1_done, 2 * b + k - 1)

            def sequence(b, more):
                todo = 0
                for e in range(NE1):
                    if more:
                        while todo < min(len(MAX1), 2 * e + 2):
                            max1_read_task(b + 1, todo)
                            todo += 1
                    if e >= len(STEPS1) or STEPS1[e][2] == 0:
                        scale1(b, e)
                    if e == 20:
                        read_o1(4 * b)
                    if e == 26:
                        norm_o1(4 * b)
                    if e == 34:
                        read_o1(4 * b + 1)
                    if e == 37:
                        norm_o1(4 * b + 1)
                    if e == 46:
                        read_o1(4 * b + 2)
                    if e == 49:
                        norm_o1(4 * b + 2)
                read_o1(4 * b + 3)
                norm_o1(4 * b + 3)
                if more:
                    shift1_of(b + 1)

            for i in range(len(MAX1)):
                max1_read_task(0, i)
            shift1_of(0)
            sequence(0, True)
            sequence(1, False)
            for j in range(4):
                dve.wait_ge(wo_made, j + 1)
                hj = h[:, 4 * j:4 * j + 4, :]
                order.then_wait(dve.tensor_tensor(hj, hj, ps[:, 4 + j, :].rearrange("p (t c) -> p t c", t=4), ALU.add))
            layer_norm(4)
            take_turned(3)

            PICKS = 13

            def picked(t, n):
                dve.wait_ge(pick_order, PICKS * t + n)

            def key_max(t, g):
                for hh in range(4 * g, 4 * g + 4):
                    for q in range(2):
                        last = dve.max(top[:, hh, q, :], s_ps[:, hh, q, :])
                last.then_inc(pick_order, 1)

            def key_places(t, g):
                for hh in range(4 * g, 4 * g + 4):
                    for q in range(2):
                        last = dve.max_index(top_at[:, hh, q, :], top[:, hh, q, :], s_ps[:, hh, q, :])
                if g == 1:
                    last.then_inc(s_picked, 1)

            def pair_sums(t):
                dve.tensor_tensor(sums, top[:, :, 0, :].unsqueeze(3).broadcast_to([P, NH, TK, TK]),
                                  top[:, :, 1, :].unsqueeze(2).broadcast_to([P, NH, TK, TK]), ALU.add).then_inc(pick_order, 1)

            def pair_max(t):
                for hh in range(NH):
                    last = dve.max(best[:, hh, :], sums[:, hh].rearrange("p i j -> p (i j)"))
                last.then_inc(pick_order, 1)

            def pair_places(t):
                picked(t, 4)
                dve.tensor_tensor(evd, best, best[:, :, 0:1].broadcast_to([P, NH, TK]), ALU.subtract).then_inc(diff_done, 1)
                for hh in range(NH):
                    last = dve.max_index(best_at[:, hh, :], best[:, hh, :], sums[:, hh].rearrange("p i j -> p (i j)"))
                last.then_inc(pick_order, 1)

            def pair_sides(t):
                picked(t, 5)
                dve.tensor_scalar(side[0], best_at, 3, None, ALU.logical_shift_right)
                dve.tensor_scalar(side[1], best_at, 7, None, ALU.bitwise_and).then_inc(pick_order, 1)

            def match_places(t):
                picked(t, 6)
                eight = iota_f[:, 0:TK].unsqueeze(1).unsqueeze(1).broadcast_to([P, NH, TK, TK])
                for q in range(2):
                    last = dve.tensor_tensor(match[q], side[q].unsqueeze(3).broadcast_to([P, NH, TK, TK]), eight, ALU.is_equal)
                last.then_inc(pick_order, 1)

            def match_keys(t):
                picked(t, 7)
                dve.wait_ge(s_picked, t + 1)
                for q in range(2):
                    last = dve.tensor_tensor(match[q], match[q],
                                             top_at[:, :, q, :].unsqueeze(2).broadcast_to([P, NH, TK, TK]), ALU.mult)
                last.then_inc(pick_order, 1)

            def sum_keys(t):
                picked(t, 8)
                for q in range(2):
                    last = dve.tensor_reduce(key_at[q].rearrange("p (h k) -> p h k", h=NH), match[q], X, ALU.add)
                last.then_inc(pick_order, 1)

            def key_high(t):
                picked(t, 9)
                dve.tensor_scalar(upper, key_at[1], float(VL), None, ALU.is_ge).then_inc(pick_order, 1)
                dve.wait_ge(pexp_done, t + 1)
                dve.tensor_reduce(esum, ev, X, ALU.add).then_inc(pick_order, 1)

            def split_number(t):
                picked(t, 11)
                if not isinstance(t, int) or t >= 1:
                    dve.wait_ge(trip_turned, t)
                for d in range(2):
                    last = dve.scalar_tensor_tensor(out=trip[:, 0, d, :], in0=key_at[0], scalar=2.0, in1=upper,
                                                    op0=ALU.mult, op1=ALU.add)
                dve.scalar_tensor_tensor(out=trip[:, 1, 0, :], in0=upper, scalar=-float(VL), in1=key_at[1], op0=ALU.mult,
                                         op1=ALU.add).then_inc(pick_order, 1)
                dve.reciprocal(rsum, esum).then_inc(pick_order, 1)

            def weights(t):
                picked(t, 13)
                dve.tensor_scalar(trip[:, 1, 1, :], trip[:, 1, 0, :], float(VL), None, ALU.add)
                for d in range(2):
                    last = dve.tensor_tensor(trip[:, 2, d, :].rearrange("p (h k) -> p h k", h=NH), ev, spread(rsum, TK), ALU.mult)
                last.then_inc(trip_done, 1)

            def onehot_v(t, x, g):
                if g == 0:
                    dve.wait_ge(uvw_ready, 2 * t + 2)
                if not (isinstance(t, int) and 8 * t + g < 2):
                    dve.wait_ge(g_made, 8 * t + g - 1)
                dve.tensor_tensor(weigh[:, g % 2], iota_f[:, 0:64].unsqueeze(1).broadcast_to([P, 8, 64]),
                                  spread(uvw[:, x, 1, 8 * g:8 * g + 8], 64), ALU.is_equal).then_inc(b_made, 1)

            def onehot_u(t, x, g):
                dve.tensor_tensor(onehot[:, g % 2], iota_f[:].unsqueeze(1).broadcast_to([P, 8, P]),
                                  spread(uvw[:, x, 0, 8 * g:8 * g + 8], P), ALU.is_equal).then_inc(a_made, 1)

            def gate_inner(t, x, q):
                dve.wait_ge(inner_ready, 8 * t + q + 1)
                if q == 0:
                    dve.wait_ge(ge_out, 8 * t + 8)
                if not (isinstance(t, int) and 8 * t + q < 2):
                    dve.wait_ge(acc_used, 8 * t + q - 1)
                dve.scalar_tensor_tensor(out=gated[:, q % 2], in0=in_ps[:, q % 2, :].rearrange("p (i n) -> p i n", i=4),
                                         scalar=0.0, in1=ge[:, x, 4 * q:4 * q + 4, :], op0=ALU.max, op1=ALU.mult)\
                    .then_inc(gr_done, 1)

            def add_out(t):
                dve.wait_ge(acc_used, 8 * t + 8)
                ht = h[:, bass.ts(t, 1), :].rearrange("p o c -> p (o c)")
                dve.tensor_tensor(ht, ht, acc_ps, ALU.add).then_inc(h_out, 1)

            def tile(t, x, back, more):
                for g in range(8):
                    n = t + 1
                    if more and g == 0:
                        dve.wait_ge(s_ready, t + 2)
                    onehot_v(t, x, g)
                    if more and g < 2:
                        key_max(n, g)
                        picked(n, g + 1)
                    if more and g == 2:
                        pair_sums(n)
                        picked(n, 3)
                    if more and g == 3:
                        pair_places(n)
                    if more and g == 4:
                        match_places(n)
                    if more and g == 5:
                        sum_keys(n)
                    onehot_u(t, x, g)
                    if more and g < 2:
                        key_places(n, g)
                    if more and g == 2:
                        pair_max(n)
                    if more and g == 3:
                        pair_sides(n)
                    if more and g == 4:
                        match_keys(n)
                    if more and g == 5:
                        key_high(n)
                        split_number(n)
                    if back == 2 and g == 0:
                        add_out(t - 2)
                    if back:
                        gate_inner(t - 1, 1 - x, g)
                    if more and g == 5:
                        weights(n)

            dve.wait_ge(s_ready, 1)
            for g in range(2):
                key_max(0, g)
                picked(0, g + 1)
                key_places(0, g)
            pair_sums(0)
            picked(0, 3)
            for step in (pair_max, pair_places, pair_sides, match_places, match_keys, sum_keys, key_high, split_number, weights):
                step(0)
            tile(0, 0, 0, True)
            tile(1, 1, 1, True)
            with dve.Fori(1, NT // 2 - 1) as m:
                for x in range(2):
                    tile(2 * m + x, x, 2, True)
            tile(NT - 2, 0, 2, True)
            tile(NT - 1, 1, 2, False)
            add_out(NT - 2)
            for q in range(8):
                gate_inner(NT - 1, 1, q)
            add_out(NT - 1)


def kernel(**inputs):
    import numpy as np
    import concourse.bacc as bacc
    from concourse.bass_utils import run_bass_kernel_spmd

    nc = bacc.Bacc("TRN2", target_bir_lowering=False, num_devices=1)
    arrays, aps = {}, {}

    def put(name, arr):
        arr = np.ascontiguousarray(arr)
        arrays[name + "_in"] = arr
        aps[name] = nc.dram_tensor(name + "_in", arr.shape, mybir.dt.from_np(arr.dtype), kind="ExternalInput").ap()

    put("tok", np.asarray(inputs["x"]).reshape(NT, P).T)
    put("emb", np.asarray(inputs["L0_tok_W"]).T)
    put("bqt", np.asarray(inputs["L1_ffn_bq"]).reshape(NH, P).T)
    for name in _WEIGHTS:
        put(name, np.asarray(inputs[name]))
    for name in ("L1_attn_gamma", "L1_attn_theta"):
        put(name, np.asarray(inputs[name]).reshape(1))
    out = nc.dram_tensor("out_dram", (B, S, C), F32, kind="ExternalOutput").ap()
    build_tower(nc, aps, out)
    r = run_bass_kernel_spmd(nc, [arrays], core_ids=[0])
    return r.results[0]["out_dram"]


_WEIGHTS = ["L0_attn_wq", "L0_attn_bq", "L0_attn_wk", "L0_attn_bk", "L0_attn_wv", "L0_attn_bv",
            "L0_attn_gamma", "L0_attn_beta", "L1_attn_Wq", "L1_attn_bq", "L1_attn_Wk", "L1_attn_bk",
            "L1_attn_Wv", "L1_attn_bv", "L1_attn_Wout", "L1_attn_bout", "L1_ffn_Wq", "L1_ffn_keys",
            "L1_ffn_w_down", "L1_ffn_w_up"]
```

```python
from contextlib import ExitStack

import numpy as np

import concourse.bass as bass
from concourse import mybir

F32 = mybir.dt.float32
BF16 = mybir.dt.bfloat16
U32 = mybir.dt.uint32
I32 = mybir.dt.int32
ALU = mybir.AluOpType
ACT = mybir.ActivationFunctionType
X = mybir.AxisListType.X

P = 128
C = 128
B = 2
S = 1024
NTOK = B * S
NT = NTOK // P
KT = S // P
HL = 4
H0, D0 = 16, 8
UNITS = B * H0 // HL
H1, D1 = 4, 16
E1 = H1 * D1
WIN = 32
QC = 512
LN_EPS, BN_EPS = 1e-5, 1e-3
BIG = 1e30
Q_PART = (0, 0, 1, 0, 2, 1)
K_PART = (0, 1, 0, 2, 0, 1)
LEAD1 = 12
LEAD0 = 20
SHIFT0 = len(Q_PART) * D0
SHIFT1 = len(Q_PART) * D1
TW = S + S - P
NH, NK, TK = 8, 64, 8
VL = 32
HT = P // 2


class Tally:

    def __init__(self, eng, sem):
        self.eng, self.sem, self.n = eng, sem, 0

    def then_wait(self, ins):
        ins.then_inc(self.sem, 1)
        self.n += 1
        self.eng.wait_ge(self.sem, self.n)


def build_tower(nc, a, out):
    ctx = ExitStack()
    with ctx:
        def sb(name, shape, dt=F32):
            return ctx.enter_context(nc.sbuf_tensor(name, shape, dt))

        sems = {}

        def sem(name):
            if name not in sems:
                sems[name] = ctx.enter_context(nc.semaphore(name))
            return sems[name]

        h = sb("h", [P, NT, C])
        xn = sb("xn", [P, NT, C])
        tmp = sb("tmp", [P, NT, C])
        xT = sb("xT", [C, NTOK])
        stat = sb("stat", [P, 8, NT])
        halves = sb("halves", [P, NT, 6])
        moments = sb("moments", [P, NT, 2])
        ident = sb("ident", [P, P])
        ones = sb("ones", [P, P])
        idx = sb("idx", [P, NT], I32)
        wts = sb("wts", [C, 3, C])
        cols = sb("cols", [C, 4])
        rows = sb("rows", [1, 4, C])
        big = sb("big", [P, 48 * 1024], BF16)
        vall = sb("vall", [P, UNITS, KT, HL, D0 + 1])
        vst = sb("vst", [P, KT, HL, 32])
        probs = sb("probs", [P, 2, HL, QC])
        osb = sb("osb", [P, QC])
        mhalf = sb("mhalf", [P, 32, 2])
        mx = sb("mx", [P, 32])
        shf = sb("shf", [32, P])
        sh = sb("sh", [32, 3, P], BF16)
        rden = sb("rden", [P, 4, HL])
        bn = sb("bn", [P, 5, C])
        bn_r = bn[:, 3, :]
        w1 = sb("w1", [C, 3, E1])
        wout = sb("wout", [E1 + 1, C])
        cols1 = sb("cols1", [E1, 2])
        rows1 = sb("rows1", [1, 1, C])
        gt = sb("gt", [P, 2])
        minus_theta = sb("minus_theta", [P, 1])
        dist = sb("dist", [P, TW])
        near = sb("near", [P, 3, P])
        wmask = sb("wmask", [P, 256])
        wscr = sb("wscr", [P, 2, 192])
        mx1 = sb("mx1", [P, 64])
        wf = sb("wf", [C, NH * P])
        bf = sb("bf", [1, NH * P])
        bqt = sb("bqt", [P, NH])
        bf3 = sb("bf3", [3, NH * P], BF16)
        ones3 = sb("ones3", [3, P], BF16)
        ps = ctx.enter_context(nc.psum_tensor("ps", [P, 8, QC], F32))
        score_ps = ps[:, 0:4, :].rearrange("p (s x) n -> p s x n", s=2)
        max_ps = ps[:, 4:6, :]
        o_ps = ps[:, 6:8, :]

        QS = big[:, 0:32768].rearrange("p (r u x n) -> p r u x n", r=2, u=UNITS, x=2)
        KS = big[:, 32768:49152].rearrange("p (u h n) -> p u h n", u=UNITS, h=2)
        attn = tmp[:].rearrange("p t c -> p (t c)").rearrange("p (u t c) -> p u t c", u=UNITS, t=KT)
        q_cm = probs[:].rearrange("p a b n -> p (a b n)")[:, 0:NTOK]
        k_cm = probs[:].rearrange("p a b n -> p (a b n)")[:, NTOK:2 * NTOK]
        splits = sb("splits", [C, 2, 3, S], BF16)
        bfs = splits[0:1, 0, :, 0:NH * P]

        def part(at, n):
            return big[:, at:at + n]
        QS1 = part(0, 8192).rearrange("p (b h n) -> p b h n", b=B, h=H1)
        more_probs = part(8192, 8192).bitcast(F32).rearrange("p (s h n) -> p s h n", s=2, h=H1)
        probs1 = [probs[:, 0], probs[:, 1], more_probs[:, 0], more_probs[:, 1]]
        KS1 = part(16384, 8192).rearrange("p (b h n) -> p b h n", b=B, h=H1)
        wdt = part(24576, 8192).bitcast(F32).rearrange("p (v u) -> p v u", v=VL)
        wup = part(32768, 8192).bitcast(F32).rearrange("p (v d) -> p v d", v=VL)
        wdr = part(40960, 8192).bitcast(F32).rearrange("p (v d) -> p v d", v=VL)
        sh1 = sb("sh1", [64, 3, P], BF16)
        shf1 = sb("shf1", [64, P])
        vall1 = vall[:].rearrange("p u t h d -> p (u t h d)")[:, 0:B * KT * H1 * (D1 + 1)]\
            .rearrange("p (b t h d) -> p b t h d", b=B, t=KT, h=H1)
        attn1 = tmp[:].rearrange("p t c -> p (t c)")[:, 0:NT * E1].rearrange("p (t c) -> p t c", t=NT)
        aT = xT[0:E1 + 1, :]
        ge = part(0, 16384).bitcast(F32).rearrange("p (x v n) -> p x v n", x=2, v=VL)
        onehot = part(16384, 4096).bitcast(F32).rearrange("p (x c u) -> p x c u", x=2, c=8)
        weigh = part(20480, 2048).bitcast(F32).rearrange("p (x c v) -> p x c v", x=2, c=8)
        gated = part(22528, 2048).bitcast(F32).rearrange("p (x i n) -> p x i n", x=2, i=4)
        relued = splits[:].rearrange("p w s n -> p (w s n)")[:, 0:2048].bitcast(F32)\
            .rearrange("p (x i n) -> p x i n", x=2, i=4)
        flat = probs[:].rearrange("p a b n -> p (a b n)")
        room = [0]

        def pick(n):
            room[0] += n
            return flat[:, room[0] - n:room[0]]
        top = pick(128).rearrange("p (h q k) -> p h q k", h=NH, q=2)
        top_at = pick(128).bitcast(U32).rearrange("p (h q k) -> p h q k", h=NH, q=2)
        sums = pick(512).rearrange("p (h i j) -> p h i j", h=NH, i=TK)
        best = pick(64).rearrange("p (h k) -> p h k", h=NH)
        best_at = pick(64).bitcast(U32).rearrange("p (h k) -> p h k", h=NH)
        side = [pick(64).bitcast(U32).rearrange("p (h k) -> p h k", h=NH) for _ in range(2)]
        match = [pick(512).rearrange("p (h k i) -> p h k i", h=NH, k=TK) for _ in range(2)]
        key_at = [pick(64) for _ in range(2)]
        upper = pick(64)
        ev = pick(64).rearrange("p (h k) -> p h k", h=NH)
        evd = pick(64).rearrange("p (h k) -> p h k", h=NH)
        esum = pick(8)
        rsum = pick(8)
        trip = pick(384).rearrange("p (w d n) -> p w d n", w=3, d=2)
        uvw = pick(384).rearrange("p (x w n) -> p x w n", x=2, w=3)
        zt = pick(128)
        assert room[0] <= flat.shape[1]
        iota_f = sb("iota_f", [P, P])
        kbd = flat[:, 0:1024].rearrange("p (h c) -> p h c", h=NH)
        wqr = flat[:, 1024:2048]
        wqT = flat[:, 2048:3072].rearrange("p (h c) -> p h c", h=NH)
        kT = flat[:, 3072:4096].rearrange("p (h n) -> p h n", h=NH)
        s_ps = ps[:, 0:2, :].rearrange("p a n -> p (a n)").rearrange("p (h q n) -> p h q n", h=NH, q=2)
        g_ps, in_ps, acc_ps, t_ps = ps[:, 2:4, :], ps[:, 4:6, :], ps[:, 6, 0:C], ps[:, 7, :]

        q_scr = nc.dram_tensor("q_scr", [3, C, NTOK], BF16).ap()
        k_scr = nc.dram_tensor("k_scr", [3, C, NTOK], BF16).ap()
        q1_scr = nc.dram_tensor("q1_scr", [3, E1, NTOK], BF16).ap()
        k1_scr = nc.dram_tensor("k1_scr", [3, E1, NTOK], BF16).ap()
        out_v = out.rearrange("b (t p) c -> p (b t) c", p=P)

        big_f = big[:].bitcast(F32)
        Q_ZEROS = 12288
        TWO_MINUS_ONES = float(np.array([0xBF80BF80], np.uint32).view(np.float32)[0])

        def spread(col, n):
            return col.unsqueeze(2).broadcast_to([col.shape[0], col.shape[1], n])

        block = ctx.enter_context(nc.Block())

        w_in, tok_in = sem("w_in"), sem("tok_in")
        gathered = [sem(f"gathered_{b}") for b in range(B)]
        consts, consts_f, zeroed = sem("consts"), sem("consts_f"), sem("zeroed")
        ln_var, ln_sqrt, ln_done = sem("ln_var"), sem("ln_sqrt"), sem("ln_done")
        turned, turned_out = sem("turned"), sem("turned_out")
        proj, proj_out = sem("proj"), sem("proj_out")
        split_done, split_out = sem("split_done"), sem("split_out")
        stack_in = [sem(f"stack_in_{b}") for b in range(B)]
        v_done, v_out = sem("v_done"), sem("v_out")
        max_scores, max_read, unit_max = sem("max_scores"), sem("max_read"), sem("unit_max")
        max_turned, shift_split, shift_rows = sem("max_turned"), sem("shift_split"), sem("shift_rows")
        scores_ready, exp_done, pv_done = sem("scores_ready"), sem("exp_done"), sem("pv_done")
        v_staged, o_read, o_turned, o_norm = sem("v_staged"), sem("o_read"), sem("o_turned"), sem("o_norm")
        saved = sem("saved")
        bn_ready, bn_made, bn_root = sem("bn_ready"), sem("bn_made"), sem("bn_root")
        w1_in, fold_in, fold_ready, fold_made, fold_out = (sem(x) for x in (
            "w1_in", "fold_in", "fold_ready", "fold_made", "fold_out"))
        dist_num, dist_arg, dist_done = sem("dist_num"), sem("dist_arg"), sem("dist_done")
        wd_in, wu_in, wd_turned, wd_out = sem("wd_in"), sem("wu_in"), sem("wd_turned"), sem("wd_out")
        proj1, proj1_out, split1_done, split1_out = (sem(x) for x in (
            "proj1", "proj1_out", "split1_done", "split1_out"))
        stack1_in = [sem(f"stack1_in_{b}") for b in range(B)]
        bn_centred, bn_squared = sem("bn_centred"), sem("bn_squared")
        zeroed1, v1_done, v1_out = sem("zeroed1"), sem("v1_done"), sem("v1_out")
        max1_scores, max1_read, unit1_max, max1_turned, shift1_split, shift1_rows = (sem(x) for x in (
            "max1_scores", "max1_read", "unit1_max", "max1_turned", "shift1_split", "shift1_rows"))
        scores1_ready, exp1_done, scaled_dve, scaled_pool, pv1_done = (sem(x) for x in (
            "scores1_ready", "exp1_done", "scaled_dve", "scaled_pool", "pv1_done"))
        v1_staged, o1_read, o1_turned, o1_norm = (sem(x) for x in ("v1_staged", "o1_read", "o1_turned", "o1_norm"))
        attn1_done, a_turned, a_out, wo_made = (sem(x) for x in (
            "attn1_done", "a_turned", "a_out", "wo_made"))
        zt_staged, s_ready, s_picked, diff_done, pexp_done, trip_done, trip_turned, uvw_ready = (sem(x) for x in (
            "zt_staged", "s_ready", "s_picked", "diff_done", "pexp_done", "trip_done", "trip_turned", "uvw_ready"))
        a_made, b_made, b_weighted, g_made, ge_out, inner_ready, gr_done, acc_used, h_out = (sem(x) for x in (
            "a_made", "b_made", "b_weighted", "g_made", "ge_out", "inner_ready", "gr_done", "acc_used", "h_out"))
        inner_relu = sem("inner_relu")
        pick_order, bf_split, bf_in = sem("pick_order"), sem("bf_split"), sem("bf_in")

        STEPS1 = [(qh, kt, pr) for qh in range(2) for kt in range(KT) for pr in range(2)]
        WSTEPS = [(i, k) for i in range(KT) for k in (i - 1, i, i + 1) if 0 <= k < KT]
        NE1, NV1 = len(STEPS1) + len(WSTEPS), KT * 2 + len(WSTEPS)
        MAX1 = [("full", hl, qt, kh) for hl in range(HL) for qt in range(KT) for kh in range(2)] + \
               [("near", hl, qt, 0) for hl in range(HL) for qt in range(KT)]

        def score_at(e):
            return score_ps[:, e % 2] if e < len(STEPS1) else ps[:, (e - len(STEPS1)) % 4, :]

        def score_turn(b, e):
            w = e - len(STEPS1)
            if e < 2:
                return NE1 * b
            return NE1 * b + (e - 1 if w < 0 else e - 1 - w % 2 if w < 2 else len(STEPS1) if w < 4 else e - 3)

        def v_due(e):
            if e < len(STEPS1):
                return e // 2 - 3 if e % 2 == 0 and e >= 6 else None
            return e - len(STEPS1) + 13

        def on_pool(b, e):
            return e < len(STEPS1) and e % 2 == 1 and (b == 0 or e % 4 == 3)

        def scaled_until(b, e, pool_side):
            return sum(on_pool(bb, ee) == pool_side for bb in range(B) for ee in range(NE1) if (bb, ee) <= (b, e))

        LN_SEQ = (0, 1, 0, 0, 1, 1, 0, 1)

        def ln_tiles(k):
            return slice(KT * LN_SEQ[k - 1], KT * LN_SEQ[k - 1] + KT)

        def slot_turn(b, v):
            if v >= 4:
                return NV1 * b + v - 3
            return NV1 * b if b else 0

        def window_of(qt):
            return (0, 64) if qt == 0 else (S - 192, 0) if qt == KT - 1 else (qt * P - WIN, 32)

        STEPS0 = [(qh, kt, pr) for qh in range(2) for kt in range(KT) for pr in range(2)]
        MAX0 = [(par, x, qt, kh) for par in range(2) for x in range(2) for qt in range(KT) for kh in range(2)]
        MAXED = (len(MAX0) - LEAD0) // 2 - 1

        def score_slot(e, left):
            return ps[:, 2 * (e % 3):2 * (e % 3) + 2, :] if left == 0 else score_ps[:, e % 2]

        def max_bank(n, i):
            return 2 + i % 4 if isinstance(n, int) and n == 0 else 4 + i % 2

        def max_unit_at(n, k, left):
            ahead, i = divmod(k + LEAD0, len(MAX0))
            return (n + 1 + ahead, i) if left > ahead else None

        @block.sync
        def _(sp):
            sp.dma_start(wqr, a["L1_ffn_Wq"]).then_inc(fold_in, 16)
            sp.dma_start(bqt[:], a["bqt"]).then_inc(fold_in, 16)
            sp.wait_ge(fold_ready, 1)
            for q in range(2):
                sp.dma_start(kbd[NK * q:NK * q + NK, :, NK * q:NK * q + NK],
                             a["L1_ffn_keys"][:, q].rearrange("h n c -> n h c")).then_inc(fold_in, 16)
            for i, w in enumerate(("L0_attn_wq", "L0_attn_wk", "L0_attn_wv")):
                sp.dma_start(wts[:, i, :], a[w]).then_inc(w_in, 16)
            for i, w in enumerate(("L0_attn_bq", "L0_attn_bk")):
                sp.dma_start(cols[:, i:i + 1], a[w].rearrange("(c o) -> c o", o=1)).then_inc(w_in, 16)
            for i, w in enumerate(("L0_attn_bv", "L0_attn_gamma", "L0_attn_beta")):
                sp.dma_start(rows[:, i, :], a[w].rearrange("(o c) -> o c", o=1)).then_inc(w_in, 16)
            for i, w in enumerate(("L1_attn_Wq", "L1_attn_Wk", "L1_attn_Wv")):
                sp.dma_start(w1[:, i, :], a[w]).then_inc(w1_in, 16)
            sp.dma_start(wout[0:E1, :], a["L1_attn_Wout"]).then_inc(w1_in, 16)
            for i, w in enumerate(("L1_attn_bq", "L1_attn_bk")):
                sp.dma_start(cols1[:, i:i + 1], a[w].rearrange("(c o) -> c o", o=1)).then_inc(w1_in, 16)
            sp.dma_start(rows1[:, 0, 0:E1], a["L1_attn_bv"].rearrange("(o c) -> o c", o=1)).then_inc(w1_in, 16)
            sp.dma_start(wout[E1:E1 + 1, :], a["L1_attn_bout"].rearrange("(o c) -> o c", o=1)).then_inc(w1_in, 16)

            def send_splits(b, scr, rows_, done, sent):
                for w in range(2):
                    sp.wait_ge(done, 6 * b + 3 * w + 3)
                    sp.dma_start(scr[w][:, :, b * S:(b + 1) * S].rearrange("s c t -> c s t"),
                                 splits[0:rows_, w]).then_inc(sent, 16)
                sp.wait_ge(sent, 32 * (b + 1))

            Q8 = big[:, 0:32768].rearrange("p (r b g n) -> p r b g n", r=2, b=B, g=8)
            K8 = big[:, 32768:49152].rearrange("p (b g n) -> p b g n", b=B, g=8)
            for b in range(B):
                send_splits(b, (q_scr, k_scr), C, split_done, split_out)
                sp.wait_ge(zeroed, 3)
                for r in range(len(Q_PART)):
                    for par in range(2):
                        at = 64 * par + D0 * r
                        qsrc = q_scr[Q_PART[r], :, b * S:(b + 1) * S].rearrange("(g r d) t -> r d g t", r=2, d=D0)
                        ksrc = k_scr[K_PART[r], :, b * S:(b + 1) * S].rearrange("(g r d) t -> r d g t", r=2, d=D0)
                        sp.dma_start(Q8[at:at + D0, par, b, :, :], qsrc[par]).then_inc(stack_in[b], 16)
                        sp.dma_start(K8[at:at + D0, b, :, :], ksrc[par]).then_inc(stack_in[b], 16)
            def send_shift(n):
                sp.wait_ge(shift_split, 4 * n + 4)
                for i in range(3):
                    for par in range(2):
                        at = 64 * par + SHIFT0 + i
                        sp.dma_start(QS[at:at + 1, par, n, :, :].rearrange("o x (t n) -> o (x t) n", n=P),
                                     sh[16 * par:16 * par + 16, i, :]).then_inc(shift_rows, 16)

            with sp.Fori(0, UNITS) as n:
                send_shift(n)
            sp.wait_ge(bf_split, 1)
            sp.dma_start(bf3[:], bfs).then_inc(bf_in, 16)
            sp.wait_ge(pv_done, 16 * UNITS)
            sp.dma_start(wdr, a["L1_ffn_w_down"].rearrange("(u v) d -> u v d", v=VL)).then_inc(wd_in, 16)
            sp.dma_start(wup, a["L1_ffn_w_up"].rearrange("(u v) d -> u v d", v=VL)).then_inc(wu_in, 16)
            for b in range(B):
                send_splits(b, (q1_scr, k1_scr), E1, split1_done, split1_out)
                for r in range(len(Q_PART)):
                    at = D1 * r
                    qsrc = q1_scr[Q_PART[r], :, b * S:(b + 1) * S].rearrange("(h d) t -> d h t", d=D1)
                    ksrc = k1_scr[K_PART[r], :, b * S:(b + 1) * S].rearrange("(h d) t -> d h t", d=D1)
                    sp.dma_start(QS1[at:at + D1, b, :, :], qsrc).then_inc(stack1_in[b], 16)
                    sp.dma_start(KS1[at:at + D1, b, :, :], ksrc).then_inc(stack1_in[b], 16)
            for b in range(B):
                sp.wait_ge(shift1_split, 4 * b + 4)
                for i in range(3):
                    for w in range(2):
                        at = SHIFT1 + 3 * w + i
                        sp.dma_start(QS1[at:at + 1, b, :, :].rearrange("o h (t n) -> o (h t) n", n=P),
                                     sh1[32 * w:32 * w + 32, i, :]).then_inc(shift1_rows, 16)
            with sp.Fori(0, NT) as t:
                sp.wait_ge(h_out, t + 1)
                sp.dma_start(out_v[:, t, :], h[:, t, :]).then_inc(saved, 16)
            sp.wait_ge(saved, 16 * NT)

        @block.gpsimd
        def _(pool):
            pool.dma_start(idx[:], a["tok"]).then_inc(tok_in, 16)
            for i, w in enumerate(("L1_attn_gamma", "L1_attn_theta")):
                pool.dma_start(gt[:, i:i + 1], a[w].partition_broadcast(P)).then_inc(sem("gt_in"), 16)
            pool.memset(ident[:], 0.0).then_inc(consts, 1)
            pool.memset(ones[:], 1.0).then_inc(consts, 1)
            pool.memset(ones3[:], 1.0).then_inc(consts_f, 1)
            pool.wait_ge(consts, 2)
            pool.affine_select(out=ident[:], in_=ident[:], compare_op=ALU.not_equal, fill=1.0, base=0,
                               pattern=[[-1, P]], channel_multiplier=1).then_inc(consts, 1)
            pool.wait_ge(tok_in, 16)
            for t in range(NT):
                pool.indirect_dma_start(h[:, t, :], None, a["emb"],
                                        bass.IndirectOffsetOnAxis(idx[:, t:t + 1].bitcast(U32), 0))\
                    .then_inc(gathered[t // KT], 16)
            pool.memset(vst[:], 0.0).then_inc(consts, 1)
            pool.memset(vall[:, :, :, :, D0:D0 + 1], 1.0).then_inc(consts, 1)
            pool.iota(dist[:], [[1, TW]], base=-(S - P), channel_multiplier=-1,
                      allow_small_or_imprecise_dtypes=True).then_inc(dist_num, 1)
            pool.iota(iota_f[:], [[1, P]], base=0, channel_multiplier=0,
                      allow_small_or_imprecise_dtypes=True).then_inc(consts_f, 1)
            pool.memset(wmask[:], 0.0).then_inc(consts_f, 1)
            pool.wait_ge(consts_f, 3)
            pool.affine_select(out=wmask[:], in_=wmask[:], compare_op=ALU.is_ge, fill=-BIG, base=64 + WIN,
                               pattern=[[-1, 256]], channel_multiplier=1).then_inc(consts_f, 1)
            pool.wait_ge(consts_f, 4)
            pool.affine_select(out=wmask[:], in_=wmask[:], compare_op=ALU.is_ge, fill=-BIG, base=WIN - 64,
                               pattern=[[1, 256]], channel_multiplier=-1).then_inc(consts_f, 1)
            pool.wait_ge(dist_done, 4)
            for d in range(3):
                src = S - P - P * (d - 1)
                pool.tensor_copy(near[:, d, :], dist[:, src:src + P]).then_inc(consts_f, 1)
                pool.wait_ge(consts_f, 5 + 3 * d + 1)
                pool.affine_select(out=near[:, d, :], in_=near[:, d, :], compare_op=ALU.is_ge, fill=0.0,
                                   base=WIN + P * (d - 1), pattern=[[-1, P]], channel_multiplier=1).then_inc(consts_f, 1)
                pool.wait_ge(consts_f, 5 + 3 * d + 2)
                pool.affine_select(out=near[:, d, :], in_=near[:, d, :], compare_op=ALU.is_ge, fill=0.0,
                                   base=WIN - P * (d - 1), pattern=[[1, P]], channel_multiplier=-1).then_inc(consts_f, 1)
            pool.wait_ge(consts, 5)
            pool.wait_ge(v_out, NT)
            pool.tensor_copy(vst[:, :, :, 0:D0 + 1], vall[:, 0, :, :, :]).then_inc(v_staged, 1)
            with pool.Fori(1, UNITS) as n:
                pool.wait_ge(pv_done, 16 * n)
                pool.tensor_copy(vst[:, :, :, 0:D0 + 1], vall[:, n, :, :, :]).then_inc(v_staged, 1)
            pool.wait_ge(pv_done, 16 * UNITS)
            pool.memset(vall1[:, :, :, :, D1:D1 + 1], 1.0).then_inc(zeroed1, 1)
            pool.wait_ge(zeroed1, 1)
            pool.memset(KS1[SHIFT1:SHIFT1 + 6], -1.0).then_inc(zeroed1, 1)
            pool.wait_ge(zeroed1, 2)
            for b in range(B):
                pool.wait_ge(v1_out, NT)
                if b == 0:
                    pool.memset(aT[E1:E1 + 1, :], 1.0).then_inc(zeroed1, 1)
                    pool.wait_ge(zeroed1, 3)
                if b:
                    pool.wait_ge(pv1_done, NV1)
                pool.tensor_copy(vst[:, :, :, 0:D1 + 1], vall1[:, b, :, :, :]).then_inc(v1_staged, 1)
                for e, (qh, kt, pr) in enumerate(STEPS1):
                    if on_pool(b, e):
                        pool.wait_ge(exp1_done, NE1 * b + e + 1)
                        at = qh * QC - kt * P + S - P
                        slot = probs1[e // 2 % 4][:, 2:4, :]
                        pool.tensor_tensor(slot, slot, dist[:, at:at + QC].unsqueeze(1).broadcast_to([P, 2, QC]),
                                           ALU.mult).then_inc(scaled_pool, 1)

            def gate_inner(t, x, q):
                pool.wait_ge(inner_relu, 8 * t + q + 1)
                if q == 0:
                    pool.wait_ge(ge_out, 8 * t + 8)
                if not (isinstance(t, int) and 8 * t + q < 2):
                    pool.wait_ge(acc_used, 8 * t + q - 1)
                pool.tensor_tensor(gated[:, q % 2], relued[:, q % 2], ge[:, x, 4 * q:4 * q + 4, :], ALU.mult)\
                    .then_inc(gr_done, 1)

            def tile(t, x, back):
                for g in range(8):
                    pool.wait_ge(b_made, 8 * t + g + 1)
                    pool.tensor_tensor(weigh[:, g % 2], weigh[:, g % 2], spread(uvw[:, x, 2, 8 * g:8 * g + 8], 64),
                                       ALU.mult).then_inc(b_weighted, 1)
                    if back:
                        gate_inner(t - 1, 1 - x, g)

            tile(0, 0, False)
            tile(1, 1, True)
            with pool.Fori(1, NT // 2) as m:
                for x in range(2):
                    tile(2 * m + x, x, True)
            for q in range(8):
                gate_inner(NT - 1, 1, q)

        @block.scalar
        def _(act):
            def ln_root(k):
                act.wait_ge(ln_var, k)
                act.activation(stat[:, 3, ln_tiles(k)], stat[:, 2, ln_tiles(k)], ACT.Sqrt).then_inc(ln_sqrt, 1)

            act.wait_ge(consts, 2)
            act.activation(big_f[:, 0:Q_ZEROS], ones[:, 0:1].broadcast_to([P, Q_ZEROS]), ACT.Copy, scale=0.0)\
                .then_inc(zeroed, 1)
            for i in range(4):
                dst = (wqT, kT)[i // 2]
                act.wait_ge(fold_made, i + 1)
                act.activation(dst[:, 4 * (i % 2):4 * (i % 2) + 4, :].rearrange("p h c -> p (h c)"), ps[:, i, :],
                               ACT.Copy).then_inc(fold_out, 1)
            ln_root(1)
            for i in range(2):
                act.wait_ge(fold_made, 5)
                act.activation(wf[:, i * QC:(i + 1) * QC], ps[:, 4 + i, :], ACT.Copy).then_inc(fold_out, 1)
                act.activation(bf[:, i * QC:(i + 1) * QC], ps[0:1, 6 + i, :], ACT.Copy).then_inc(fold_out, 1)
            for b in range(B):
                if b:
                    ln_root(b + 1)
                if b == 0:
                    act.wait_ge(w_in, 16 * 8)
                    act.wait_ge(fold_made, 5)
                    act.wait_ge(consts, 5)
                for i, dst in enumerate((q_cm, k_cm)):
                    for j in range(2):
                        act.wait_ge(proj, 4 * b + 2 * i + j + 1)
                        act.activation(dst[:, b * S + j * QC:b * S + (j + 1) * QC], ps[:, 2 + 2 * i + j, :], ACT.Relu,
                                       bias=cols[:, i:i + 1]).then_inc(proj_out, 1)
                for kt in range(KT):
                    act.wait_ge(v_done, KT * b + kt + 1)
                    act.activation(vall[:, 4 * b:4 * b + 4, kt, :, 0:D0],
                                   ps[:, 6 + kt % 2, 0:C].rearrange("p (g h d) -> p g h d", g=4, h=HL),
                                   ACT.Relu).then_inc(v_out, 1)
            act.wait_ge(sem("gt_in"), 32)
            act.activation(minus_theta[:], gt[:, 1:2], ACT.Copy, scale=-1.0).then_inc(dist_arg, 1)
            act.wait_ge(dist_num, 1)
            act.activation(dist[:], dist[:], ACT.Square).then_inc(dist_done, 1)
            act.wait_ge(dist_arg, 1)
            act.wait_ge(dist_done, 1)
            act.activation(dist[:], dist[:], ACT.Abs, scale=gt[:, 0:1], bias=minus_theta[:]).then_inc(dist_done, 1)
            for i, sc in enumerate((-1.0, 1.0)):
                act.wait_ge(dist_done, i + 2)
                act.activation(dist[:], dist[:], ACT.Exp, scale=sc).then_inc(dist_done, 1)

            def exps(n, left):
                for e, (qh, kt, pr) in enumerate(STEPS0):
                    act.wait_ge(scores_ready, 32 * n + e + 1)
                    v = e // 2
                    if not isinstance(n, int) or 16 * n + v >= 2:
                        act.wait_ge(pv_done, 16 * n + v - 1)
                    act.activation(probs[:, v % 2, 2 * pr:2 * pr + 2, :], score_slot(e, left), ACT.Exp,
                                   scale=D0 ** -0.5).then_inc(exp_done, 1)

            act.wait_ge(split_done, 12)
            exps(0, UNITS - 1)
            with act.Fori(1, UNITS - 1) as n:
                exps(n, 1)
            exps(UNITS - 1, 0)
            for b in range(B):
                act.wait_ge(bn_centred, b + 1)
                act.activation(tmp[:, b * KT:(b + 1) * KT, :], xn[:, b * KT:(b + 1) * KT, :], ACT.Square).then_inc(bn_squared, 1)
            act.wait_ge(bn_ready, 3)
            act.activation(bn[:, 2, :], bn[:, 1, :], ACT.Sqrt).then_inc(bn_root, 1)
            for r in range(8):
                act.wait_ge(wd_turned, r + 1)
                act.activation(wdt[:, 4 * r:4 * r + 4, :].rearrange("p v u -> p (v u)"), ps[:, 6 + r % 2, :],
                               ACT.Copy).then_inc(wd_out, 1)
            act.wait_ge(w1_in, 16 * 8)
            act.wait_ge(zeroed1, 1)
            for b in range(B):
                ln_root(3 + 2 * b)
                ln_root(4 + 2 * b)
                for i, dst in enumerate((q_cm, k_cm)):
                    for j in range(2):
                        act.wait_ge(proj1, 4 * b + 2 * i + j + 1)
                        act.activation(dst[0:E1, b * S + j * QC:b * S + (j + 1) * QC], ps[0:E1, 2 + 2 * i + j, :],
                                       ACT.Identity, bias=cols1[:, i:i + 1]).then_inc(proj1_out, 1)
                for kt in range(KT):
                    act.wait_ge(v1_done, KT * b + kt + 1)
                    act.activation(vall1[:, b, kt, :, 0:D1],
                                   ps[:, 6 + kt % 2, 0:E1].rearrange("p (h d) -> p h d", h=H1), ACT.Copy).then_inc(v1_out, 1)
            act.wait_ge(split1_done, 12)

            def take_a(b):
                for j in range(2):
                    act.wait_ge(a_turned, 2 * b + j + 1)
                    at = b * S + j * QC
                    act.activation(aT[0:E1, at:at + QC], max_ps[0:E1, j, :], ACT.Copy).then_inc(a_out, 1)

            for b in range(B):
                for e in range(NE1):
                    act.wait_ge(scores1_ready, NE1 * b + e + 1)
                    if e < len(STEPS1):
                        qh, kt, pr = STEPS1[e]
                        v = e // 2
                        dst, src = probs1[v % 4][:, 2 * pr:2 * pr + 2, :], score_at(e)
                    else:
                        v = e - len(STEPS1) + 16
                        dst, src = probs1[v % 4][:, 0, :], score_at(e)
                    if slot_turn(b, v):
                        act.wait_ge(pv1_done, slot_turn(b, v))
                    act.activation(dst, src, ACT.Exp, scale=E1 ** -0.5).then_inc(exp1_done, 1)
                    if b and e == 6:
                        take_a(0)
                    if b and e == 17:
                        ln_root(7)

            def stage_zt(t):
                if not isinstance(t, int) or t >= 1:
                    act.wait_ge(s_ready, t)
                act.activation(zt, xT[:, bass.ts(t, P)], ACT.Copy).then_inc(zt_staged, 1)

            def pick_exp(t):
                act.wait_ge(diff_done, t + 1)
                act.activation(ev, evd, ACT.Exp).then_inc(pexp_done, 1)

            def put_picks(t, x):
                act.wait_ge(trip_turned, t + 1)
                src = t_ps[:, 0:384].rearrange("p (w n) -> p w n", w=3)
                for y in range(2):
                    act.activation(uvw[HT * y:HT * y + HT, x, :, :], src[HT * y:HT * y + HT, :, HT * y:HT * y + HT],
                                   ACT.Copy).then_inc(uvw_ready, 1)

            def ge_part(t, x, g):
                if g == 0 and not (isinstance(t, int) and t < 2):
                    act.wait_ge(gr_done, 8 * (t - 1))
                act.wait_ge(g_made, 8 * t + g + 1)
                act.activation(ge[:, x, :, :].rearrange("p v (y n) -> p y v n", y=2)[:, :, :, 8 * g:8 * g + 8],
                               g_ps[:, g % 2, :].rearrange("p (c y v) -> p y v c", c=8, y=2),
                               ACT.Copy).then_inc(ge_out, 1)

            def relu_inner(t, q):
                act.wait_ge(inner_ready, 8 * t + q + 1)
                if not (isinstance(t, int) and 8 * t + q < 2):
                    act.wait_ge(gr_done, 8 * t + q - 1)
                act.activation(relued[:, q % 2], in_ps[:, q % 2, :].rearrange("p (i n) -> p i n", i=4),
                               ACT.Relu).then_inc(inner_relu, 1)

            act.wait_ge(turned_out, 10)
            stage_zt(0)
            take_a(1)
            stage_zt(1)
            pick_exp(0)
            ln_root(8)
            put_picks(0, 0)

            def tile(t, x, back, ahead):
                if ahead == 2:
                    stage_zt(t + 2)
                for g in range(8):
                    if back:
                        relu_inner(t - 1, g)
                    ge_part(t, x, g)
                    if ahead and g == 3:
                        pick_exp(t + 1)
                    if ahead and g == 5:
                        put_picks(t + 1, 1 - x)

            tile(0, 0, False, 2)
            tile(1, 1, True, 2)
            with act.Fori(1, NT // 2 - 1) as m:
                for x in range(2):
                    tile(2 * m + x, x, True, 2)
            for x in range(2):
                tile(NT - 2 + x, x, True, 1 - x)
            for q in range(8):
                relu_inner(NT - 1, q)

        @block.tensor
        def _(pe):
            pe.wait_ge(consts, 3)

            def turn_ln(k):
                pe.wait_ge(ln_done, k)
                at = 4 if k >= 7 else 0
                for j in range(2):
                    for i in range(4):
                        last = pe.transpose(ps[:, at + j, i * P:(i + 1) * P], xn[:, KT * LN_SEQ[k - 1] + 4 * j + i, :], ident[:])
                    last.then_inc(turned, 1)

            pe.wait_ge(fold_in, 16 * 4)
            for i in range(4):
                src = (wqr.rearrange("p (h c) -> p h c", h=NH), kbd)[i // 2]
                for j in range(4):
                    last = pe.transpose(ps[:, i, j * P:(j + 1) * P], src[:, 4 * (i % 2) + j, :], ident[:])
                last.then_inc(fold_made, 1)
            pe.wait_ge(fold_out, 4)
            for hh in range(NH):
                pe.matmul(ps[:, 4 + hh // 4, hh % 4 * P:hh % 4 * P + P], wqT[:, hh, :], kT[:, hh, :], start=True, stop=True)
                last = pe.matmul(ps[0:1, 6 + hh // 4, hh % 4 * P:hh % 4 * P + P], bqt[:, hh:hh + 1], kT[:, hh, :],
                                 start=True, stop=True)
            last.then_inc(fold_made, 1)
            for b in range(B):
                turn_ln(b + 1)
                if b == 0:
                    pe.wait_ge(w_in, 16 * 8)
                    pe.wait_ge(fold_out, 8)
                pe.wait_ge(turned_out, 2 * b + 2)
                for i in range(2):
                    for j in range(2):
                        if b:
                            pe.wait_ge(proj_out, 4 * (b - 1) + 2 * i + j + 1)
                        at = b * S + j * QC
                        pe.matmul(ps[:, 2 + 2 * i + j, :], wts[:, i, :], xT[:, at:at + QC], start=True, stop=True)\
                            .then_inc(proj, 1)
                for t in range(KT * b, KT * b + KT):
                    if t >= 2:
                        pe.wait_ge(v_out, t - 1)
                    o = ps[:, 6 + t % 2, 0:C]
                    pe.matmul(o, xT[:, t * P:(t + 1) * P], wts[:, 2, :], start=True, stop=False)
                    pe.matmul(o, ones[0:1, :], rows[0:1, 0, :], start=False, stop=True).then_inc(v_done, 1)

            def max_task(n, i):
                par, x, qt, kh = MAX0[i]
                if isinstance(n, int) and n == 0:
                    if i >= 4:
                        pe.wait_ge(max_read, i - 3)
                else:
                    pe.wait_ge(max_read, 64 * n + i - 1)
                pe.matmul(ps[:, max_bank(n, i), :], QS[:, par, n, x, qt * P:(qt + 1) * P],
                          KS[:, n, x, kh * QC:(kh + 1) * QC], start=True, stop=True).then_inc(max_scores, 1)

            def turn_max(n):
                pe.wait_ge(unit_max, n + 1)
                if not isinstance(n, int) or n >= 1:
                    pe.wait_ge(o_norm, 2 * n - 1)
                pe.transpose(o_ps[0:32, 0, 0:P], mx[:], ident[:]).then_inc(max_turned, 1)

            def pv(n, v, part):
                qh, kt = divmod(v, KT)
                if v == 0 and part == 0:
                    pe.wait_ge(v_staged, n + 1)
                    pe.wait_ge(shift_split, 4 * n + 4)
                if kt == 0 and part == 0 and (not isinstance(n, int) or 2 * n + qh >= 2):
                    pe.wait_ge(o_norm, 2 * n + qh - 1)
                if part == 0:
                    pe.wait_ge(exp_done, 32 * n + 2 * v + 2)
                at = part * QC // 2
                for hl in range(HL):
                    last = pe.matmul(o_ps[32 * hl:32 * hl + 32, qh, at:at + QC // 2], vst[:, kt, hl, :],
                                     probs[:, v % 2, hl, at:at + QC // 2], start=kt == 0 and part == 0,
                                     stop=kt == KT - 1 and part == 1)
                if part == 1:
                    last.then_inc(pv_done, 1)

            def turn_o(n, qh):
                pe.wait_ge(o_read, 2 * n + qh + 1)
                for i in range(4):
                    last = pe.transpose(o_ps[:, qh, i * P:(i + 1) * P], osb[:, i * P:(i + 1) * P], ident[:])
                last.then_inc(o_turned, 1)

            def unit(n, left):
                pe.wait_ge(shift_rows, 16 * 6 * (n + 1))
                for e, (qh, kt, pr) in enumerate(STEPS0):
                    if max_unit_at(n, 2 * e, left):
                        max_task(*max_unit_at(n, 2 * e, left))
                    if left == 0 and e >= 2:
                        if e == 2:
                            pe.wait_ge(max_read, len(MAX0) * UNITS)
                        else:
                            pe.wait_ge(exp_done, 32 * n + e - 2)
                    elif not isinstance(n, int) or 32 * n + e >= 2:
                        pe.wait_ge(exp_done, 32 * n + e - 1)
                    for x in range(2):
                        last = pe.matmul(score_slot(e, left)[:, x, :], KS[:, n, pr, kt * P:(kt + 1) * P],
                                         QS[:, x, n, pr, qh * QC:(qh + 1) * QC], start=True, stop=True)
                    last.then_inc(scores_ready, 1)
                    if max_unit_at(n, 2 * e + 1, left):
                        max_task(*max_unit_at(n, 2 * e + 1, left))
                    if e >= 2:
                        pv(n, e // 2 - 1, e % 2)
                    if e == 19:
                        turn_o(n, 0)
                    if left and e == MAXED + 2:
                        turn_max(n + 1)
                pv(n, 15, 0)
                pv(n, 15, 1)
                turn_o(n, 1)

            pe.wait_ge(v_out, NT)
            pe.wait_ge(stack_in[0], 16 * 24)
            for i in range(len(MAX0)):
                max_task(0, i)
            turn_max(0)
            for i in range(LEAD0):
                max_task(1, i)
            pe.wait_ge(stack_in[1], 16 * 24)
            pe.wait_ge(max_read, len(MAX0))
            unit(0, UNITS - 1)
            with pe.Fori(1, UNITS - 2) as n:
                unit(n, 2)
            unit(UNITS - 2, 1)
            unit(UNITS - 1, 0)

            pe.wait_ge(exp_done, 32 * UNITS)
            for t in range(NT):
                if t % KT == 0:
                    pe.wait_ge(bn_ready, t // KT + 1)
                last = pe.matmul(ps[:, 4, 0:C], ones[:], xn[:, t, :], start=t == 0, stop=t == NT - 1)
            last.then_inc(bn_made, 1)
            for i in range(2):
                last = pe.matmul(ps[:, 2 + i, 0:C], ones[0:1, :], rows[0:1, 1 + i, :], start=True, stop=True)
            last.then_inc(bn_made, 1)
            for t in range(NT):
                if t % KT == 0:
                    pe.wait_ge(bn_squared, t // KT + 1)
                last = pe.matmul(ps[:, 5, 0:C], ones[:], tmp[:, t, :], start=t == 0, stop=t == NT - 1)
            last.then_inc(bn_made, 1)
            pe.wait_ge(wd_in, 16)
            for r in range(8):
                if r >= 2:
                    pe.wait_ge(wd_out, r - 1)
                for i in range(4):
                    last = pe.transpose(ps[:, 6 + r % 2, i * P:(i + 1) * P], wdr[:, 4 * r + i, :], ident[:])
                last.then_inc(wd_turned, 1)
            pe.wait_ge(w1_in, 16 * 8)
            pe.wait_ge(wd_out, 8)
            for b in range(B):
                turn_ln(4 + 2 * b)
                pe.wait_ge(turned_out, 4 + 2 * b + 2)
                for i in range(2):
                    for j in range(2):
                        if b:
                            pe.wait_ge(proj1_out, 4 * (b - 1) + 2 * i + j + 1)
                        at = b * S + j * QC
                        pe.matmul(ps[0:E1, 2 + 2 * i + j, :], w1[:, i, :], xT[:, at:at + QC], start=True, stop=True)\
                            .then_inc(proj1, 1)
                for t in range(KT * b, KT * b + KT):
                    if t >= 2:
                        pe.wait_ge(v1_out, t - 1)
                    o = ps[:, 6 + t % 2, 0:E1]
                    pe.matmul(o, xT[:, t * P:(t + 1) * P], w1[:, 2, :], start=True, stop=False)
                    pe.matmul(o, ones[0:1, :], rows1[0:1, 0, 0:E1], start=False, stop=True).then_inc(v1_done, 1)

            def max1_task(b, i):
                kind, hl, qt, kh = MAX1[i]
                k = len(MAX1) * b + i
                if i == 0 and b:
                    pe.wait_ge(shift1_split, 4 * b)
                if b:
                    pe.wait_ge(max1_read, k - 1)
                elif k >= 4:
                    pe.wait_ge(max1_read, k - 3)
                k0, n = (kh * QC, QC) if kind == "full" else (window_of(qt)[0], 192)
                pe.matmul(ps[:, max_bank(b, i), 0:n], QS1[0:SHIFT1, b, hl, qt * P:(qt + 1) * P],
                          KS1[0:SHIFT1, b, hl, k0:k0 + n],
                          start=True, stop=True).then_inc(max1_scores, 1)

            def turn_max1(b):
                pe.wait_ge(unit1_max, b + 1)
                pe.transpose(max_ps[0:64, 0, 0:P], mx1[:], ident[:]).then_inc(max1_turned, 1)

            def pv1(b, v):
                if v == 0:
                    pe.wait_ge(v1_staged, b + 1)
                if v < 16:
                    qh, kt = divmod(v, KT)
                    if kt == 0 and 4 * b + qh >= 2:
                        pe.wait_ge(o1_norm, 4 * b + qh - 1)
                    pe.wait_ge(scaled_dve, scaled_until(b, 2 * v + 1, False))
                    pe.wait_ge(scaled_pool, scaled_until(b, 2 * v + 1, True))
                    for hl in range(HL):
                        last = pe.matmul(o_ps[32 * hl:32 * hl + 32, qh, :], vst[:, kt, hl, :], probs1[v % 4][:, hl, :],
                                         start=kt == 0, stop=kt == KT - 1)
                else:
                    i, kt = WSTEPS[v - 16]
                    if i % 4 == 0 and kt == max(i - 1, 0):
                        pe.wait_ge(o1_norm, 4 * b + 2 + i // 4 - 1)
                    pe.wait_ge(scaled_dve, scaled_until(b, v + 16, False))
                    for hl in range(HL):
                        last = pe.matmul(o_ps[32 * hl:32 * hl + 32, i // 4, i % 4 * P:i % 4 * P + P], vst[:, kt, hl, :],
                                         probs1[v % 4][:, 0, hl * P:(hl + 1) * P],
                                         start=kt == max(i - 1, 0), stop=kt == min(i + 1, KT - 1))
                last.then_inc(pv1_done, 1)

            def turn_o1(w):
                pe.wait_ge(o1_read, w + 1)
                for i in range(4):
                    last = pe.transpose(o_ps[:, w % 2, i * P:(i + 1) * P], osb[:, i * P:(i + 1) * P], ident[:])
                last.then_inc(o1_turned, 1)

            def turn_a(b):
                pe.wait_ge(attn1_done, 2 * (b + 1))
                if b:
                    pe.wait_ge(turned_out, 10)
                for j in range(2):
                    for i in range(4):
                        last = pe.transpose(max_ps[0:E1, j, i * P:(i + 1) * P], attn1[:, KT * b + 4 * j + i, :], ident[:])
                    last.then_inc(a_turned, 1)

            def project_out(b):
                pe.wait_ge(zeroed1, 3)
                for j in range(2):
                    pe.wait_ge(a_out, 2 * b + j + 1)
                    for i in range(4):
                        t = KT * b + 4 * j + i
                        last = pe.matmul(max_ps[:, j, i * P:(i + 1) * P], aT[:, t * P:(t + 1) * P], wout[:],
                                         start=True, stop=True)
                    last.then_inc(wo_made, 1)

            def first_sequence_out(e):
                if e == 4:
                    turn_a(0)
                if e == 8:
                    project_out(0)
                if e == 22:
                    turn_ln(7)

            def sequence(b, more):
                pe.wait_ge(shift1_rows, 16 * 6 * (b + 1))
                todo = LEAD1
                for e in range(NE1):
                    if score_turn(b, e):
                        pe.wait_ge(exp1_done, score_turn(b, e))
                    if e < len(STEPS1):
                        qh, kt, pr = STEPS1[e]
                        for x in range(2):
                            last = pe.matmul(score_at(e)[:, x, :], KS1[0:SHIFT1 + 3, b, 2 * pr + x, kt * P:(kt + 1) * P],
                                             QS1[0:SHIFT1 + 3, b, 2 * pr + x, qh * QC:(qh + 1) * QC], start=True, stop=True)
                    else:
                        i, kt = WSTEPS[e - len(STEPS1)]
                        for hl in range(HL):
                            last = pe.matmul(score_at(e)[:, hl * P:(hl + 1) * P],
                                             KS1[0:SHIFT1 + 6, b, hl, kt * P:(kt + 1) * P],
                                             QS1[0:SHIFT1 + 6, b, hl, i * P:(i + 1) * P], start=True, stop=True)
                    last.then_inc(scores1_ready, 1)
                    if more:
                        while todo < min(len(MAX1), 2 * e + 2 + LEAD1):
                            max1_task(b + 1, todo)
                            todo += 1
                    if v_due(e) is not None:
                        pv1(b, v_due(e))
                    if e == 24:
                        turn_o1(4 * b)
                    if e == 38:
                        turn_o1(4 * b + 1)
                    if e == 49:
                        turn_o1(4 * b + 2)
                    if more and e == 45:
                        turn_max1(b + 1)
                    if not more:
                        first_sequence_out(e)
                for v in range(v_due(NE1 - 1) + 1, NV1):
                    pv1(b, v)
                turn_o1(4 * b + 3)

            pe.wait_ge(v1_out, NT)
            pe.wait_ge(zeroed1, 2)
            pe.wait_ge(stack1_in[0], 16 * 12)
            for i in range(len(MAX1)):
                max1_task(0, i)
            turn_max1(0)
            pe.wait_ge(stack1_in[1], 16 * 12)
            for i in range(LEAD1):
                max1_task(1, i)
            sequence(0, True)
            sequence(1, False)
            def key_scores(t, parts=(0, 1)):
                if 0 in parts:
                    pe.wait_ge(zt_staged, t + 1)
                    if not isinstance(t, int) or t >= 1:
                        pe.wait_ge(s_picked, t)
                for i in parts:
                    pe.matmul(ps[:, i, :], zt, wf[:, i * QC:(i + 1) * QC], start=True, stop=False)
                    last = pe.matmul(ps[:, i, :], ones3[:], bf3[:, i * QC:(i + 1) * QC], start=False, stop=True)
                if 1 in parts:
                    last.then_inc(s_ready, 1)

            def turn_trip(t):
                pe.wait_ge(trip_done, t + 1)
                if not isinstance(t, int) or t >= 1:
                    pe.wait_ge(uvw_ready, 2 * t)
                for w in range(3):
                    last = pe.transpose(t_ps[:, w * P:(w + 1) * P], trip[:, w].rearrange("p d n -> p (d n)"), ident[:])
                last.then_inc(trip_turned, 1)

            def gates(t, g):
                pe.wait_ge(a_made, 8 * t + g + 1)
                pe.wait_ge(b_weighted, 8 * t + g + 1)
                if not (isinstance(t, int) and 8 * t + g < 2):
                    pe.wait_ge(ge_out, 8 * t + g - 1)
                for c in range(8):
                    last = pe.matmul(g_ps[:, g % 2, c * 64:(c + 1) * 64], onehot[:, g % 2, c, :], weigh[:, g % 2, c, :],
                                     start=True, stop=True)
                last.then_inc(g_made, 1)

            def inner(t, q):
                if not (isinstance(t, int) and 8 * t + q < 2):
                    pe.wait_ge(inner_relu, 8 * t + q - 1)
                for i in range(4):
                    last = pe.matmul(in_ps[:, q % 2, i * P:(i + 1) * P], wdt[:, 4 * q + i, :], xT[:, bass.ts(t, P)],
                                     start=True, stop=True)
                last.then_inc(inner_ready, 1)

            def gather_out(t, q):
                pe.wait_ge(gr_done, 8 * t + q + 1)
                if q == 0 and not (isinstance(t, int) and t == 0):
                    pe.wait_ge(h_out, t)
                for i in range(4):
                    last = pe.matmul(acc_ps, gated[:, q % 2, i, :], wup[:, 4 * q + i, :],
                                     start=q == 0 and i == 0, stop=q == 7 and i == 3)
                last.then_inc(acc_used, 1)

            def tile(t, back, ahead):
                for g in range(8):
                    steps = (6, 7) if back else (3, 5)
                    if ahead == 2 and g in steps:
                        key_scores(t + 2, (steps.index(g),))
                    if back:
                        inner(t - 1, g)
                        if g:
                            gather_out(t - 1, g - 1)
                    gates(t, g)
                    if ahead and g == 6:
                        turn_trip(t + 1)
                if back:
                    gather_out(t - 1, 7)

            pe.wait_ge(wu_in, 16)
            pe.wait_ge(bf_in, 16)
            key_scores(0)
            turn_a(1)
            project_out(1)
            key_scores(1)
            turn_trip(0)
            turn_ln(8)
            pe.wait_ge(turned_out, 12)
            tile(0, False, 2)
            tile(1, True, 2)
            with pe.Fori(1, NT // 2 - 1) as m:
                for x in range(2):
                    tile(2 * m + x, True, 2)
            tile(NT - 2, True, 1)
            tile(NT - 1, True, 0)
            for q in range(8):
                inner(NT - 1, q)
                if q:
                    gather_out(NT - 1, q - 1)
            gather_out(NT - 1, 7)

        @block.vector
        def _(dve):
            order = Tally(dve, sem("dve_order"))
            dve.memset(kbd, 0.0).then_inc(fold_ready, 1)
            dve.memset(big_f[:, 16384:24576], TWO_MINUS_ONES).then_inc(zeroed, 1)
            dve.memset(big_f[:, Q_ZEROS:16384], 0.0).then_inc(zeroed, 1)

            def newton(r, x, s):
                order.then_wait(dve.tensor_tensor(s, r, r, ALU.mult))
                order.then_wait(dve.tensor_tensor(s, s, x, ALU.mult))
                order.then_wait(dve.tensor_scalar(s, s, -0.5, 1.5, ALU.mult, ALU.add))
                order.then_wait(dve.tensor_tensor(r, r, s, ALU.mult))

            def ln_begin(k):
                at = ln_tiles(k)
                for t in range(at.start, at.stop):
                    last = dve.bn_stats(halves[:, t, :], h[:, t, :])
                order.then_wait(last)
                for t in range(at.start, at.stop):
                    last = dve.bn_aggr(moments[:, t, :], halves[:, t, :])
                order.then_wait(last)
                dve.tensor_scalar(stat[:, 2, at], moments[:, at, 1], LN_EPS, None, ALU.add).then_inc(ln_var, 1)

            def ln_end(k):
                at = ln_tiles(k)
                dve.wait_ge(ln_sqrt, k)
                order.then_wait(dve.reciprocal(stat[:, 4, at], stat[:, 3, at]))
                newton(stat[:, 4, at], stat[:, 2, at], stat[:, 5, at])
                for t in range(at.start, at.stop):
                    last = dve.tensor_scalar(xn[:, t, :], h[:, t, :], moments[:, t, 0:1], stat[:, 4, t:t + 1],
                                             ALU.subtract, ALU.mult)
                last.then_inc(ln_done, 1)

            def layer_norm(k):
                ln_begin(k)
                ln_end(k)

            def take_turned(k):
                for j in range(2):
                    dve.wait_ge(turned, 2 * k + j + 1)
                    at = k % 2 * S + j * QC
                    dve.tensor_copy(xT[:, at:at + QC], ps[:, j + (4 if k >= 4 else 0), :]).then_inc(turned_out, 1)

            def split3(b, w, src, rows_, done, sent):
                scr = tmp[0:rows_].rearrange("p t c -> p (t c)")[:, 0:S]
                src = src[0:rows_, b * S:(b + 1) * S]
                dst = splits[0:rows_, w]
                n = 6 * b + 3 * w
                if b:
                    dve.wait_ge(sent, 32 * b)
                dve.tensor_copy(dst[:, 0, :], src).then_inc(done, 1)
                dve.wait_ge(done, n + 1)
                order.then_wait(dve.tensor_tensor(scr, src, dst[:, 0, :], ALU.subtract))
                dve.tensor_copy(dst[:, 1, :], scr).then_inc(done, 1)
                dve.wait_ge(done, n + 2)
                dve.tensor_tensor(dst[:, 2, :], scr, dst[:, 1, :], ALU.subtract).then_inc(done, 1)
                dve.wait_ge(done, n + 3)

            dve.wait_ge(gathered[0], 16 * KT)
            ln_begin(1)
            for b in range(B):
                ln_end(b + 1)
                take_turned(b)
                if b == 0:
                    dve.wait_ge(gathered[1], 16 * KT)
                    ln_begin(2)
                for w, src in enumerate((q_cm, k_cm)):
                    dve.wait_ge(proj_out, 4 * b + 2 * w + 2)
                    split3(b, w, src, C, split_done, split_out)
            def split_bias():
                dve.wait_ge(fold_out, 8)
                dve.wait_ge(split_out, 64)
                rowr = xT[0:1, 0:NH * P]
                order.then_wait(dve.tensor_copy(bfs[:, 0, :], bf[:]))
                order.then_wait(dve.tensor_tensor(rowr, bf[:], bfs[:, 0, :], ALU.subtract))
                order.then_wait(dve.tensor_copy(bfs[:, 1, :], rowr))
                dve.tensor_tensor(bfs[:, 2, :], rowr, bfs[:, 1, :], ALU.subtract).then_inc(bf_split, 1)
                dve.wait_ge(bf_split, 1)

            def max_read_task(n, i):
                par, x, qt, kh = i // 32, i // 16 % 2, i // 2 % 8, i % 2
                if i == 0 and not (isinstance(n, int) and n == 0):
                    dve.wait_ge(unit_max, n)
                dve.wait_ge(max_scores, 64 * n + i + 1)
                dve.tensor_reduce(mhalf[:, i // 2, kh:kh + 1], ps[:, max_bank(n, i), :], X, ALU.max).then_inc(max_read, 1)

            def max_of(n):
                dve.wait_ge(max_read, 64 * n + 64)
                if not isinstance(n, int) or n >= 1:
                    dve.wait_ge(max_turned, n)
                dve.tensor_reduce(mx[:], mhalf[:], X, ALU.max).then_inc(unit_max, 1)

            def shift_of(n):
                dve.wait_ge(max_turned, n + 1)
                if not isinstance(n, int) or n >= 1:
                    dve.wait_ge(shift_rows, 16 * 6 * n)
                src = o_ps[0:32, 0, 0:P]
                dve.tensor_copy(sh[:, 0, :], src).then_inc(shift_split, 1)
                dve.wait_ge(shift_split, 4 * n + 1)
                dve.tensor_tensor(shf[:], src, sh[:, 0, :], ALU.subtract).then_inc(shift_split, 1)
                dve.wait_ge(shift_split, 4 * n + 2)
                dve.tensor_copy(sh[:, 1, :], shf[:]).then_inc(shift_split, 1)
                dve.wait_ge(shift_split, 4 * n + 3)
                dve.tensor_tensor(sh[:, 2, :], shf[:], sh[:, 1, :], ALU.subtract).then_inc(shift_split, 1)

            def read_o(n, qh):
                dve.wait_ge(pv_done, 16 * n + 8 * qh + 8)
                if not isinstance(n, int) or 2 * n + qh >= 1:
                    dve.wait_ge(o_turned, 2 * n + qh)
                dve.tensor_copy(osb[:], o_ps[:, qh, :]).then_inc(o_read, 1)

            def norm_o(n, qh):
                dve.wait_ge(o_turned, 2 * n + qh + 1)
                if not isinstance(n, int) or 2 * n + qh >= 1:
                    dve.wait_ge(o_norm, 2 * n + qh)
                o = o_ps[:, qh, :].rearrange("p (t h m) -> p t h m", t=4, h=HL)
                dve.reciprocal(rden[:], o[:, :, :, D0]).then_inc(sem("rden_done"), 1)
                dve.wait_ge(sem("rden_done"), 2 * n + qh + 1)
                dst = attn[:, n, 4 * qh:4 * qh + 4, :].rearrange("p t (h d) -> p t h d", h=HL)
                dve.tensor_tensor(dst, o[:, :, :, 0:D0],
                                  rden[:].unsqueeze(3).broadcast_to([P, 4, HL, D0]), ALU.mult).then_inc(o_norm, 1)

            def unit(n, left):
                for e in range(len(STEPS0)):
                    for k in (2 * e, 2 * e + 1):
                        if max_unit_at(n, k, left):
                            max_read_task(*max_unit_at(n, k, left))
                    if e == 18:
                        read_o(n, 0)
                    if e == 20:
                        norm_o(n, 0)
                    if left and e == MAXED:
                        max_of(n + 1)
                    if left and e == MAXED + 2:
                        shift_of(n + 1)
                read_o(n, 1)
                norm_o(n, 1)

            for i in range(len(MAX0)):
                max_read_task(0, i)
            max_of(0)
            shift_of(0)
            for i in range(LEAD0):
                max_read_task(1, i)
            unit(0, UNITS - 1)
            with dve.Fori(1, UNITS - 2) as n:
                unit(n, 2)
            unit(UNITS - 2, 1)

            def attn_residual(b):
                dve.wait_ge(o_norm, UNITS * (b + 1))
                xb = xn[:, b * KT:(b + 1) * KT, :].rearrange("p t (g c) -> p g t c", g=4)
                dve.tensor_tensor(xb, xb, attn[:, 4 * b:4 * b + 4, :, :], ALU.add).then_inc(bn_ready, 1)
                dve.wait_ge(bn_ready, b + 1)

            split_bias()
            attn_residual(0)
            unit(UNITS - 1, 0)
            attn_residual(1)

            def along_tokens(row):
                return row.unsqueeze(1).broadcast_to([P, KT, C])

            dve.wait_ge(bn_made, 1)
            order.then_wait(dve.tensor_scalar(bn[:, 0, :], ps[:, 4, 0:C], 1.0 / NTOK, None, ALU.mult))
            seqs = [slice(b * KT, (b + 1) * KT) for b in range(B)]
            for b in range(B):
                xb = xn[:, seqs[b], :]
                dve.tensor_tensor(xb, xb, along_tokens(bn[:, 0, :]), ALU.subtract).then_inc(bn_centred, 1)
            dve.wait_ge(bn_made, 2)
            for b in range(B):
                hb = h[:, seqs[b], :]
                last = dve.tensor_tensor(hb, hb, along_tokens(ps[:, 3, 0:C]), ALU.add)
            order.then_wait(last)
            dve.wait_ge(bn_made, 3)
            dve.tensor_scalar(bn[:, 1, :], ps[:, 5, 0:C], 1.0 / NTOK, BN_EPS, ALU.mult, ALU.add).then_inc(bn_ready, 1)
            dve.wait_ge(bn_root, 1)
            order.then_wait(dve.reciprocal(bn_r, bn[:, 2, :]))
            newton(bn_r, bn[:, 1, :], bn[:, 4, :])
            order.then_wait(dve.tensor_tensor(bn_r, bn_r, ps[:, 2, 0:C], ALU.mult))
            def finish_bn(b):
                hb, xb = h[:, seqs[b], :], xn[:, seqs[b], :]
                order.then_wait(dve.tensor_tensor(xb, xb, along_tokens(bn_r), ALU.mult))
                order.then_wait(dve.tensor_tensor(hb, hb, xb, ALU.add))
                ln_begin(3 + 2 * b)

            finish_bn(0)
            for b in range(B):
                hb, xb = h[:, seqs[b], :], xn[:, seqs[b], :]
                ln_end(3 + 2 * b)
                dve.wait_ge(ln_done, 3 + 2 * b)
                order.then_wait(dve.tensor_tensor(hb, hb, xb, ALU.add))
                layer_norm(4 + 2 * b)
                take_turned(2 + b)
                if b == 0:
                    finish_bn(1)
                for w, src in enumerate((q_cm, k_cm)):
                    dve.wait_ge(proj1_out, 4 * b + 2 * w + 2)
                    dve.wait_ge(bf_in, 16)
                    split3(b, w, src, E1, split1_done, split1_out)

            def max1_read_task(b, i):
                kind, hl, qt, kh = MAX1[i]
                k = len(MAX1) * b + i
                if i == 0 and b:
                    dve.wait_ge(unit1_max, b)
                dve.wait_ge(max1_scores, k + 1)
                if kind == "full":
                    dve.tensor_reduce(mhalf[:, i // 2, kh:kh + 1], ps[:, max_bank(b, i), :], X, ALU.max).then_inc(max1_read, 1)
                else:
                    at = window_of(qt)[1]
                    if k >= 2:
                        dve.wait_ge(max1_read, k - 1)
                    dve.tensor_tensor_reduce(wscr[:, i % 2, :], ps[:, max_bank(b, i), 0:192], wmask[:, at:at + 192], 1.0, -3e38,
                                             ALU.add, ALU.max, mx1[:, 32 + 8 * hl + qt:33 + 8 * hl + qt]).then_inc(max1_read, 1)

            def max1_of(b):
                dve.wait_ge(max1_read, len(MAX1) * (b + 1))
                if b:
                    dve.wait_ge(max1_turned, b)
                order.then_wait(dve.tensor_reduce(mx1[:, 0:32], mhalf[:], X, ALU.max))
                dve.tensor_tensor(mx1[:, 32:64], mx1[:, 32:64], mx1[:, 0:32], ALU.subtract).then_inc(unit1_max, 1)

            def shift1_of(b):
                dve.wait_ge(max1_turned, b + 1)
                if b:
                    dve.wait_ge(shift1_rows, 16 * 6 * b)
                src = max_ps[0:64, 0, 0:P]
                dve.tensor_copy(sh1[:, 0, :], src).then_inc(shift1_split, 1)
                dve.wait_ge(shift1_split, 4 * b + 1)
                dve.tensor_tensor(shf1[:], src, sh1[:, 0, :], ALU.subtract).then_inc(shift1_split, 1)
                dve.wait_ge(shift1_split, 4 * b + 2)
                dve.tensor_copy(sh1[:, 1, :], shf1[:]).then_inc(shift1_split, 1)
                dve.wait_ge(shift1_split, 4 * b + 3)
                dve.tensor_tensor(sh1[:, 2, :], shf1[:], sh1[:, 1, :], ALU.subtract).then_inc(shift1_split, 1)

            def scale1(b, e):
                dve.wait_ge(exp1_done, NE1 * b + e + 1)
                if e < len(STEPS1):
                    qh, kt, pr = STEPS1[e]
                    at = qh * QC - kt * P + S - P
                    slot = probs1[e // 2 % 4][:, 2 * pr:2 * pr + 2, :]
                    by = dist[:, at:at + QC].unsqueeze(1).broadcast_to([P, 2, QC])
                else:
                    i, kt = WSTEPS[e - len(STEPS1)]
                    v = e - len(STEPS1) + 16
                    slot = probs1[v % 4][:, 0, :].rearrange("p (h n) -> p h n", h=HL)
                    by = near[:, kt - i + 1, :].unsqueeze(1).broadcast_to([P, HL, P])
                dve.tensor_tensor(slot, slot, by, ALU.mult).then_inc(scaled_dve, 1)

            def read_o1(w):
                b, k = divmod(w, 4)
                dve.wait_ge(pv1_done, NV1 * b + (8, 16, 16 + 11, NV1)[k])
                if w:
                    dve.wait_ge(o1_turned, w)
                dve.tensor_copy(osb[:], o_ps[:, w % 2, :]).then_inc(o1_read, 1)

            def norm_o1(w):
                b, k = divmod(w, 4)
                dve.wait_ge(o1_turned, w + 1)
                o = o_ps[:, w % 2, :].rearrange("p (t h m) -> p t h m", t=4, h=HL)
                order.then_wait(dve.reciprocal(rden[:], o[:, :, :, D1]))
                at = KT * b + 4 * (k % 2)
                dst = attn1[:, at:at + 4, :].rearrange("p t (h d) -> p t h d", h=H1)
                r4 = rden[:].unsqueeze(3).broadcast_to([P, 4, H1, D1])
                if k < 2:
                    dve.scalar_tensor_tensor(out=dst, in0=o[:, :, :, 0:D1], scalar=0.5, in1=r4, op0=ALU.mult,
                                             op1=ALU.mult).then_inc(o1_norm, 1)
                    dve.wait_ge(o1_norm, w + 1)
                else:
                    o2 = relued[:, 0].rearrange("p i n -> p (i n)")[:, 0:4 * E1].rearrange("p (t h d) -> p t h d", t=4, h=H1)
                    dve.scalar_tensor_tensor(out=o2, in0=o[:, :, :, 0:D1], scalar=0.5, in1=r4, op0=ALU.mult,
                                             op1=ALU.mult).then_inc(o1_norm, 1)
                    dve.wait_ge(o1_norm, w + 1)
                    dve.tensor_tensor(dst, dst, o2, ALU.add).then_inc(attn1_done, 1)
                    dve.wait_ge(attn1_done, 2 * b + k - 1)

            def add_attn1(b):
                for j in range(2):
                    dve.wait_ge(wo_made, 2 * b + j + 1)
                    hj = h[:, KT * b + 4 * j:KT * b + 4 * j + 4, :]
                    order.then_wait(dve.tensor_tensor(hj, hj, max_ps[:, j, :].rearrange("p (t c) -> p t c", t=4), ALU.add))

            def first_sequence_out(e):
                if e == 12:
                    add_attn1(0)
                if e == 13:
                    layer_norm(7)
                if e == 25:
                    take_turned(4)

            def sequence(b, more):
                todo = LEAD1
                for e in range(NE1):
                    if more:
                        while todo < min(len(MAX1), 2 * e + 2 + LEAD1):
                            max1_read_task(b + 1, todo)
                            todo += 1
                    if not on_pool(b, e):
                        scale1(b, e)
                    if e == 22:
                        read_o1(4 * b)
                    if e == 26:
                        norm_o1(4 * b)
                    if e == 36:
                        read_o1(4 * b + 1)
                    if e == 40:
                        norm_o1(4 * b + 1)
                    if e == 47:
                        read_o1(4 * b + 2)
                    if e == 51:
                        norm_o1(4 * b + 2)
                    if more and e == 43:
                        max1_of(b + 1)
                    if more and e == 45:
                        shift1_of(b + 1)
                    if not more:
                        first_sequence_out(e)
                read_o1(4 * b + 3)
                norm_o1(4 * b + 3)

            for i in range(len(MAX1)):
                max1_read_task(0, i)
            max1_of(0)
            shift1_of(0)
            for i in range(LEAD1):
                max1_read_task(1, i)
            dve.wait_ge(split1_out, 64)
            sequence(0, True)
            sequence(1, False)
            PICKS = 13

            def picked(t, n):
                dve.wait_ge(pick_order, PICKS * t + n)

            def key_max(t, g):
                for hh in range(4 * g, 4 * g + 4):
                    for q in range(2):
                        last = dve.max(top[:, hh, q, :], s_ps[:, hh, q, :])
                last.then_inc(pick_order, 1)

            def key_places(t, g):
                for hh in range(4 * g, 4 * g + 4):
                    for q in range(2):
                        last = dve.max_index(top_at[:, hh, q, :], top[:, hh, q, :], s_ps[:, hh, q, :])
                if g == 1:
                    last.then_inc(s_picked, 1)

            def pair_sums(t):
                dve.tensor_tensor(sums, top[:, :, 0, :].unsqueeze(3).broadcast_to([P, NH, TK, TK]),
                                  top[:, :, 1, :].unsqueeze(2).broadcast_to([P, NH, TK, TK]), ALU.add).then_inc(pick_order, 1)

            def pair_max(t):
                for hh in range(NH):
                    last = dve.max(best[:, hh, :], sums[:, hh].rearrange("p i j -> p (i j)"))
                last.then_inc(pick_order, 1)

            def pair_places(t):
                picked(t, 4)
                dve.tensor_tensor(evd, best, best[:, :, 0:1].broadcast_to([P, NH, TK]), ALU.subtract).then_inc(diff_done, 1)
                for hh in range(NH):
                    last = dve.max_index(best_at[:, hh, :], best[:, hh, :], sums[:, hh].rearrange("p i j -> p (i j)"))
                last.then_inc(pick_order, 1)

            def pair_sides(t):
                picked(t, 5)
                dve.tensor_scalar(side[0], best_at, 3, None, ALU.logical_shift_right)
                dve.tensor_scalar(side[1], best_at, 7, None, ALU.bitwise_and).then_inc(pick_order, 1)

            def match_places(t):
                picked(t, 6)
                eight = iota_f[:, 0:TK].unsqueeze(1).unsqueeze(1).broadcast_to([P, NH, TK, TK])
                for q in range(2):
                    last = dve.tensor_tensor(match[q], side[q].unsqueeze(3).broadcast_to([P, NH, TK, TK]), eight, ALU.is_equal)
                last.then_inc(pick_order, 1)

            def match_keys(t):
                picked(t, 7)
                dve.wait_ge(s_picked, t + 1)
                for q in range(2):
                    last = dve.tensor_tensor(match[q], match[q],
                                             top_at[:, :, q, :].unsqueeze(2).broadcast_to([P, NH, TK, TK]), ALU.mult)
                last.then_inc(pick_order, 1)

            def sum_keys(t):
                picked(t, 8)
                for q in range(2):
                    last = dve.tensor_reduce(key_at[q].rearrange("p (h k) -> p h k", h=NH), match[q], X, ALU.add)
                last.then_inc(pick_order, 1)

            def key_high(t):
                picked(t, 9)
                dve.tensor_scalar(upper, key_at[1], float(VL), None, ALU.is_ge).then_inc(pick_order, 1)
                dve.wait_ge(pexp_done, t + 1)
                dve.tensor_reduce(esum, ev, X, ALU.add).then_inc(pick_order, 1)

            def split_number(t):
                picked(t, 11)
                if not isinstance(t, int) or t >= 1:
                    dve.wait_ge(trip_turned, t)
                for d in range(2):
                    last = dve.scalar_tensor_tensor(out=trip[:, 0, d, :], in0=key_at[0], scalar=2.0, in1=upper,
                                                    op0=ALU.mult, op1=ALU.add)
                dve.scalar_tensor_tensor(out=trip[:, 1, 0, :], in0=upper, scalar=-float(VL), in1=key_at[1], op0=ALU.mult,
                                         op1=ALU.add).then_inc(pick_order, 1)
                dve.reciprocal(rsum, esum).then_inc(pick_order, 1)

            def weights(t):
                picked(t, 13)
                dve.tensor_scalar(trip[:, 1, 1, :], trip[:, 1, 0, :], float(VL), None, ALU.add)
                for d in range(2):
                    last = dve.tensor_tensor(trip[:, 2, d, :].rearrange("p (h k) -> p h k", h=NH), ev, spread(rsum, TK), ALU.mult)
                last.then_inc(trip_done, 1)

            def onehot_v(t, x, g):
                if g == 0:
                    dve.wait_ge(uvw_ready, 2 * t + 2)
                if not (isinstance(t, int) and 8 * t + g < 2):
                    dve.wait_ge(g_made, 8 * t + g - 1)
                dve.tensor_tensor(weigh[:, g % 2], iota_f[:, 0:64].unsqueeze(1).broadcast_to([P, 8, 64]),
                                  spread(uvw[:, x, 1, 8 * g:8 * g + 8], 64), ALU.is_equal).then_inc(b_made, 1)

            def onehot_u(t, x, g):
                dve.tensor_tensor(onehot[:, g % 2], iota_f[:].unsqueeze(1).broadcast_to([P, 8, P]),
                                  spread(uvw[:, x, 0, 8 * g:8 * g + 8], P), ALU.is_equal).then_inc(a_made, 1)

            def add_out(t):
                dve.wait_ge(acc_used, 8 * t + 8)
                ht = h[:, bass.ts(t, 1), :].rearrange("p o c -> p (o c)")
                dve.tensor_tensor(ht, ht, acc_ps, ALU.add).then_inc(h_out, 1)

            def tile(t, x, back, more):
                for g in range(8):
                    n = t + 1
                    if more and g == 0:
                        dve.wait_ge(s_ready, t + 2)
                    onehot_v(t, x, g)
                    if more and g < 2:
                        key_max(n, g)
                        picked(n, g + 1)
                    if more and g == 2:
                        pair_sums(n)
                        picked(n, 3)
                    if more and g == 3:
                        pair_places(n)
                    if more and g == 4:
                        match_places(n)
                    if more and g == 5:
                        sum_keys(n)
                    onehot_u(t, x, g)
                    if more and g < 2:
                        key_places(n, g)
                    if more and g == 2:
                        pair_max(n)
                    if more and g == 3:
                        pair_sides(n)
                    if more and g == 4:
                        match_keys(n)
                    if more and g == 5:
                        key_high(n)
                        split_number(n)
                    if back and g == 0:
                        add_out(t - 2)
                    if more and g == 5:
                        weights(n)

            dve.wait_ge(s_ready, 1)
            for g in range(2):
                key_max(0, g)
                picked(0, g + 1)
                key_places(0, g)
            pair_sums(0)
            picked(0, 3)
            for step in (pair_max, pair_places, pair_sides, match_places, match_keys, sum_keys, key_high, split_number, weights):
                step(0)
            add_attn1(1)
            layer_norm(8)
            take_turned(5)
            tile(0, 0, False, True)
            tile(1, 1, False, True)
            with dve.Fori(1, NT // 2 - 1) as m:
                for x in range(2):
                    tile(2 * m + x, x, True, True)
            tile(NT - 2, 0, True, True)
            tile(NT - 1, 1, True, False)
            add_out(NT - 2)
            add_out(NT - 1)


def kernel(**inputs):
    import numpy as np
    import concourse.bacc as bacc
    from concourse.bass_utils import run_bass_kernel_spmd

    nc = bacc.Bacc("TRN2", target_bir_lowering=False, num_devices=1)
    arrays, aps = {}, {}

    def put(name, arr):
        arr = np.ascontiguousarray(arr)
        arrays[name + "_in"] = arr
        aps[name] = nc.dram_tensor(name + "_in", arr.shape, mybir.dt.from_np(arr.dtype), kind="ExternalInput").ap()

    put("tok", np.asarray(inputs["x"]).reshape(NT, P).T)
    put("emb", np.asarray(inputs["L0_tok_W"]).T)
    put("bqt", np.asarray(inputs["L1_ffn_bq"]).reshape(NH, P).T)
    for name in _WEIGHTS:
        put(name, np.asarray(inputs[name]))
    for name in ("L1_attn_gamma", "L1_attn_theta"):
        put(name, np.asarray(inputs[name]).reshape(1))
    out = nc.dram_tensor("out_dram", (B, S, C), F32, kind="ExternalOutput").ap()
    build_tower(nc, aps, out)
    r = run_bass_kernel_spmd(nc, [arrays], core_ids=[0])
    return r.results[0]["out_dram"]


_WEIGHTS = ["L0_attn_wq", "L0_attn_bq", "L0_attn_wk", "L0_attn_bk", "L0_attn_wv", "L0_attn_bv",
            "L0_attn_gamma", "L0_attn_beta", "L1_attn_Wq", "L1_attn_bq", "L1_attn_Wk", "L1_attn_bk",
            "L1_attn_Wv", "L1_attn_bv", "L1_attn_Wout", "L1_attn_bout", "L1_ffn_Wq", "L1_ffn_keys",
            "L1_ffn_w_down", "L1_ffn_w_up"]
```
